# Optimizing a Trainium2 kernel written in Bass

```python
import numpy as np
import jax
import jax.numpy as jnp

def _softmax(x, axis=-1):
    return jax.nn.softmax(x, axis=axis)

def _gelu(x):
    return jax.nn.gelu(x, approximate=True)

def _silu(x):
    return jax.nn.silu(x)

def _sigmoid(x):
    return jax.nn.sigmoid(x)

def _layernorm(x, axis=-1, eps=1e-05):
    m = jnp.mean(x, axis=axis, keepdims=True)
    v = jnp.var(x, axis=axis, keepdims=True)
    return (x - m) / jnp.sqrt(v + eps)

def _scatter_add(tgt, idx, src, axis=0):
    return tgt.at[idx].add(src)

def _segment_sum(src, seg, n):
    return jax.ops.segment_sum(src, seg, n)
kernel_name = 'mk_gnn_preln_d4_gnn_r64_a2ced2'

def setup_inputs(seed: int=0):
    np.random.seed(seed)
    _w = jnp.asarray

    def _rec_inputs():
        import jax
        import jax.numpy as jnp
        _gk = jax.random.key(seed)
        x = -0.000202 + 1 * jax.random.normal(jax.random.fold_in(_gk, 1), (100000, 64), jnp.float32)
        src = jax.random.randint(jax.random.fold_in(_gk, 2), (50000,), 0, 100000, jnp.int32)
        dst = jnp.minimum((100000 * jax.random.uniform(jax.random.fold_in(_gk, 3), (50000,)) ** 2.0).astype(jnp.int32), 99999)
        _o = jnp.argsort(dst, stable=True)
        src = src[_o]
        dst = dst[_o]
        edge_attr_32 = 0.000196303 + 1.00016 * jax.random.normal(jax.random.fold_in(_gk, 12), (50000, 32), jnp.float32)
        edge_type_8 = jax.random.randint(jax.random.fold_in(_gk, 14), (50000,), 0, 8, jnp.int32)
        edge_weight1 = jax.random.uniform(jax.random.fold_in(_gk, 15), (50000, 1), jnp.float32, 0.0, 1)
        return (x, src, dst, edge_attr_32, edge_type_8, edge_weight1)
    x, src, dst, edge_attr_32, edge_type_8, edge_weight1 = _rec_inputs()

    def _L0_gnn_setup():
        import jax, jax.numpy as jnp
        import numpy as np
        N = 100000
        E = 25000
        D = 64
        ALPHA = 0.05
        BETA = 1.5
        key = jax.random.key(seed)
        k1, k2, k3, k4 = jax.random.split(key, 4)
        x = jax.random.normal(k1, (N, D), dtype=jnp.float32)
        edge_index = jax.random.randint(k2, (2, E), 0, N, dtype=jnp.int64)
        W = jax.random.normal(k3, (D, D), dtype=jnp.float32) / np.sqrt(D)
        b = jax.random.normal(k4, (D,), dtype=jnp.float32) * 0.01
        return {'x': x, 'edge_index': edge_index, 'W': W, 'b': b}
    _L0_gnn_all = _L0_gnn_setup()
    _L0_gnn_in = {k: v for k, v in _L0_gnn_all.items() if k in ('W', 'b')}
    del _L0_gnn_all

    def _L1_gnn_setup():
        import jax, jax.numpy as jnp
        import numpy as np
        N_NODES = 100000
        N_EDGES = 25000
        IN_FEAT = 64
        OUT_FEAT = 64
        NUM_RELS = 8
        key = jax.random.key(seed)
        k1, k2, k3, k4, k5, k6 = jax.random.split(key, 6)
        feat = jax.random.normal(k1, (N_NODES, IN_FEAT), dtype=jnp.float32)
        norm = jax.random.uniform(k2, (N_EDGES, 1), dtype=jnp.float32)
        bound = 1.0 / np.sqrt(IN_FEAT)
        weight = jax.random.uniform(k3, (NUM_RELS, IN_FEAT, OUT_FEAT), dtype=jnp.float32, minval=-bound, maxval=bound)
        etypes = jax.random.randint(k4, (N_EDGES,), 0, NUM_RELS, dtype=jnp.int64 if jax.config.jax_enable_x64 else jnp.int32)
        src = jax.random.randint(k5, (N_EDGES,), 0, N_NODES, dtype=jnp.int32)
        dst = jax.random.randint(k6, (N_EDGES,), 0, N_NODES, dtype=jnp.int32)
        return {'feat': feat, 'norm': norm, 'weight': weight, 'etypes': etypes, 'src': src, 'dst': dst}
    _L1_gnn_all = _L1_gnn_setup()
    _L1_gnn_in = {k: v for k, v in _L1_gnn_all.items() if k in ('weight',)}
    del _L1_gnn_all

    def _L2_gnn_setup():
        import jax, jax.numpy as jnp
        import numpy as np
        N = 50000
        E = 12500
        D = 64
        H = 64
        DE = 32

        def _transformer_conv(x, src, dst, edge_attr, wq, bq, wk, bk, wv, bv, we, ws, bs, n_nodes):
            q = x @ wq + bq
            k = x @ wk + bk
            v = x @ wv + bv
            e = edge_attr @ we
            ke = k[src] + e
            score = jnp.sum(q[dst] * ke, axis=-1) / jnp.sqrt(jnp.asarray(ke.shape[-1], x.dtype))
            smax = jax.ops.segment_max(score, dst, num_segments=n_nodes)
            a = jnp.exp(score - smax[dst])
            denom = jax.ops.segment_sum(a, dst, num_segments=n_nodes)
            alpha = a / denom[dst]
            msg = alpha[:, None] * (v[src] + e)
            out = jax.ops.segment_sum(msg, dst, num_segments=n_nodes)
            out = out + x @ ws + bs
            return out
        key = jax.random.key(seed)
        ks = jax.random.split(key, 24)

        def g(i, shape, scale):
            return jax.random.normal(ks[i], shape, dtype=jnp.float32) * scale
        inp = {'x': g(0, (N, D), 1.0), 'edge_index': jax.random.randint(ks[1], (2, E), 0, N, dtype=jnp.int64), 'edge_attr': g(2, (E, DE), 1.0), 'q1_w': g(3, (D, H), D ** (-0.5)), 'q1_b': jnp.zeros((H,), jnp.float32), 'k1_w': g(4, (D, H), D ** (-0.5)), 'k1_b': jnp.zeros((H,), jnp.float32), 'v1_w': g(5, (D, H), D ** (-0.5)), 'v1_b': jnp.zeros((H,), jnp.float32), 'e1_w': g(6, (DE, H), DE ** (-0.5)), 's1_w': g(7, (D, H), D ** (-0.5)), 's1_b': jnp.zeros((H,), jnp.float32), 'q2_w': g(8, (H, H), H ** (-0.5)), 'q2_b': jnp.zeros((H,), jnp.float32), 'k2_w': g(9, (H, H), H ** (-0.5)), 'k2_b': jnp.zeros((H,), jnp.float32), 'v2_w': g(10, (H, H), H ** (-0.5)), 'v2_b': jnp.zeros((H,), jnp.float32), 'e2_w': g(11, (DE, H), DE ** (-0.5)), 's2_w': g(12, (H, H), H ** (-0.5)), 's2_b': jnp.zeros((H,), jnp.float32), 'skip_w': g(13, (2 * H, D), (2 * H) ** (-0.5)), 'skip_b': jnp.zeros((D,), jnp.float32)}
        return inp
    _L2_gnn_all = _L2_gnn_setup()
    _L2_gnn_in = {k: v for k, v in _L2_gnn_all.items() if k in ('q1_w', 'q1_b', 'k1_w', 'k1_b', 'v1_w', 'v1_b', 'e1_w', 's1_w', 's1_b', 'q2_w', 'q2_b', 'k2_w', 'k2_b', 'v2_w', 'v2_b', 'e2_w', 's2_w', 's2_b', 'skip_w', 'skip_b')}
    del _L2_gnn_all

    def _L3_gnn_setup():
        import jax, jax.numpy as jnp
        import numpy as np
        N_NODES = 100000

        def gcn_conv(x, src, dst, W, b):
            n = x.shape[0]
            deg = jax.ops.segment_sum(jnp.ones_like(src, dtype=x.dtype), dst, num_segments=n)
            dinv = jnp.where(deg > 0, jax.lax.rsqrt(deg), 0.0)
            norm = dinv[src] * dinv[dst]
            h = x @ W
            msg = h[src] * norm[:, None]
            out = jax.ops.segment_sum(msg, dst, num_segments=n)
            return out + b

        def add_self_loops(edge_index, n):
            loop = jnp.arange(n, dtype=edge_index.dtype)
            src = jnp.concatenate([edge_index[0], loop])
            dst = jnp.concatenate([edge_index[1], loop])
            return (src, dst)
        key = jax.random.key(seed)
        k1, k2, k3, k4 = jax.random.split(key, 4)
        F_in, F_mid = (64, 32)
        x = jax.random.normal(k1, (N_NODES, F_in), dtype=jnp.float32)
        edge_index = jax.random.randint(k2, (2, 18750), 0, N_NODES, dtype=jnp.int64)
        W1 = jax.random.normal(k3, (F_in, F_mid), dtype=jnp.float32) * (1.0 / np.sqrt(F_in))
        b1 = jnp.zeros((F_mid,), dtype=jnp.float32)
        W2 = jax.random.normal(k4, (F_mid, F_in), dtype=jnp.float32) * (1.0 / np.sqrt(F_mid))
        b2 = jnp.zeros((F_in,), dtype=jnp.float32)
        return {'x': x, 'edge_index': edge_index, 'W1': W1, 'b1': b1, 'W2': W2, 'b2': b2}
    _L3_gnn_all = _L3_gnn_setup()
    _L3_gnn_in = {k: v for k, v in _L3_gnn_all.items() if k in ('W1', 'b1', 'W2', 'b2')}
    del _L3_gnn_all
    return {'x': x, 'src': src, 'dst': dst, 'edge_attr_32': edge_attr_32, 'edge_type_8': edge_type_8, 'edge_weight1': edge_weight1, 'L0_gnn_W': _L0_gnn_in['W'], 'L0_gnn_b': _L0_gnn_in['b'], 'L1_gnn_weight': _L1_gnn_in['weight'], 'L2_gnn_q1_w': _L2_gnn_in['q1_w'], 'L2_gnn_q1_b': _L2_gnn_in['q1_b'], 'L2_gnn_k1_w': _L2_gnn_in['k1_w'], 'L2_gnn_k1_b': _L2_gnn_in['k1_b'], 'L2_gnn_v1_w': _L2_gnn_in['v1_w'], 'L2_gnn_v1_b': _L2_gnn_in['v1_b'], 'L2_gnn_e1_w': _L2_gnn_in['e1_w'], 'L2_gnn_s1_w': _L2_gnn_in['s1_w'], 'L2_gnn_s1_b': _L2_gnn_in['s1_b'], 'L2_gnn_q2_w': _L2_gnn_in['q2_w'], 'L2_gnn_q2_b': _L2_gnn_in['q2_b'], 'L2_gnn_k2_w': _L2_gnn_in['k2_w'], 'L2_gnn_k2_b': _L2_gnn_in['k2_b'], 'L2_gnn_v2_w': _L2_gnn_in['v2_w'], 'L2_gnn_v2_b': _L2_gnn_in['v2_b'], 'L2_gnn_e2_w': _L2_gnn_in['e2_w'], 'L2_gnn_s2_w': _L2_gnn_in['s2_w'], 'L2_gnn_s2_b': _L2_gnn_in['s2_b'], 'L2_gnn_skip_w': _L2_gnn_in['skip_w'], 'L2_gnn_skip_b': _L2_gnn_in['skip_b'], 'L3_gnn_W1': _L3_gnn_in['W1'], 'L3_gnn_b1': _L3_gnn_in['b1'], 'L3_gnn_W2': _L3_gnn_in['W2'], 'L3_gnn_b2': _L3_gnn_in['b2']}

def reference(x, src, dst, edge_attr_32, edge_type_8, edge_weight1, L0_gnn_W, L0_gnn_b, L1_gnn_weight, L2_gnn_q1_w, L2_gnn_q1_b, L2_gnn_k1_w, L2_gnn_k1_b, L2_gnn_v1_w, L2_gnn_v1_b, L2_gnn_e1_w, L2_gnn_s1_w, L2_gnn_s1_b, L2_gnn_q2_w, L2_gnn_q2_b, L2_gnn_k2_w, L2_gnn_k2_b, L2_gnn_v2_w, L2_gnn_v2_b, L2_gnn_e2_w, L2_gnn_s2_w, L2_gnn_s2_b, L2_gnn_skip_w, L2_gnn_skip_b, L3_gnn_W1, L3_gnn_b1, L3_gnn_W2, L3_gnn_b2):
    import jax
    import jax.numpy as jnp

    def _L0_gnn_ref(x, edge_index, W, b):
        import jax, jax.numpy as jnp
        import numpy as np
        N = 100000
        E = 25000
        D = 64
        ALPHA = 0.05
        BETA = 1.5
        h = x @ W.T + b
        n = h.shape[0]
        loops = jnp.arange(n, dtype=edge_index.dtype)
        row = jnp.concatenate([edge_index[0], loops])
        col = jnp.concatenate([edge_index[1], loops])
        deg = jax.ops.segment_sum(jnp.ones_like(row, dtype=h.dtype), row, num_segments=n)
        deg_inv_sqrt = jnp.where(deg > 0, jax.lax.rsqrt(jnp.maximum(deg, 1.0)), 0.0)
        norm = deg_inv_sqrt[row] * deg_inv_sqrt[col]
        agg = jax.ops.segment_sum(norm[:, None] * h[col], row, num_segments=n)
        diffusion = ALPHA * (agg - h)
        reaction = BETA * jax.nn.relu(h)
        return h + diffusion + reaction

    def _L1_gnn_ref(feat, norm, weight, etypes, src, dst):
        import jax, jax.numpy as jnp
        import numpy as np
        N_NODES = 100000
        N_EDGES = 25000
        IN_FEAT = 64
        OUT_FEAT = 64
        NUM_RELS = 8
        transformed = jnp.einsum('ni,rio->rno', feat, weight)
        msg = transformed[etypes, src]
        msg = msg * norm
        out = jax.ops.segment_sum(msg, dst, num_segments=feat.shape[0])
        return out

    def _L2_gnn_ref(x, edge_index, edge_attr, q1_w, q1_b, k1_w, k1_b, v1_w, v1_b, e1_w, s1_w, s1_b, q2_w, q2_b, k2_w, k2_b, v2_w, v2_b, e2_w, s2_w, s2_b, skip_w, skip_b):
        import jax, jax.numpy as jnp
        import numpy as np
        N = 50000
        E = 12500
        D = 64
        H = 64
        DE = 32

        def _transformer_conv(x, src, dst, edge_attr, wq, bq, wk, bk, wv, bv, we, ws, bs, n_nodes):
            q = x @ wq + bq
            k = x @ wk + bk
            v = x @ wv + bv
            e = edge_attr @ we
            ke = k[src] + e
            score = jnp.sum(q[dst] * ke, axis=-1) / jnp.sqrt(jnp.asarray(ke.shape[-1], x.dtype))
            smax = jax.ops.segment_max(score, dst, num_segments=n_nodes)
            a = jnp.exp(score - smax[dst])
            denom = jax.ops.segment_sum(a, dst, num_segments=n_nodes)
            alpha = a / denom[dst]
            msg = alpha[:, None] * (v[src] + e)
            out = jax.ops.segment_sum(msg, dst, num_segments=n_nodes)
            out = out + x @ ws + bs
            return out
        src, dst = (edge_index[0], edge_index[1])
        n = x.shape[0]
        h1 = jax.nn.relu(_transformer_conv(x, src, dst, edge_attr, q1_w, q1_b, k1_w, k1_b, v1_w, v1_b, e1_w, s1_w, s1_b, n))
        h2 = jax.nn.relu(_transformer_conv(h1, src, dst, edge_attr, q2_w, q2_b, k2_w, k2_b, v2_w, v2_b, e2_w, s2_w, s2_b, n))
        skip_xs = jnp.concatenate([h1, h2], axis=-1)
        return jax.nn.relu(skip_xs @ skip_w + skip_b)

    def _L3_gnn_ref(x, edge_index, W1, b1, W2, b2):
        import jax, jax.numpy as jnp
        import numpy as np
        N_NODES = 100000

        def gcn_conv(x, src, dst, W, b):
            n = x.shape[0]
            deg = jax.ops.segment_sum(jnp.ones_like(src, dtype=x.dtype), dst, num_segments=n)
            dinv = jnp.where(deg > 0, jax.lax.rsqrt(deg), 0.0)
            norm = dinv[src] * dinv[dst]
            h = x @ W
            msg = h[src] * norm[:, None]
            out = jax.ops.segment_sum(msg, dst, num_segments=n)
            return out + b

        def add_self_loops(edge_index, n):
            loop = jnp.arange(n, dtype=edge_index.dtype)
            src = jnp.concatenate([edge_index[0], loop])
            dst = jnp.concatenate([edge_index[1], loop])
            return (src, dst)
        src, dst = add_self_loops(edge_index, x.shape[0])
        h = jax.nn.relu(gcn_conv(x, src, dst, W1, b1))
        out = gcn_conv(h, src, dst, W2, b2)
        return out
    edge_index = jnp.stack([src, dst])
    h = jnp.maximum(_layernorm(x, axis=-1), 0.0)
    x = x + _L0_gnn_ref(h, edge_index, L0_gnn_W, L0_gnn_b)
    h = jnp.maximum(_layernorm(x, axis=-1), 0.0)
    x = x + _L1_gnn_ref(h, edge_weight1, L1_gnn_weight, edge_type_8, src, dst)
    h = jnp.maximum(_layernorm(x, axis=-1), 0.0)
    x = x + _L2_gnn_ref(h, edge_index, edge_attr_32, L2_gnn_q1_w, L2_gnn_q1_b, L2_gnn_k1_w, L2_gnn_k1_b, L2_gnn_v1_w, L2_gnn_v1_b, L2_gnn_e1_w, L2_gnn_s1_w, L2_gnn_s1_b, L2_gnn_q2_w, L2_gnn_q2_b, L2_gnn_k2_w, L2_gnn_k2_b, L2_gnn_v2_w, L2_gnn_v2_b, L2_gnn_e2_w, L2_gnn_s2_w, L2_gnn_s2_b, L2_gnn_skip_w, L2_gnn_skip_b)
    h = jnp.maximum(_layernorm(x, axis=-1), 0.0)
    x = x + _L3_gnn_ref(h, edge_index, L3_gnn_W1, L3_gnn_b1, L3_gnn_W2, L3_gnn_b2)
    return x

_drawn_inputs = setup_inputs


def setup_inputs(seed=0):
    import zlib

    import numpy as np

    out = dict(_drawn_inputs(seed))
    spreads = {'L2_gnn_q1_b': (0.0, 0.8),
     'L2_gnn_k1_b': (0.0, 0.8),
     'L2_gnn_v1_b': (0.0, 0.505),
     'L2_gnn_s1_b': (0.0, 0.383),
     'L2_gnn_q2_b': (0.0, 0.8),
     'L2_gnn_k2_b': (0.0, 0.8),
     'L2_gnn_v2_b': (0.0, 0.699),
     'L2_gnn_s2_b': (0.0, 0.382),
     'L2_gnn_skip_b': (0.0, 0.1),
     'L3_gnn_b1': (0.0, 0.1),
     'L3_gnn_b2': (0.0, 0.1)}
    factors = {'L0_gnn_b': 4.024, 'L2_gnn_k1_w': 3.942, 'L2_gnn_k2_w': 4.711}
    for name, (base, spread) in spreads.items():
        noise = np.random.default_rng([zlib.crc32(name.encode()), seed]).standard_normal(out[name].shape)
        drawn = base * np.exp(spread * noise) if base else spread * noise
        out[name] = jnp.asarray(drawn.astype(out[name].dtype))
    for name, factor in factors.items():
        out[name] = (out[name] * factor).astype(out[name].dtype)
    return out
```

```python
import numpy as np
import concourse.bass as bass
from concourse import mybir
from contextlib import ExitStack

fp32 = mybir.dt.float32
i32 = mybir.dt.int32
bf16 = mybir.dt.bfloat16
fp16 = mybir.dt.float16
ALU = mybir.AluOpType
ACT = mybir.ActivationFunctionType
AXX = mybir.AxisListType.X

P = 128
D = 64
DE = 32
MID = 32
RELS = 8
N = 100000
E = 50000
J = 16
CHUNK = P * J
STEPS = 49
NP = STEPS * CHUNK
LASTP = (N - (STEPS - 1) * CHUNK) // J
B = 8
T = STEPS * B
FULL = E // T
REST = E - FULL * T
COLS = STEPS * J
PADROW = NP + P - 1
HUGE = 3.0e38
EPS = 1e-5
assert (N - (STEPS - 1) * CHUNK) % J == 0 and FULL == P - 1 and NP >= N


class Batch:

    def __init__(self, number, slot, nth):
        self.number, self.slot, self.nth = number, slot, nth


def pipeline(eng, *stages, steps=STEPS, oldest_first=False):
    def step(base, k):
        for d, stage in sorted(enumerate(stages), reverse=oldest_first, key=lambda e: e[0]):
            if isinstance(base, int):
                b = base + k - d
                if 0 <= b < steps:
                    stage(Batch(b, b % 2, b // 2 + 1))
            else:
                o = k - d
                stage(Batch(base * 2 + o, o % 2, base + (o // 2 + 1)))

    lead = (len(stages) - 1 + 1) // 2 * 2
    end = steps // 2 * 2
    for c in range(lead):
        step(0, c)
    with eng.Fori(lead // 2, end // 2) as i:
        step(i, 0)
        step(i, 1)
    for c in range(end, steps + len(stages) - 1):
        step(0, c)


class Link:

    def __init__(self, eng, sem):
        self.eng, self.sem, self.n = eng, sem, 0

    def __call__(self, ins):
        self.n += 1
        ins.then_inc(self.sem, 1)
        self.eng.wait_ge(self.sem, self.n)

    def restart(self):
        self.eng.sem_clear(self.sem)
        self.n = 0


DMA_SIGNALS = {"loaded", "weights", "attrs", "zeroed", "x_in", "stored", "got", "ea_in", "seam_got", "seam_put",
               ("de", "added"), ("dd", "cleared")}


class Room:

    def __init__(self, nc, g, name):
        self.g = g
        self.nc, self.name, self.stack, self.sems = nc, name, ExitStack(), []

    def __enter__(self):
        return self

    def __exit__(self, *e):
        if self.sems and e[0] is None:
            with self.nc.Block() as block:
                @block.sync
                def _(sp):
                    for sem in self.sems:
                        sp.sem_clear(sem)
        return self.stack.__exit__(*e)

    def sb(self, name, shape, dt=fp32):
        return self.stack.enter_context(self.nc.sbuf_tensor(f"{self.name}_{name}", shape, dt))

    def ps(self, name, shape, dt=fp32):
        return self.stack.enter_context(self.nc.psum_tensor(f"{self.name}_{name}", shape, dt))

    def sem(self, name):
        if (self.name, name) in DMA_SIGNALS or name.rstrip("01") in DMA_SIGNALS:
            return self.g.keeper.enter_context(self.nc.semaphore(f"{self.name}_{name}"))
        self.sems.append(self.stack.enter_context(self.nc.semaphore(f"{self.name}_{name}")))
        return self.sems[-1]


def held(eng, sem, value, passed):
    eng.wait_ge(sem, value)
    eng.sem_inc(passed, 1)


def spread(ap, width):
    return ap.unsqueeze(2).to_broadcast([ap.shape[0], ap.shape[1], width])


def each_group(row, groups):
    return row.unsqueeze(1).to_broadcast([row.shape[0], groups, row.shape[1]])


def grouped(ap, width):
    return ap.rearrange("p (g f) -> p g f", f=width)


def chunk_of(table, c):
    return table[0:NP, :].rearrange("(c p j) d -> c p (j d)", p=P, j=J)[c]


def build(nc, a, out):
    with ExitStack() as ctx:
        def keep(name, shape, dt=fp32):
            return ctx.enter_context(nc.sbuf_tensor(name, shape, dt))

        def table(name, rows, width):
            return nc.dram_tensor(name, (rows, width), fp32, kind="Internal").ap()

        g = Graph()
        g.keeper = ctx
        g.passed = ctx.enter_context(nc.semaphore("passed"))
        g.t0 = table("t0", NP, D)
        g.base0 = table("base0", NP, D)
        g.acc0 = table("acc0", NP + P, D)
        g.x1 = table("x1", NP, D)
        g.agg1 = table("agg1", NP, D)
        g.x2 = table("x2", NP, D)
        g.h2 = table("h2", NP, D)
        g.agg2 = table("agg2", NP, D)
        g.g1 = table("g1", NP, D)
        g.agg3 = table("agg3", NP, D)
        g.x3 = table("x3", NP, D)
        g.t3 = table("t3", NP, MID)
        g.agg4 = table("agg4", NP, MID)
        g.t4 = table("t4", NP, MID)
        g.agg5 = table("agg5", NP, MID)
        g.attr = table("attr", P * T, DE)
        g.ident = keep("ident", [P, P])
        g.ones = keep("ones", [P, P])
        g.zeros = keep("zeros", [P, 1024])
        g.eps = keep("eps", [P, 1])
        g.dummy_row = keep("dummy_row", [P, 1])
        g.src_f = keep("src_f", [P, T])
        g.src_rows = keep("src_rows", [P, T], i32)
        g.dst_rows = keep("dst_rows", [P, T], i32)
        g.last_rows = keep("last_rows", [P, T], i32)
        g.dst_f = keep("dst_f", [P, T])
        g.goes_on = keep("goes_on", [P, T])
        g.etype_f = keep("etype_f", [P, T])
        g.norm = keep("norm", [P, T])
        g.dis = keep("dis", [P, COLS])
        g.dinv = keep("dinv", [P, COLS])
        g.first_first = keep("first_first", [P, P])
        g.first_last = keep("first_last", [P, P])
        g.last_first = keep("last_first", [P, P])
        g.last_last = keep("last_last", [P, P])
        g.seam_sum = keep("seam_sum", [P, P])
        g.one_dst = keep("one_dst", [P, 1])
        g.seam_from = keep("seam_from", [P, 1], i32)
        g.seam_to = keep("seam_to", [P, 1], i32)
        for name in PAIR_WEIGHTS:
            setw(g, name, keep("w_" + name, [P, P]))
        for name in ("e1", "e2", "gcn2"):
            setw(g, name, keep("w_" + name, [P, 4 * D]))
        setw(g, "gcn1", keep("w_gcn1", [P, 2 * MID]))
        setw(g, "rel", keep("w_rel", [P, RELS * D]))
        for name in BIASES:
            setw(g, name, keep("b_" + name, [P, D]))

        setup(nc, g, a)
        degrees(nc, g)
        diffusion_dense(nc, g, a)
        diffusion_edges(nc, g)
        diffusion_close(nc, g)
        relation_edges(nc, g)
        norm_dense(nc, g)
        attention_edges(nc, g, "at1", g.h2, g.agg2, ("q1", "k1", "v1", "e1"), ("bq1", "bk1", "bv1"), g.agg3)
        conv_close(nc, g)
        attention_edges(nc, g, "at2", g.g1, g.agg3, ("q2", "k2", "v2", "e2"), ("bq2", "bk2", "bv2"), None)
        skip_dense(nc, g)
        gcn_edges(nc, g, "gc1", g.t3, g.agg4)
        gcn_middle(nc, g)
        gcn_edges(nc, g, "gc2", g.t4, g.agg5)
        gcn_close(nc, g, out)


PAIR_WEIGHTS = {"w0": "W0T", "q1": "L2_gnn_q1_w", "k1": "L2_gnn_k1_w", "v1": "L2_gnn_v1_w", "s1": "L2_gnn_s1_w",
                "q2": "L2_gnn_q2_w", "k2": "L2_gnn_k2_w", "v2": "L2_gnn_v2_w", "s2": "L2_gnn_s2_w",
                "skip_a": "L2_gnn_skip_w", "skip_b": "L2_gnn_skip_w"}
BIASES = {"b0": "L0_gnn_b", "bq1": "L2_gnn_q1_b", "bk1": "L2_gnn_k1_b", "bv1": "L2_gnn_v1_b", "bs1": "L2_gnn_s1_b",
          "bq2": "L2_gnn_q2_b", "bk2": "L2_gnn_k2_b", "bv2": "L2_gnn_v2_b", "bs2": "L2_gnn_s2_b",
          "bskip": "L2_gnn_skip_b", "bg1": "L3_gnn_b1", "bg2": "L3_gnn_b2"}


class Graph:

    def __init__(self):
        self.w = {}


def setw(g, name, ap):
    g.w[name] = ap


def edge_load(eng, tile, flat, sem, shift=0):
    eng.dma_start(tile[0:FULL, :], flat[shift:shift + FULL * T].rearrange("(p t) -> p t", t=T)).then_inc(sem, 16)
    eng.dma_start(tile[FULL:P, 0:REST - shift], flat[FULL * T + shift:E].unsqueeze(0)).then_inc(sem, 16)


def setup(nc, g, a):
    w = g.w
    with Room(nc, g, "setup") as r:
        src_i, dst_i, next_i, type_i = (r.sb(n, [P, T], i32) for n in ("src_i", "dst_i", "next_i", "type_i"))
        next_f, ends, pad = r.sb("next_f", [P, T]), r.sb("ends", [P, T]), r.sb("pad", [P, T])
        diag = r.sb("diag", [P, 2, P])
        before, after = r.sb("before", [P, P]), r.sb("after", [P, P])
        tmp = r.sb("tmp", [P, 4])
        ps_rows = r.ps("ps_rows", [P, 2 * P])
        cleared, loaded, weights, link_s, dve_diag, pe_rows, made, attrs = (r.sem(n) for n in (
            "cleared", "loaded", "weights", "link", "dve_diag", "pe_rows", "made", "attrs"))
        with nc.Block() as block:
            @block.vector
            def _(dve):
                link = Link(dve, link_s)
                for t in w:
                    nc.vector.memset(w[t][:, :], 0.0)
                for t, v in ((src_i, PADROW), (dst_i, PADROW), (next_i, PADROW), (type_i, 0)):
                    nc.vector.memset(t[:, :], v)
                nc.vector.memset(g.norm[:, :], 0.0)
                nc.vector.memset(g.eps[:, :], EPS)
                nc.vector.memset(g.ones[:, :], 1.0)
                nc.vector.memset(g.zeros[:, :], 0.0).then_inc(cleared, 1)
                dve.wait_ge(loaded, 5 * 32)
                link(nc.vector.tensor_copy(g.src_f[:, :], src_i[:, :]))
                link(nc.vector.tensor_copy(g.dst_f[:, :], dst_i[:, :]))
                link(nc.vector.tensor_copy(next_f[:, :], next_i[:, :]))
                link(nc.vector.tensor_copy(g.etype_f[:, :], type_i[:, :]))
                link(nc.vector.tensor_scalar(g.src_rows[:, :], g.src_f[:, :], float(N - 1), None, ALU.min))
                link(nc.vector.tensor_scalar(g.dst_rows[:, :], g.dst_f[:, :], float(N - 1), None, ALU.min))
                link(nc.vector.tensor_tensor(ends[:, :], g.dst_f[:, :], next_f[:, :], ALU.is_equal))
                link(nc.vector.memset(g.goes_on[:, 0:1], 0.0))
                link(nc.vector.tensor_copy(g.goes_on[:, 1:T], ends[:, 0:T - 1]))
                link(nc.vector.tensor_scalar(pad[:, :], ends[:, :], float(2 * NP), None, ALU.mult))
                link(nc.vector.tensor_tensor(g.last_rows[:, :], pad[:, :], g.dst_f[:, :], ALU.add))
                dve.wait_ge(made, 4)
                link(nc.vector.tensor_scalar(diag[:, 0, :], g.ident[:, :], g.dst_f[:, 0:1], None, ALU.mult))
                nc.vector.tensor_scalar(diag[:, 1, :], g.ident[:, :], g.dst_f[:, T - 1:T], None, ALU.mult).then_inc(dve_diag, 1)
                dve.wait_ge(pe_rows, 1)
                firsts, lasts = ps_rows[:, 0:P], ps_rows[:, P:2 * P]
                first, last = g.dst_f[:, 0:1], g.dst_f[:, T - 1:T]
                link(nc.vector.tensor_scalar(g.first_first[:, :], firsts, first, None, ALU.is_equal))
                link(nc.vector.tensor_scalar(g.first_last[:, :], lasts, first, None, ALU.is_equal))
                link(nc.vector.tensor_scalar(g.last_first[:, :], firsts, last, None, ALU.is_equal))
                link(nc.vector.tensor_scalar(g.last_last[:, :], lasts, last, None, ALU.is_equal))
                nc.vector.tensor_tensor(g.one_dst[:, :], first, last, ALU.is_equal).then_inc(dve_diag, 1)
                link(nc.vector.tensor_tensor(diag[:, 0, :], g.first_last[:, :], before[:, :], ALU.mult))
                link(nc.vector.tensor_reduce(tmp[:, 2:3], diag[:, 0, :], AXX, ALU.add))
                link(nc.vector.tensor_tensor(diag[:, 0, :], g.first_first[:, :], after[:, :], ALU.mult))
                link(nc.vector.tensor_reduce(tmp[:, 3:4], diag[:, 0, :], AXX, ALU.add))
                link(nc.vector.tensor_scalar(tmp[:, 2:4], tmp[:, 2:4], 1.0, None, ALU.min))
                link(nc.vector.tensor_scalar(tmp[:, 3:4], tmp[:, 3:4], -1.0, 1.0, ALU.mult, ALU.add))
                link(nc.vector.tensor_tensor(tmp[:, 0:1], tmp[:, 2:3], tmp[:, 3:4], ALU.mult))
                link(nc.vector.tensor_scalar(tmp[:, 0:1], tmp[:, 0:1], float(-2 * NP), float(2 * NP), ALU.mult, ALU.add))
                link(nc.vector.tensor_tensor(g.seam_to[:, :], tmp[:, 0:1], first, ALU.add))
                link(nc.vector.tensor_copy(g.seam_from[:, :], g.dst_rows[:, 0:1]))

            @block.tensor
            def _(pe):
                pe.wait_ge(dve_diag, 1)
                nc.tensor.matmul(ps_rows[:, 0:P], g.ones[:, :], diag[:, 0, :], start=True, stop=True)
                nc.tensor.matmul(ps_rows[:, P:2 * P], g.ones[:, :], diag[:, 1, :], start=True, stop=True).then_inc(pe_rows, 1)

            @block.gpsimd
            def _(pool):
                nc.gpsimd.iota(g.dummy_row[:, :], pattern=[[0, 1]], base=NP, channel_multiplier=1,
                               allow_small_or_imprecise_dtypes=True).then_inc(made, 1)
                pool.wait_ge(cleared, 1)
                nc.gpsimd.affine_select(out=g.ident[:, :], in_=g.zeros[:, 0:P], compare_op=ALU.not_equal, fill=1.0,
                                        base=0, pattern=[[-1, P]], channel_multiplier=1).then_inc(made, 1)
                for mask, sign in ((before, -1), (after, 1)):
                    nc.gpsimd.affine_select(out=mask[:, :], in_=g.ones[:, :], compare_op=ALU.is_gt, fill=0.0,
                                            base=0, pattern=[[sign, P]], channel_multiplier=-sign).then_inc(made, 1)
                pool.wait_ge(dve_diag, 2)
                nc.gpsimd.affine_select(out=g.seam_sum[:, :], in_=g.last_first[:, :], compare_op=ALU.is_gt, fill=0.0,
                                        base=0, pattern=[[1, P]], channel_multiplier=-1)

            @block.sync
            def _(sp):
                sp.wait_ge(cleared, 1)
                edge_load(sp, src_i, a["src"], loaded)
                edge_load(sp, dst_i, a["dst"], loaded)
                edge_load(sp, next_i, a["dst"], loaded, shift=1)
                edge_load(sp, type_i, a["edge_type_8"], loaded)
                edge_load(sp, g.norm, a["edge_weight1"].rearrange("e o -> (e o)"), loaded)
                sp.dma_start(g.attr[0:E, :].rearrange("(p k) d -> p (k d)", p=80),
                             a["edge_attr_32"].rearrange("(p k) d -> p (k d)", p=80)).then_inc(attrs, 16)
                sp.dma_start(g.attr[E:P * T, :].rearrange("(p k) d -> p (k d)", p=16),
                             g.zeros[0:16, 0:(P * T - E) * DE // 16]).then_inc(attrs, 16)
                sp.wait_ge(attrs, 32)
                sp.wait_ge(loaded, 5 * 32)

            @block.scalar
            def _(act):
                act.wait_ge(cleared, 1)
                count = 0

                def load(dst, src):
                    act.dma_start(dst, src).then_inc(weights, 16)

                for name, given in PAIR_WEIGHTS.items():
                    rows = a[given]
                    rows = rows[D:2 * D, :] if name == "skip_b" else rows[0:D, :]
                    for k in range(2):
                        load(w[name][k * D:(k + 1) * D, k * D:(k + 1) * D], rows)
                        count += 1
                for name, given in (("e1", "L2_gnn_e1_w"), ("e2", "L2_gnn_e2_w"), ("gcn2", "L3_gnn_W2")):
                    for k in range(4):
                        load(w[name][k * DE:(k + 1) * DE, k * D:(k + 1) * D], a[given])
                        count += 1
                for k in range(2):
                    load(w["gcn1"][k * D:(k + 1) * D, k * MID:(k + 1) * MID], a["L3_gnn_W1"])
                    load(w["rel"][k * D:(k + 1) * D, :].rearrange("i (r o) -> i r o", r=RELS),
                         a["L1_gnn_weight"].rearrange("r i o -> i r o"))
                    count += 2
                for name, given in BIASES.items():
                    f = a[given].shape[0]
                    load(w[name][:, 0:f], a[given].unsqueeze(0).to_broadcast([P, f]))
                    count += 1
                act.wait_ge(weights, 16 * count)


def degrees(nc, g):
    with Room(nc, g, "deg") as r:
        as_int, part_i = r.sb("as_int", [P, T], i32), r.sb("part_i", [P, T], i32)
        low_f, chunk_f, part_f = ([r.sb(f"{n}{k}", [P, T]) for k in range(2)] for n in ("low", "chunk", "part"))
        col_f = [r.sb(f"col{k}", [P, T]) for k in range(2)]
        iota = r.sb("iota", [P, COLS], fp16)
        hot_part = r.sb("hot_part", [P, 2, 2, B, P], bf16)
        hot_col = r.sb("hot_col", [P, 2, 2, B, COLS], bf16)
        blank = r.sb("blank", [P, P], bf16)
        counts = [r.ps(f"counts{k}", [P, 1024]) for k in range(2)]
        link_s, ready, hot, used, counted, root, rooted = (r.sem(n) for n in ("link", "ready", "hot", "used", "counted", "root", "rooted"))
        HALVES = ((0, 512), (512, COLS))
        with nc.Block() as block:
            @block.gpsimd
            def _(pool):
                nc.gpsimd.iota(iota[:, :], pattern=[[1, COLS]], base=0, channel_multiplier=0,
                               allow_small_or_imprecise_dtypes=True).then_inc(ready, 1)

            @block.vector
            def _(dve):
                link = Link(dve, link_s)
                link(nc.vector.memset(blank[:, :], 0.0))
                for k, index in enumerate((g.src_f, g.dst_f)):
                    link(nc.vector.tensor_copy(as_int[:, :], index[:, :]))
                    link(nc.vector.tensor_scalar(part_i[:, :], as_int[:, :], 4, 127, ALU.logical_shift_right, ALU.bitwise_and))
                    link(nc.vector.tensor_copy(part_f[k][:, :], part_i[:, :]))
                    link(nc.vector.tensor_scalar(part_i[:, :], as_int[:, :], 15, None, ALU.bitwise_and))
                    link(nc.vector.tensor_copy(low_f[k][:, :], part_i[:, :]))
                    link(nc.vector.tensor_scalar(part_i[:, :], as_int[:, :], 11, None, ALU.logical_shift_right))
                    link(nc.vector.tensor_copy(chunk_f[k][:, :], part_i[:, :]))
                    link(nc.vector.scalar_tensor_tensor(col_f[k][:, :], chunk_f[k][:, :], float(J), low_f[k][:, :], ALU.mult, ALU.add))
                dve.wait_ge(ready, 1)
                nc.vector.sem_inc(used, 2)

                def one_hot(b):
                    dve.wait_ge(used, b.number + 1)
                    last = None
                    for k in range(2):
                        for t in range(B):
                            at = bass.ds(b.number * B + t, 1)
                            nc.vector.tensor_scalar(hot_part[:, b.slot, k, t, :], iota[:, 0:P], part_f[k][:, at], None, ALU.is_equal)
                            last = nc.vector.tensor_scalar(hot_col[:, b.slot, k, t, :], iota[:, :], col_f[k][:, at], None, ALU.is_equal)
                    last.then_inc(hot, 1)
                pipeline(dve, one_hot)
                dve.wait_ge(counted, 1)
                for k, to in enumerate((g.dis, g.dinv)):
                    link(nc.vector.tensor_scalar(to[:, :], counts[k][:, 0:COLS], 1.0, None, ALU.add))
                    link(nc.vector.reciprocal(to[:, :], to[:, :]))
                nc.vector.sem_inc(root, 1)

            @block.tensor
            def _(pe):
                pe.wait_ge(hot, 1)
                for k in range(2):
                    for lo, hi in HALVES:
                        nc.tensor.matmul(counts[k][:, lo:hi], blank[:, :], hot_col[:, 0, k, 0, lo:hi], start=True, stop=False)

                def count(b):
                    pe.wait_ge(hot, b.number + 1)
                    last = None
                    for k in range(2):
                        for t in range(B):
                            for lo, hi in HALVES:
                                last = nc.tensor.matmul(counts[k][:, lo:hi], hot_part[:, b.slot, k, t, :],
                                                        hot_col[:, b.slot, k, t, lo:hi], start=False, stop=False)
                    last.then_inc(used, 1)
                pipeline(pe, count)
                for k in range(2):
                    for lo, hi in HALVES:
                        last = nc.tensor.matmul(counts[k][:, lo:hi], blank[:, :], hot_col[:, 0, k, 0, lo:hi], start=False, stop=True)
                last.then_inc(counted, 1)

            @block.scalar
            def _(act):
                act.wait_ge(root, 1)
                nc.scalar.activation(g.dis[:, :], g.dis[:, :], ACT.Sqrt)
                nc.scalar.activation(g.dinv[:, :], g.dinv[:, :], ACT.Sqrt).then_inc(rooted, 1)
                act.wait_ge(rooted, 1)

            @block.sync
            def _(sp):
                zero_table(sp, g, g.acc0, NP + P, r.sem("zeroed"))


def zero_table(sp, g, table, rows, done):
    width = table.shape[1]
    span = 1024 // width
    n = 0
    whole = rows // (P * span)
    view = table[0:whole * P * span, :].rearrange("(c p j) d -> p c (j d)", p=P, j=span)
    for c in range(0, whole, 14):
        m = min(14, whole - c)
        sp.dma_start(view[:, c:c + m, :], g.zeros[:, :].unsqueeze(1).to_broadcast([P, m, 1024])).then_inc(done, 16)
        n += 1
    rest = rows - whole * P * span
    if rest:
        sp.dma_start(table[whole * P * span:rows, :].rearrange("(p j) d -> p (j d)", p=P),
                     g.zeros[:, 0:rest // P * width]).then_inc(done, 16)
        n += 1
    sp.wait_ge(done, 16 * n)


def transpose_pairs(nc, to, src, ident, n):
    for k in range(n):
        last = nc.tensor.transpose(to[:, k * P:(k + 1) * P], src[:, k * P:(k + 1) * P], ident[:, :])
    return last


def times(nc, to, left, weight, n, start=True, stop=True):
    wide = weight.shape[1]
    for k in range(n):
        last = nc.tensor.matmul(to[:, k * wide:(k + 1) * wide], left[:, k * P:(k + 1) * P], weight[:, :],
                                start=start, stop=stop, skip_group_check=not (start and stop))
    return last


def mean_off(nc, link, x, centred, sums, groups):
    link(nc.vector.tensor_reduce(sums, grouped(x, D), AXX, ALU.add))
    link(nc.vector.tensor_scalar(sums, sums, -1.0 / D, None, ALU.mult))
    return nc.vector.tensor_tensor(grouped(centred, D), grouped(x, D), spread(sums, D), ALU.add)


def diffusion_dense(nc, g, a):
    W = J * D
    with Room(nc, g, "dd") as r:
        x, cen, sq, lo, hi, hT = ([r.sb(f"{n}{k}", [P, W]) for k in range(2)] for n in ("x", "cen", "sq", "t0", "base", "hT"))
        h0, rl = r.sb("h0", [P, W]), r.sb("rl", [P, W])
        sums, sd = r.sb("sums", [P, 2, J]), r.sb("sd", [P, 2, J])
        psT = [r.ps(f"psT{k}", [P, W]) for k in range(2)]
        psH = [r.ps(f"psH{k}", [P, W]) for k in range(2)]
        x_in = [r.sem(f"x_in{k}") for k in range(2)]
        stored = [r.sem(f"stored{k}") for k in range(2)]
        x_free, o_free, link_s, squared, centred, summed, rooted, normed, turned, evac, product, ready, cleared = (r.sem(n) for n in (
            "x_free", "o_free", "link", "squared", "centred", "summed", "rooted", "normed", "turned", "evac", "product", "ready", "cleared"))
        with nc.Block() as block:
            @block.sync
            def _(sp):
                sp.sem_inc(x_free, 2)
                view = a["x"]

                def load(b):
                    sp.wait_ge(x_free, b.number + 1)
                    if isinstance(b.number, int) and b.number == STEPS - 1:
                        sp.dma_start(x[b.slot][LASTP:P, :], g.zeros[LASTP:P, :]).then_inc(cleared, 16)
                        sp.wait_ge(cleared, 16)
                        sp.dma_start(x[b.slot][0:LASTP, :], view[(STEPS - 1) * CHUNK:N, :].rearrange("(p j) d -> p (j d)", j=J)).then_inc(x_in[b.slot], 16)
                    else:
                        whole = view[0:(STEPS - 1) * CHUNK, :].rearrange("(c p j) d -> c p (j d)", p=P, j=J)
                        sp.dma_start(x[b.slot][:, :], whole[b.number]).then_inc(x_in[b.slot], 16)
                pipeline(sp, load)

            @block.vector
            def _(dve):
                link = Link(dve, link_s)

                def centre(b):
                    s = b.slot
                    dve.wait_ge(x_in[s], 16 * b.nth)
                    mean_off(nc, link, x[s][:, :], cen[s][:, :], sums[:, s, :], J).then_inc(centred, 1)

                def variance(b):
                    s = b.slot
                    dve.wait_ge(squared, b.number + 1)
                    nc.vector.tensor_reduce(sd[:, s, :], grouped(sq[s][:, :], D), AXX, ALU.add).then_inc(summed, 1)

                def scale(b):
                    s = b.slot
                    dve.wait_ge(rooted, b.number + 1)
                    link(nc.vector.reciprocal(sd[:, s, :], sd[:, s, :]))
                    nc.vector.tensor_tensor(grouped(cen[s][:, :], D), grouped(cen[s][:, :], D), spread(sd[:, s, :], D), ALU.mult).then_inc(normed, 1)

                def close(b):
                    s = b.slot
                    dve.wait_ge(product, b.number + 1)
                    dve.wait_ge(o_free, b.number + 1)
                    dis = g.dis[:, bass.ds(b.number * J, J)]
                    link(nc.vector.tensor_tensor(grouped(h0[:, :], D), grouped(psH[s][:, :], D), each_group(g.w["b0"][:, :], J), ALU.add))
                    link(nc.vector.tensor_tensor(grouped(lo[s][:, :], D), grouped(h0[:, :], D), spread(dis, D), ALU.mult))
                    link(nc.vector.scalar_tensor_tensor(hi[s][:, :], h0[:, :], 0.95, x[s][:, :], ALU.mult, ALU.add))
                    link(nc.vector.tensor_scalar(rl[:, :], h0[:, :], 0.0, 1.5, ALU.max, ALU.mult))
                    link(nc.vector.tensor_tensor(hi[s][:, :], hi[s][:, :], rl[:, :], ALU.add))
                    link(nc.vector.tensor_tensor(grouped(rl[:, :], D), grouped(lo[s][:, :], D), spread(dis, D), ALU.mult))
                    link.restart()
                    nc.vector.scalar_tensor_tensor(hi[s][:, :], rl[:, :], 0.05, hi[s][:, :], ALU.mult, ALU.add).then_inc(ready, 1)
                    dve.wait_ge(ready, b.number + 1)
                    nc.vector.sem_inc(x_free, 1)

                def all_of(b):
                    centre(b)
                    variance(b)
                    scale(b)
                pipeline(dve, all_of, close)

            @block.scalar
            def _(act):
                def norm(b):
                    s = b.slot
                    act.wait_ge(centred, b.number + 1)
                    nc.scalar.activation(sq[s][:, :], cen[s][:, :], ACT.Square).then_inc(squared, 1)
                    act.wait_ge(summed, b.number + 1)
                    nc.scalar.activation(sd[:, s, :], sd[:, s, :], ACT.Sqrt, bias=g.eps[:, :], scale=1.0 / D).then_inc(rooted, 1)

                def turn(b):
                    s = b.slot
                    act.wait_ge(turned, b.number + 1)
                    nc.scalar.activation(hT[s][:, :], psT[s][:, :], ACT.Relu).then_inc(evac, 1)
                pipeline(act, norm, turn)

            @block.tensor
            def _(pe):
                def turn(b):
                    s = b.slot
                    pe.wait_ge(normed, b.number + 1)
                    transpose_pairs(nc, psT[s], cen[s], g.ident, J // 2).then_inc(turned, 1)
                    pe.wait_ge(evac, b.number + 1)
                    times(nc, psH[s], hT[s], g.w["w0"], J // 2).then_inc(product, 1)
                pipeline(pe, turn)

            @block.gpsimd
            def _(pool):
                pool.sem_inc(o_free, 2)

                def store(b):
                    s = b.slot
                    held(pool, ready, b.number + 1, g.passed)
                    pool.dma_start(chunk_of(g.t0, b.number), lo[s][:, :]).then_inc(stored[s], 16)
                    pool.dma_start(chunk_of(g.base0, b.number), hi[s][:, :]).then_inc(stored[s], 16)

                def landed(b):
                    held(pool, stored[b.slot], 32 * b.nth, g.passed)
                    pool.sem_inc(o_free, 1)
                pipeline(pool, store, landed, oldest_first=True)


def gather(nc, buf, table, rows, sem, groups=B):
    width = table.shape[1]
    for t in range(groups):
        nc.gpsimd.indirect_dma_start(buf[:, t * width:(t + 1) * width], None, table,
                                     bass.IndirectOffsetOnAxis(ap=rows[:, t:t + 1], axis=0)).then_inc(sem, 16)


def scatter_rows(nc, buf, table, rows, sem, groups=B):
    width = table.shape[1]
    for t in range(groups):
        nc.gpsimd.indirect_dma_start(table[0:N, :], bass.IndirectOffsetOnAxis(ap=rows[:, t:t + 1], axis=0),
                                     buf[:, t * width:(t + 1) * width], None,
                                     bounds_check=N - 1, oob_is_err=False).then_inc(sem, 16)


def diffusion_edges(nc, g):
    W = B * D
    with Room(nc, g, "de") as r:
        rows = [r.sb(f"rows{k}", [P, W]) for k in range(2)]
        summed = [r.sb(f"summed{k}", [P, W]) for k in range(2)]
        take = [r.sb(f"take{k}", [P, B], i32) for k in range(2)]
        put = [r.sb(f"put{k}", [P, B], i32) for k in range(2)]
        diag = r.sb("diag", [P, B, P])
        same = [r.sb(f"same{k}", [P, B, P]) for k in range(2)]
        later = r.sb("later", [P, P])
        dup, toward = r.sb("dup", [P, B]), r.sb("toward", [P, B])
        ps_src = r.ps("ps_src", [P, B * P])
        ps_sum = [r.ps(f"ps_sum{k}", [P, W]) for k in range(2)]
        got = [r.sem(f"got{k}") for k in range(2)]
        free, link_s, staged, mask, dve_diag, src_rows, same_made, product, ready, added, zeroed = (r.sem(n) for n in (
            "free", "link", "staged", "mask", "dve_diag", "src_rows", "same_made", "product", "ready", "added", "zeroed"))
        with nc.Block() as block:
            @block.gpsimd
            def _(pool):
                nc.gpsimd.affine_select(out=later[:, :], in_=g.ones[:, :], compare_op=ALU.is_gt, fill=0.0,
                                        base=0, pattern=[[1, P]], channel_multiplier=-1).then_inc(mask, 1)
                pool.sem_inc(free, 2)

                def fetch(b):
                    s = b.slot
                    held(pool, free, b.number + 1, g.passed)
                    nc.gpsimd.tensor_copy(take[s][:, :], g.dst_rows[:, bass.ds(b.number * B, B)]).then_inc(staged, 1)
                    held(pool, staged, b.number + 1, g.passed)

                def add(b):
                    held(pool, ready, b.number + 1, g.passed)

                def both(f, d):
                    for t in range(B):
                        if f is not None:
                            s = f.slot
                            nc.gpsimd.indirect_dma_start(rows[s][:, t * D:(t + 1) * D], None, g.t0,
                                                         bass.IndirectOffsetOnAxis(ap=take[s][:, t:t + 1], axis=0)).then_inc(got[s], 16)
                        if d is not None:
                            s = d.slot
                            if not (isinstance(d.number, int) and d.number == 0 and t == 0):
                                held(pool, added, 16 * (d.number * B + t), g.passed)
                            nc.gpsimd.indirect_dma_start(g.acc0, bass.IndirectOffsetOnAxis(ap=put[s][:, t:t + 1], axis=0),
                                                         summed[s][:, t * D:(t + 1) * D], None, compute_op=ALU.add).then_inc(added, 16)

                for c in (0, 1):
                    fetch(Batch(c, c, 1))
                    both(Batch(c, c, 1), None)
                with pool.Fori(1, STEPS // 2) as i:
                    for k in range(2):
                        f, d = Batch(i * 2 + k, k, i + 1), Batch(i * 2 + k - 2, k, i)
                        add(d)
                        fetch(f)
                        both(f, d)
                last, d = Batch(STEPS - 1, 0, STEPS // 2 + 1), Batch(STEPS - 3, 0, STEPS // 2)
                add(d)
                fetch(last)
                both(last, d)
                for d in (Batch(STEPS - 2, 1, 0), Batch(STEPS - 1, 0, 0)):
                    add(d)
                    both(None, d)
                pool.wait_ge(added, 16 * T)

            @block.vector
            def _(dve):
                link = Link(dve, link_s)
                dve.wait_ge(mask, 1)

                def equal(b):
                    s = b.slot
                    src = g.src_f[:, bass.ds(b.number * B, B)]
                    nc.vector.tensor_tensor(diag[:, :, :], each_group(g.ident[:, :], B), spread(src, P), ALU.mult).then_inc(dve_diag, 1)
                    dve.wait_ge(src_rows, b.number + 1)
                    link(nc.vector.tensor_tensor(same[s][:, :, :], ps_src[:, :].rearrange("p (b q) -> p b q", q=P), spread(src, P), ALU.is_equal))
                    nc.vector.sem_inc(same_made, 1)
                    link(nc.vector.tensor_tensor(diag[:, :, :], same[s][:, :, :], each_group(later[:, :], B), ALU.mult))
                    link(nc.vector.tensor_reduce(dup[:, :], diag[:, :, :], AXX, ALU.max))
                    link(nc.vector.tensor_scalar(toward[:, :], src, -1.0, g.dummy_row[:, :], ALU.mult, ALU.add))
                    link(nc.vector.tensor_tensor(toward[:, :], toward[:, :], dup[:, :], ALU.mult))
                    if not (isinstance(b.number, int) and b.number < 2):
                        dve.wait_ge(added, 16 * B * (b.number - 1))
                    link(nc.vector.tensor_tensor(put[s][:, :], toward[:, :], src, ALU.add))
                    link.restart()

                def carry(b):
                    s = b.slot
                    dve.wait_ge(product, b.number + 1)
                    nc.vector.tensor_copy(summed[s][:, :], ps_sum[s][:, :]).then_inc(ready, 1)
                    dve.wait_ge(ready, b.number + 1)
                pipeline_from_two(dve, equal, carry)

            @block.tensor
            def _(pe):
                def turn(b):
                    pe.wait_ge(dve_diag, b.number + 1)
                    for h in range(2):
                        last = nc.tensor.matmul(ps_src[:, h * 512:(h + 1) * 512], g.ones[:, :],
                                                diag[:, :, :].rearrange("p b q -> p (b q)")[:, h * 512:(h + 1) * 512], start=True, stop=True)
                    last.then_inc(src_rows, 1)

                def merge(b):
                    s = b.slot
                    pe.wait_ge(same_made, b.number + 1)
                    pe.wait_ge(got[s], 16 * B * b.nth)
                    for t in range(B):
                        last = nc.tensor.matmul(ps_sum[s][:, t * D:(t + 1) * D], same[s][:, t, :],
                                                rows[s][:, t * D:(t + 1) * D], start=True, stop=True)
                    last.then_inc(product, 1)
                    pe.wait_ge(product, b.number + 1)
                    pe.sem_inc(free, 1)
                pipeline(pe, turn, merge)


def pipeline_from_two(eng, *stages):
    first, second = stages

    def at(c, k=None):
        return Batch(c, c % 2, c // 2 + 1)
    first(at(0))
    first(at(1))
    second(at(0))
    with eng.Fori(1, STEPS // 2) as i:
        first(Batch(i * 2, 0, i + 1))
        second(Batch(i * 2 - 1, 1, i))
        first(Batch(i * 2 + 1, 1, i + 1))
        second(Batch(i * 2, 0, i + 1))
    first(at(STEPS - 1))
    second(at(STEPS - 2))
    second(at(STEPS - 1))


def diffusion_close(nc, g):
    W = J * D
    with Room(nc, g, "dc") as r:
        base, acc = ([r.sb(f"{n}{k}", [P, W]) for k in range(2)] for n in ("base", "acc"))
        tiny = r.sb("tiny", [P, COLS])
        x_in, stored = ([r.sem(f"{n}{k}") for k in range(2)] for n in ("x_in", "stored"))
        free, link_s, ready, zeroed = (r.sem(n) for n in ("free", "link", "ready", "zeroed"))
        with nc.Block() as block:
            @block.sync
            def _(sp):
                sp.sem_inc(free, 2)

                def load(b):
                    sp.wait_ge(free, b.number + 1)
                    sp.dma_start(base[b.slot][:, :], chunk_of(g.base0, b.number)).then_inc(x_in[b.slot], 16)
                    sp.dma_start(acc[b.slot][:, :], chunk_of(g.acc0, b.number)).then_inc(x_in[b.slot], 16)
                pipeline(sp, load)

            @block.vector
            def _(dve):
                link = Link(dve, link_s)
                link(nc.vector.tensor_scalar(tiny[:, :], g.dis[:, :], 0.05, None, ALU.mult))

                def close(b):
                    s = b.slot
                    link.restart()
                    dve.wait_ge(x_in[s], 32 * b.nth)
                    link(nc.vector.tensor_tensor(grouped(acc[s][:, :], D), grouped(acc[s][:, :], D), spread(tiny[:, bass.ds(b.number * J, J)], D), ALU.mult))
                    nc.vector.tensor_tensor(base[s][:, :], base[s][:, :], acc[s][:, :], ALU.add).then_inc(ready, 1)
                pipeline(dve, close)

            @block.scalar
            def _(act):
                def store(b):
                    s = b.slot
                    act.wait_ge(ready, b.number + 1)
                    act.dma_start(chunk_of(g.x1, b.number), base[s][:, :]).then_inc(stored[s], 16)

                def landed(b):
                    act.wait_ge(stored[b.slot], 16 * b.nth)
                    act.sem_inc(free, 1)
                pipeline(act, store, landed, oldest_first=True)

            @block.gpsimd
            def _(pool):
                zero_table(pool, g, g.agg1, NP, zeroed)


def running_sums(nc, link, tot, slot, msg, g, b, width):
    for t in range(B):
        if t == B - 1:
            link.restart()
        before = tot[slot][:, (t - 1) * width:t * width] if t else tot[1 - slot][:, (B - 1) * width:B * width]
        ins = nc.vector.scalar_tensor_tensor(tot[slot][:, t * width:(t + 1) * width], before,
                                             g.goes_on[:, bass.ds(b.number * B + t, 1)],
                                             msg[:, t * width:(t + 1) * width], ALU.mult, ALU.add)
        if t < B - 1:
            link(ins)
    return ins


def seam(nc, g, r, agg, tot, width):
    row, carried = r.sb("seam_row", [P, width]), r.sb("seam_sum", [P, width])
    ps = r.ps("seam_ps", [P, width])
    got, product, summed, put = (r.sem("seam_" + n) for n in ("got", "product", "summed", "put"))
    with nc.Block() as block:
        @block.tensor
        def _(pe):
            nc.tensor.matmul(ps[:, :], g.seam_sum[:, :], tot[:, (B - 1) * width:B * width], start=True, stop=True).then_inc(product, 1)

        @block.gpsimd
        def _(pool):
            gather(nc, row, agg, g.seam_from, got, groups=1)
            pool.wait_ge(summed, 1)
            scatter_rows(nc, carried, agg, g.seam_to, put, groups=1)
            pool.wait_ge(put, 16)

        @block.vector
        def _(dve):
            dve.wait_ge(product, 1)
            dve.wait_ge(got, 16)
            nc.vector.tensor_tensor(carried[:, :], row[:, :], ps[:, :], ALU.add).then_inc(summed, 1)


def relation_edges(nc, g):
    W = B * D
    with Room(nc, g, "re") as r:
        rows, hT, tot, cen = ([r.sb(f"{n}{k}", [P, W]) for k in range(2)] for n in ("rows", "hT", "tot", "cen"))
        take, put = ([r.sb(f"{n}{k}", [P, B], i32) for k in range(2)] for n in ("take", "put"))
        sq, msg = (r.sb(n, [P, W]) for n in ("sq", "msg"))
        sums, sd = r.sb("sums", [P, B]), r.sb("sd", [P, B])
        rel = r.sb("rel", [P, RELS])
        coef = r.sb("coef", [P, B, RELS])
        picked = [r.sb(f"picked{k}", [P, RELS * D]) for k in range(2)]
        psT = r.ps("psT", [P, W])
        psR = [r.ps(f"psR{k}", [P, RELS * D]) for k in range(4)]
        got, stored = ([r.sem(f"{n}{k}") for k in range(2)] for n in ("got", "stored"))
        free, sum_free, link_s, relno, staged, staged_put, centred, squared, summed, rooted, normed, turned, evac, product, read, ready, zeroed = (r.sem(n) for n in (
            "free", "sum_free", "link", "relno", "staged", "staged_put", "centred", "squared", "summed", "rooted", "normed", "turned", "evac", "product", "read", "ready", "zeroed"))
        with nc.Block() as block:
            @block.gpsimd
            def _(pool):
                nc.gpsimd.iota(rel[:, :], pattern=[[1, RELS]], base=0, channel_multiplier=0,
                               allow_small_or_imprecise_dtypes=True).then_inc(relno, 1)
                pool.sem_inc(free, 2)
                pool.sem_inc(sum_free, 2)

                def fetch(b):
                    s = b.slot
                    held(pool, free, b.number + 1, g.passed)
                    nc.gpsimd.tensor_copy(take[s][:, :], g.src_rows[:, bass.ds(b.number * B, B)]).then_inc(staged, 1)
                    held(pool, staged, b.number + 1, g.passed)
                    gather(nc, rows[s], g.x1, take[s], got[s])

                def send(b):
                    s = b.slot
                    held(pool, ready, b.number + 1, g.passed)
                    nc.gpsimd.tensor_copy(put[s][:, :], g.last_rows[:, bass.ds(b.number * B, B)]).then_inc(staged_put, 1)
                    held(pool, staged_put, b.number + 1, g.passed)
                    scatter_rows(nc, tot[s], g.agg1, put[s], stored[s])

                def landed(b):
                    held(pool, stored[b.slot], 16 * B * b.nth, g.passed)
                    pool.sem_inc(sum_free, 1)

                interleave(pool, fetch, send, landed)

            @block.vector
            def _(dve):
                link = Link(dve, link_s)
                dve.wait_ge(relno, 1)
                link(nc.vector.memset(tot[1][:, :], 0.0))
                link.restart()

                def norm(b):
                    s = b.slot
                    dve.wait_ge(got[s], 16 * B * b.nth)
                    mean_off(nc, link, rows[s][:, :], cen[s][:, :], sums[:, :], B).then_inc(centred, 1)
                    dve.wait_ge(centred, b.number + 1)
                    nc.vector.sem_inc(free, 1)
                    dve.wait_ge(squared, b.number + 1)
                    nc.vector.tensor_reduce(sd[:, :], grouped(sq[:, :], D), AXX, ALU.add).then_inc(summed, 1)
                    dve.wait_ge(rooted, b.number + 1)
                    link(nc.vector.reciprocal(sd[:, :], sd[:, :]))
                    nc.vector.tensor_tensor(grouped(cen[s][:, :], D), grouped(cen[s][:, :], D), spread(sd[:, :], D), ALU.mult).then_inc(normed, 1)

                def pick(b):
                    s = b.slot
                    at = bass.ds(b.number * B, B)
                    link(nc.vector.tensor_tensor(coef[:, :, :], each_group(rel[:, :], B), spread(g.etype_f[:, at], RELS), ALU.is_equal))
                    link(nc.vector.tensor_tensor(coef[:, :, :], coef[:, :, :], spread(g.norm[:, at], RELS), ALU.mult))
                    for t in range(B):
                        dve.wait_ge(product, b.number * B + t + 1)
                        last = nc.vector.tensor_tensor(grouped(picked[t % 2][:, :], D), grouped(psR[t % 4][:, :], D),
                                                       spread(coef[:, t, :], D), ALU.mult)
                        last.then_inc(read, 1)
                        dve.wait_ge(read, b.number * B + t + 1)
                        link(nc.vector.tensor_reduce(msg[:, t * D:(t + 1) * D], picked[t % 2][:, :].rearrange("p (r o) -> p o r", r=RELS), AXX, ALU.add))
                    dve.wait_ge(sum_free, b.number + 1)
                    running_sums(nc, link, tot, s, msg, g, b, D).then_inc(ready, 1)
                    dve.wait_ge(ready, b.number + 1)
                pipeline(dve, norm, pick)

            @block.scalar
            def _(act):
                def norm(b):
                    act.wait_ge(centred, b.number + 1)
                    nc.scalar.activation(sq[:, :], cen[b.slot][:, :], ACT.Square).then_inc(squared, 1)
                    act.wait_ge(summed, b.number + 1)
                    nc.scalar.activation(sd[:, :], sd[:, :], ACT.Sqrt, bias=g.eps[:, :], scale=1.0 / D).then_inc(rooted, 1)
                    act.wait_ge(turned, b.number + 1)
                    nc.scalar.activation(hT[b.slot][:, :], psT[:, :], ACT.Relu).then_inc(evac, 1)
                pipeline(act, norm)

            @block.tensor
            def _(pe):
                def turn(b):
                    pe.wait_ge(normed, b.number + 1)
                    transpose_pairs(nc, psT, cen[b.slot], g.ident, B // 2).then_inc(turned, 1)

                def relate(b):
                    s = b.slot
                    pe.wait_ge(evac, b.number + 1)
                    for t in range(B):
                        if not (isinstance(b.number, int) and b.number == 0 and t < 4):
                            pe.wait_ge(read, b.number * B + (t - 3))
                        h = (t % 2) * D
                        nc.tensor.matmul(psR[t % 4][:, :], hT[s][h:h + D, (t // 2) * P:(t // 2 + 1) * P],
                                         g.w["rel"][h:h + D, :], start=True, stop=True).then_inc(product, 1)
                turn(Batch(0, 0, 1))
                relate(Batch(0, 0, 1))
                with pe.Fori(0, STEPS // 2) as i:
                    for k in range(2):
                        turn(Batch(i * 2 + (k + 1), (k + 1) % 2, None))
                        relate(Batch(i * 2 + (k + 1), (k + 1) % 2, None))

            @block.sync
            def _(sp):
                zero_table(sp, g, g.agg2, NP, zeroed)
        seam(nc, g, r, g.agg1, tot[(STEPS - 1) % 2], D)


def interleave(eng, fetch, send, landed, lag=2):
    pipeline(eng, fetch, lambda b: None, send, landed)


def norm_dense(nc, g):
    W = J * D
    with Room(nc, g, "nd") as r:
        x, agg, cen, sq, h = ([r.sb(f"{n}{k}", [P, W]) for k in range(2)] for n in ("x", "agg", "cen", "sq", "h"))
        sums, sd = r.sb("sums", [P, 2, J]), r.sb("sd", [P, 2, J])
        x_in, stored = ([r.sem(f"{n}{k}") for k in range(2)] for n in ("x_in", "stored"))
        free, link_s, added, centred, squared, summed, rooted, normed, ready = (r.sem(n) for n in (
            "free", "link", "added", "centred", "squared", "summed", "rooted", "normed", "ready"))
        with nc.Block() as block:
            @block.sync
            def _(sp):
                sp.sem_inc(free, 2)

                def load(b):
                    sp.wait_ge(free, b.number + 1)
                    sp.dma_start(x[b.slot][:, :], chunk_of(g.x1, b.number)).then_inc(x_in[b.slot], 16)
                    sp.dma_start(agg[b.slot][:, :], chunk_of(g.agg1, b.number)).then_inc(x_in[b.slot], 16)
                pipeline(sp, load)

            @block.vector
            def _(dve):
                link = Link(dve, link_s)

                def centre(b):
                    s = b.slot
                    link.restart()
                    dve.wait_ge(x_in[s], 32 * b.nth)
                    nc.vector.tensor_tensor(x[s][:, :], x[s][:, :], agg[s][:, :], ALU.add).then_inc(added, 1)
                    dve.wait_ge(added, b.number + 1)
                    mean_off(nc, link, x[s][:, :], cen[s][:, :], sums[:, s, :], J).then_inc(centred, 1)

                def scale(b):
                    s = b.slot
                    dve.wait_ge(squared, b.number + 1)
                    nc.vector.tensor_reduce(sd[:, s, :], grouped(sq[s][:, :], D), AXX, ALU.add).then_inc(summed, 1)
                    dve.wait_ge(rooted, b.number + 1)
                    link(nc.vector.reciprocal(sd[:, s, :], sd[:, s, :]))
                    nc.vector.tensor_tensor(grouped(cen[s][:, :], D), grouped(cen[s][:, :], D), spread(sd[:, s, :], D), ALU.mult).then_inc(normed, 1)
                pipeline(dve, centre, scale)

            @block.scalar
            def _(act):
                def norm(b):
                    s = b.slot
                    act.wait_ge(centred, b.number + 1)
                    nc.scalar.activation(sq[s][:, :], cen[s][:, :], ACT.Square).then_inc(squared, 1)

                def relu(b):
                    s = b.slot
                    act.wait_ge(summed, b.number + 1)
                    nc.scalar.activation(sd[:, s, :], sd[:, s, :], ACT.Sqrt, bias=g.eps[:, :], scale=1.0 / D).then_inc(rooted, 1)
                    act.wait_ge(normed, b.number + 1)
                    nc.scalar.activation(h[s][:, :], cen[s][:, :], ACT.Relu).then_inc(ready, 1)
                pipeline(act, norm, relu)

            @block.gpsimd
            def _(pool):
                def store(b):
                    s = b.slot
                    held(pool, ready, b.number + 1, g.passed)
                    held(pool, added, b.number + 1, g.passed)
                    pool.dma_start(chunk_of(g.x2, b.number), x[s][:, :]).then_inc(stored[s], 16)
                    pool.dma_start(chunk_of(g.h2, b.number), h[s][:, :]).then_inc(stored[s], 16)

                def landed(b):
                    held(pool, stored[b.slot], 32 * b.nth, g.passed)
                    pool.sem_inc(free, 1)
                pipeline(pool, store, landed, oldest_first=True)


def attention_edges(nc, g, name, nodes, agg, weights, biases, clear):
    with Room(nc, g, name) as r:
        scores = r.sb("scores", [P, T])
        values = r.sb("values", [P, T * D])
        attention_scores(nc, g, name, nodes, weights, biases, clear, scores, values)
        segment_softmax(nc, g, name, scores)
        attention_sums(nc, g, name, agg, scores, values)


def attention_scores(nc, g, name, nodes, weights, biases, clear, scores, values):
    W = B * D
    wq, wk, wv, we = (g.w[n] for n in weights)
    bq, bk, bv = (g.w[n] for n in biases)
    with Room(nc, g, name + "s") as r:
        hs, hd = ([r.sb(f"{n}{k}", [P, W]) for k in range(2)] for n in ("hs", "hd"))
        ea = [r.sb(f"ea{k}", [P, B * DE]) for k in range(2)]
        take_s, take_d = ([r.sb(f"{n}{k}", [P, B], i32) for k in range(2)] for n in ("take_s", "take_d"))
        hsT, hdT, eaT, q, k_ = (r.sb(n, [P, w]) for n, w in (("hsT", W), ("hdT", W), ("eaT", B * DE), ("q", W), ("k", W)))
        psS, psD, psE, psQ, psK, psV = (r.ps(n, [P, 512]) for n in ("psS", "psD", "psE", "psQ", "psK", "psV"))
        got, ea_in = ([r.sem(f"{n}{k}") for k in range(2)] for n in ("got", "ea_in"))
        free, staged, link_s, turned, evac, product, used, zeroed = (r.sem(n) for n in (
            "free", "staged", "link", "turned", "evac", "product", "used", "zeroed"))
        with nc.Block() as block:
            @block.gpsimd
            def _(pool):
                def fetch(b):
                    s = b.slot
                    held(pool, free, b.number + 1, g.passed)
                    nc.gpsimd.tensor_copy(take_s[s][:, :], g.src_rows[:, bass.ds(b.number * B, B)])
                    nc.gpsimd.tensor_copy(take_d[s][:, :], g.dst_rows[:, bass.ds(b.number * B, B)]).then_inc(staged, 1)
                    held(pool, staged, b.number + 1, g.passed)
                    gather(nc, hs[s], nodes, take_s[s], got[s])
                    gather(nc, hd[s], nodes, take_d[s], got[s])
                pipeline(pool, fetch)

            @block.sync
            def _(sp):
                rows = g.attr.rearrange("(p c t) d -> c p (t d)", p=P, t=B)

                def load(b):
                    sp.wait_ge(free, b.number + 1)
                    sp.dma_start(ea[b.slot][:, :], rows[b.number]).then_inc(ea_in[b.slot], 16)
                pipeline(sp, load)
                if clear is not None:
                    zero_table(sp, g, clear, NP, zeroed)
                else:
                    zero_table(sp, g, g.agg4, NP, zeroed)

            @block.tensor
            def _(pe):
                pe.sem_inc(free, 2)

                def turn(b):
                    s = b.slot
                    pe.wait_ge(got[s], 16 * 2 * B * b.nth)
                    pe.wait_ge(ea_in[s], 16 * b.nth)
                    transpose_pairs(nc, psS, hs[s], g.ident, B // 2)
                    transpose_pairs(nc, psD, hd[s], g.ident, B // 2)
                    transpose_pairs(nc, psE, ea[s], g.ident, B // 4).then_inc(turned, 1)
                    pe.wait_ge(turned, b.number + 1)
                    pe.sem_inc(free, 1)

                def project(b):
                    pe.wait_ge(evac, b.number + 1)
                    if not (isinstance(b.number, int) and b.number == 0):
                        pe.wait_ge(used, b.number)
                    times(nc, psQ, hdT, wq, B // 2)
                    for to, w in ((psK, wk), (psV, wv)):
                        for h in range(2):
                            nc.tensor.matmul(to[:, h * 256:(h + 1) * 256], eaT[:, h * P:(h + 1) * P], we[:, :], start=True, stop=False,
                                             skip_group_check=True)
                            for k in range(2):
                                j = 2 * h + k
                                last = nc.tensor.matmul(to[:, j * P:(j + 1) * P], hsT[:, j * P:(j + 1) * P], w[:, :], start=False, stop=(k == 1),
                                                        skip_group_check=True)
                    last.then_inc(product, 1)
                pipeline_first_peeled(pe, turn, project)

            @block.scalar
            def _(act):
                def turn(b):
                    act.wait_ge(turned, b.number + 1)
                    if not (isinstance(b.number, int) and b.number == 0):
                        act.wait_ge(product, b.number)
                    nc.scalar.activation(hsT[:, :], psS[:, :], ACT.Copy)
                    nc.scalar.activation(hdT[:, :], psD[:, :], ACT.Copy)
                    nc.scalar.activation(eaT[:, :], psE[:, 0:B * DE], ACT.Copy).then_inc(evac, 1)
                first_peeled(act, turn)

            @block.vector
            def _(dve):
                link = Link(dve, link_s)

                def score(b):
                    link.restart()
                    dve.wait_ge(product, b.number + 1)
                    nc.vector.tensor_tensor(grouped(q[:, :], D), grouped(psQ[:, :], D), each_group(bq[:, :], B), ALU.add)
                    nc.vector.tensor_tensor(grouped(values[:, bass.ds(b.number * W, W)], D), grouped(psV[:, :], D), each_group(bv[:, :], B), ALU.add)
                    nc.vector.tensor_tensor(grouped(k_[:, :], D), grouped(psK[:, :], D), each_group(bk[:, :], B), ALU.add).then_inc(used, 1)
                    dve.wait_ge(used, b.number + 1)
                    link(nc.vector.tensor_tensor(q[:, :], q[:, :], k_[:, :], ALU.mult))
                    link(nc.vector.tensor_reduce(scores[:, bass.ds(b.number * B, B)], grouped(q[:, :], D), AXX, ALU.add))
                pipeline(dve, score)


def first_peeled(eng, stage):
    stage(Batch(0, 0, 1))
    with eng.Fori(0, STEPS // 2) as i:
        stage(Batch(i * 2 + 1, 1, i + 1))
        stage(Batch(i * 2 + 2, 0, i + 2))


def pipeline_first_peeled(eng, turn, project):
    def both(b):
        turn(b)
        project(b)
    first_peeled(eng, both)


def segment_softmax(nc, g, name, scores):
    with Room(nc, g, name + "m") as r:
        fence, fence_back, keep_back, last = (r.sb(n, [P, T]) for n in ("fence", "fence_back", "keep_back", "last"))
        fwd, full, at_first, at_last, ends = (r.sb(n, [P, T]) for n in ("fwd", "full", "at_first", "at_last", "ends"))
        diag = r.sb("diag", [P, 2, P])
        near_first, near_last = r.sb("near_first", [P, 2, P]), r.sb("near_last", [P, 2, P])
        masks = r.sb("masks", [P, 2, 2, P])
        both = r.sb("both", [P, 2])
        tail = r.sb("tail", [P, 1])
        two = r.sb("two", [P, 1])
        ps = r.ps("ps", [P, 2 * P])
        link_s, spread_s, rows_s, shifted, exped = (r.sem(n) for n in ("link", "diag", "rows", "shifted", "exped"))
        rev = slice(None, None, -1)
        with nc.Block() as block:
            @block.tensor
            def _(pe):
                for n in range(2):
                    pe.wait_ge(spread_s, n + 1)
                    nc.tensor.matmul(ps[:, :], g.ones[:, :], diag[:, :, :].rearrange("p a q -> p (a q)"), start=True, stop=True).then_inc(rows_s, 1)

            @block.scalar
            def _(act):
                act.wait_ge(shifted, 1)
                nc.scalar.activation(scores[:, :], scores[:, :], ACT.Exp, scale=0.125).then_inc(exped, 1)

            @block.vector
            def _(dve):
                link = Link(dve, link_s)
                v = nc.vector
                link(v.tensor_scalar(fence[:, :], g.goes_on[:, :], HUGE, -HUGE, ALU.mult, ALU.add))
                link(v.memset(keep_back[:, T - 1:T], 0.0))
                link(v.tensor_copy(keep_back[:, 0:T - 1], g.goes_on[:, 1:T]))
                link(v.tensor_scalar(fence_back[:, :], keep_back[:, :], HUGE, -HUGE, ALU.mult, ALU.add))
                link(v.tensor_scalar(last[:, :], keep_back[:, :], -1.0, 1.0, ALU.mult, ALU.add))
                link(v.tensor_scalar(at_first[:, :], g.dst_f[:, :], g.dst_f[:, 0:1], None, ALU.is_equal))
                link(v.tensor_scalar(at_last[:, :], g.dst_f[:, :], g.dst_f[:, T - 1:T], None, ALU.is_equal))
                link(v.tensor_tensor(tail[:, :], g.dst_f[:, 0:1], g.dst_f[:, T - 1:T], ALU.not_equal))
                for k, m in enumerate((g.first_first, g.first_last, g.last_first, g.last_last)):
                    link(v.tensor_copy(masks[:, k // 2, k % 2, :], m[:, :]))

                def ends_of(a, z, n):
                    link(v.tensor_scalar(diag[:, 0, :], g.ident[:, :], a, None, ALU.mult))
                    v.tensor_scalar(diag[:, 1, :], g.ident[:, :], z, None, ALU.mult).then_inc(spread_s, 1)
                    dve.wait_ge(rows_s, n)

                rows = ps[:, :].rearrange("p (a q) -> p a q", q=P)
                link(v.tensor_tensor_scan(fwd[:, :], fence[:, :], scores[:, :], 0.0, ALU.add, ALU.max))
                link(v.tensor_tensor_scan(full[:, rev], fence_back[:, rev], fwd[:, rev], 0.0, ALU.add, ALU.max))
                ends_of(full[:, 0:1], fwd[:, T - 1:T], 1)
                for k, near in enumerate((near_first, near_last)):
                    link(v.tensor_scalar(near[:, :, :], masks[:, k, :, :], HUGE, -HUGE, ALU.mult, ALU.add))
                    link(v.tensor_tensor(near[:, :, :], near[:, :, :], rows, ALU.add))
                    link(v.tensor_reduce(both[:, k:k + 1], near[:, :, :].rearrange("p a q -> p (a q)"), AXX, ALU.max))
                for k, at in enumerate((at_first, at_last)):
                    link(v.tensor_scalar(ends[:, :], at[:, :], HUGE, -HUGE, ALU.mult, ALU.add))
                    link(v.scalar_tensor_tensor(full[:, :], ends[:, :], both[:, k:k + 1], full[:, :], ALU.add, ALU.max))
                v.tensor_tensor(scores[:, :], scores[:, :], full[:, :], ALU.subtract).then_inc(shifted, 1)
                dve.wait_ge(exped, 1)
                link(v.tensor_tensor_scan(fwd[:, :], g.goes_on[:, :], scores[:, :], 0.0, ALU.mult, ALU.add))
                link(v.tensor_tensor(last[:, :], last[:, :], fwd[:, :], ALU.mult))
                link(v.tensor_tensor_scan(full[:, rev], keep_back[:, rev], last[:, rev], 0.0, ALU.mult, ALU.add))
                link(v.tensor_tensor(two[:, :], fwd[:, T - 1:T], tail[:, :], ALU.mult))
                ends_of(full[:, 0:1], two[:, :], 2)
                for k, near in enumerate((near_first, near_last)):
                    link(v.tensor_tensor(near[:, :, :], masks[:, k, :, :], rows, ALU.mult))
                    link(v.tensor_reduce(both[:, k:k + 1], near[:, :, :].rearrange("p a q -> p (a q)"), AXX, ALU.add))
                for k, at in enumerate((at_first, at_last)):
                    link(v.scalar_tensor_tensor(full[:, :], at[:, :], both[:, k:k + 1], full[:, :], ALU.mult, ALU.max))
                link(v.reciprocal(full[:, :], full[:, :]))
                link(v.tensor_tensor(scores[:, :], scores[:, :], full[:, :], ALU.mult))


def attention_sums(nc, g, name, agg, alpha, values):
    W = B * D
    with Room(nc, g, name + "w") as r:
        tot = [r.sb(f"tot{k}", [P, W]) for k in range(2)]
        put = [r.sb(f"put{k}", [P, B], i32) for k in range(2)]
        msg = r.sb("msg", [P, W])
        stored = [r.sem(f"stored{k}") for k in range(2)]
        sum_free, link_s, staged, ready = (r.sem(n) for n in ("sum_free", "link", "staged", "ready"))
        with nc.Block() as block:
            @block.vector
            def _(dve):
                link = Link(dve, link_s)
                link(nc.vector.memset(tot[1][:, :], 0.0))
                link.restart()

                def add(b):
                    s = b.slot
                    dve.wait_ge(sum_free, b.number + 1)
                    link(nc.vector.tensor_tensor(grouped(msg[:, :], D), grouped(values[:, bass.ds(b.number * W, W)], D),
                                                 spread(alpha[:, bass.ds(b.number * B, B)], D), ALU.mult))
                    running_sums(nc, link, tot, s, msg, g, b, D).then_inc(ready, 1)
                    dve.wait_ge(ready, b.number + 1)
                pipeline(dve, add)

            @block.gpsimd
            def _(pool):
                pool.sem_inc(sum_free, 2)
                scatter_pipeline(nc, pool, g, tot, put, agg, ready, staged, stored, sum_free)
        seam(nc, g, r, agg, tot[(STEPS - 1) % 2], D)


def scatter_pipeline(nc, pool, g, tot, put, agg, ready, staged, stored, sum_free):
    def send(b):
        s = b.slot
        held(pool, ready, b.number + 1, g.passed)
        nc.gpsimd.tensor_copy(put[s][:, :], g.last_rows[:, bass.ds(b.number * B, B)]).then_inc(staged, 1)
        held(pool, staged, b.number + 1, g.passed)
        scatter_rows(nc, tot[s], agg, put[s], stored[s])

    def landed(b):
        held(pool, stored[b.slot], 16 * B * b.nth, g.passed)
        pool.sem_inc(sum_free, 1)
    pipeline(pool, send, landed)


def conv_close(nc, g):
    W = J * D
    with Room(nc, g, "cc") as r:
        h, agg, hT, o = ([r.sb(f"{n}{k}", [P, W]) for k in range(2)] for n in ("h", "agg", "hT", "o"))
        psT, psH = ([r.ps(f"{n}{k}", [P, W]) for k in range(2)] for n in ("psT", "psH"))
        x_in, stored = ([r.sem(f"{n}{k}") for k in range(2)] for n in ("x_in", "stored"))
        x_free, o_free, link_s, turned, evac, product, summed, ready = (r.sem(n) for n in (
            "x_free", "o_free", "link", "turned", "evac", "product", "summed", "ready"))
        with nc.Block() as block:
            @block.sync
            def _(sp):
                sp.sem_inc(x_free, 2)

                def load(b):
                    sp.wait_ge(x_free, b.number + 1)
                    sp.dma_start(h[b.slot][:, :], chunk_of(g.h2, b.number)).then_inc(x_in[b.slot], 16)
                    sp.dma_start(agg[b.slot][:, :], chunk_of(g.agg2, b.number)).then_inc(x_in[b.slot], 16)
                pipeline(sp, load)

            @block.tensor
            def _(pe):
                def turn(b):
                    pe.wait_ge(x_in[b.slot], 32 * b.nth)
                    transpose_pairs(nc, psT[b.slot], h[b.slot], g.ident, J // 2).then_inc(turned, 1)

                def project(b):
                    pe.wait_ge(evac, b.number + 1)
                    times(nc, psH[b.slot], hT[b.slot], g.w["s1"], J // 2).then_inc(product, 1)
                pipeline(pe, turn, project)

            @block.vector
            def _(dve):
                link = Link(dve, link_s)

                def turn(b):
                    dve.wait_ge(turned, b.number + 1)
                    nc.vector.tensor_copy(hT[b.slot][:, :], psT[b.slot][:, :]).then_inc(evac, 1)

                def close(b):
                    s = b.slot
                    link.restart()
                    dve.wait_ge(x_in[s], 32 * b.nth)
                    dve.wait_ge(product, b.number + 1)
                    link(nc.vector.tensor_tensor(agg[s][:, :], agg[s][:, :], psH[s][:, :], ALU.add))
                    nc.vector.tensor_tensor(grouped(agg[s][:, :], D), grouped(agg[s][:, :], D), each_group(g.w["bs1"][:, :], J), ALU.add).then_inc(summed, 1)
                pipeline(dve, turn, close)

            @block.scalar
            def _(act):
                def relu(b):
                    s = b.slot
                    act.wait_ge(summed, b.number + 1)
                    act.wait_ge(o_free, b.number + 1)
                    nc.scalar.activation(o[s][:, :], agg[s][:, :], ACT.Relu).then_inc(ready, 1)
                    act.wait_ge(ready, b.number + 1)
                    act.sem_inc(x_free, 1)
                pipeline(act, relu)

            @block.gpsimd
            def _(pool):
                pool.sem_inc(o_free, 2)

                def store(b):
                    held(pool, ready, b.number + 1, g.passed)
                    pool.dma_start(chunk_of(g.g1, b.number), o[b.slot][:, :]).then_inc(stored[b.slot], 16)

                def landed(b):
                    held(pool, stored[b.slot], 16 * b.nth, g.passed)
                    pool.sem_inc(o_free, 1)
                pipeline(pool, store, landed, oldest_first=True)


def skip_dense(nc, g):
    W = J * D
    with Room(nc, g, "sk") as r:
        x, agg, g1, gT, g2T = ([r.sb(f"{n}{k}", [P, W]) for k in range(2)] for n in ("x", "agg", "g1", "gT", "g2T"))
        cen, hT = ([r.sb(f"{n}{k}", [P, W]) for k in range(2)] for n in ("cen", "hT"))
        sq = r.sb("sq", [P, W])
        o = [r.sb(f"o{k}", [P, J * MID]) for k in range(2)]
        sums, sd = r.sb("sums", [P, 2, J]), r.sb("sd", [P, 2, J])
        psA, psB, psC = (r.ps(n, [P, W]) for n in ("psA", "psB", "psC"))
        x_in, stored = ([r.sem(f"{n}{k}") for k in range(2)] for n in ("x_in", "stored"))
        names = ("free", "link", "turned1", "evac1", "made1", "pre2", "turned2", "evac2", "made2", "relu2", "centred", "squared",
                 "summed", "rooted", "normed", "turned3", "evac3", "made3", "ready", "added")
        (free, link_s, turned1, evac1, made1, pre2, turned2, evac2, made2, relu2, centred, squared,
         summed, rooted, normed, turned3, evac3, made3, ready, added) = (r.sem(n) for n in names)
        with nc.Block() as block:
            @block.sync
            def _(sp):
                sp.sem_inc(free, 2)

                def load(b):
                    sp.wait_ge(free, b.number + 1)
                    sp.dma_start(x[b.slot][:, :], chunk_of(g.x2, b.number)).then_inc(x_in[b.slot], 16)
                    sp.dma_start(agg[b.slot][:, :], chunk_of(g.agg3, b.number)).then_inc(x_in[b.slot], 16)
                    sp.dma_start(g1[b.slot][:, :], chunk_of(g.g1, b.number)).then_inc(x_in[b.slot], 16)
                pipeline(sp, load)

            @block.tensor
            def _(pe):
                def all_of(b):
                    s = b.slot
                    pe.wait_ge(x_in[s], 48 * b.nth)
                    transpose_pairs(nc, psA, g1[s], g.ident, J // 2).then_inc(turned1, 1)
                    pe.wait_ge(evac1, b.number + 1)
                    if not (isinstance(b.number, int) and b.number == 0):
                        pe.wait_ge(ready, b.number)
                    times(nc, psB, gT[s], g.w["s2"], J // 2).then_inc(made1, 1)
                    pe.wait_ge(pre2, b.number + 1)
                    transpose_pairs(nc, psA, agg[s], g.ident, J // 2).then_inc(turned2, 1)
                    pe.wait_ge(evac2, b.number + 1)
                    for k in range(J // 2):
                        nc.tensor.matmul(psC[:, k * P:(k + 1) * P], gT[s][:, k * P:(k + 1) * P], g.w["skip_a"][:, :], start=True, stop=False)
                        last = nc.tensor.matmul(psC[:, k * P:(k + 1) * P], g2T[s][:, k * P:(k + 1) * P], g.w["skip_b"][:, :], start=False, stop=True)
                    last.then_inc(made2, 1)
                    pe.wait_ge(normed, b.number + 1)
                    transpose_pairs(nc, psA, cen[s], g.ident, J // 2).then_inc(turned3, 1)
                    pe.wait_ge(evac3, b.number + 1)
                    times(nc, psB[:, 0:J * MID], hT[s], g.w["gcn1"], J // 2).then_inc(made3, 1)
                first_peeled(pe, all_of)

            @block.scalar
            def _(act):
                def all_of(b):
                    s = b.slot
                    act.wait_ge(turned1, b.number + 1)
                    nc.scalar.activation(gT[s][:, :], psA[:, :], ACT.Copy).then_inc(evac1, 1)
                    act.wait_ge(turned2, b.number + 1)
                    nc.scalar.activation(g2T[s][:, :], psA[:, :], ACT.Relu).then_inc(evac2, 1)
                    act.wait_ge(centred, b.number + 1)
                    nc.scalar.activation(sq[:, :], cen[s][:, :], ACT.Square).then_inc(squared, 1)
                    act.wait_ge(summed, b.number + 1)
                    nc.scalar.activation(sd[:, s, :], sd[:, s, :], ACT.Sqrt, bias=g.eps[:, :], scale=1.0 / D).then_inc(rooted, 1)
                    act.wait_ge(turned3, b.number + 1)
                    nc.scalar.activation(hT[s][:, :], psA[:, :], ACT.Relu).then_inc(evac3, 1)
                pipeline(act, all_of)

            @block.vector
            def _(dve):
                link = Link(dve, link_s)

                def all_of(b):
                    s = b.slot
                    dve.wait_ge(x_in[s], 48 * b.nth)
                    dve.wait_ge(made1, b.number + 1)
                    link(nc.vector.tensor_tensor(agg[s][:, :], agg[s][:, :], psB[:, :], ALU.add))
                    nc.vector.tensor_tensor(grouped(agg[s][:, :], D), grouped(agg[s][:, :], D), each_group(g.w["bs2"][:, :], J), ALU.add).then_inc(pre2, 1)
                    dve.wait_ge(made2, b.number + 1)
                    link(nc.vector.tensor_tensor(grouped(g1[s][:, :], D), grouped(psC[:, :], D), each_group(g.w["bskip"][:, :], J), ALU.add))
                    nc.vector.scalar_tensor_tensor(x[s][:, :], g1[s][:, :], 0.0, x[s][:, :], ALU.max, ALU.add).then_inc(added, 1)
                    dve.wait_ge(added, b.number + 1)
                    mean_off(nc, link, x[s][:, :], cen[s][:, :], sums[:, s, :], J).then_inc(centred, 1)
                    dve.wait_ge(squared, b.number + 1)
                    nc.vector.tensor_reduce(sd[:, s, :], grouped(sq[:, :], D), AXX, ALU.add).then_inc(summed, 1)
                    dve.wait_ge(rooted, b.number + 1)
                    link(nc.vector.reciprocal(sd[:, s, :], sd[:, s, :]))
                    link.restart()
                    nc.vector.tensor_tensor(grouped(cen[s][:, :], D), grouped(cen[s][:, :], D), spread(sd[:, s, :], D), ALU.mult).then_inc(normed, 1)
                    dve.wait_ge(made3, b.number + 1)
                    nc.vector.tensor_tensor(grouped(o[s][:, :], MID), grouped(psB[:, 0:J * MID], MID),
                                            spread(g.dinv[:, bass.ds(b.number * J, J)], MID), ALU.mult).then_inc(ready, 1)
                    dve.wait_ge(ready, b.number + 1)
                pipeline(dve, all_of)

            @block.gpsimd
            def _(pool):
                def store(b):
                    s = b.slot
                    held(pool, added, b.number + 1, g.passed)
                    pool.dma_start(chunk_of(g.x3, b.number), x[s][:, :]).then_inc(stored[s], 16)
                    held(pool, ready, b.number + 1, g.passed)
                    pool.dma_start(chunk_of(g.t3, b.number), o[s][:, :]).then_inc(stored[s], 16)

                def landed(b):
                    held(pool, stored[b.slot], 32 * b.nth, g.passed)
                    pool.sem_inc(free, 1)
                pipeline(pool, store, landed, oldest_first=True)


def gcn_edges(nc, g, name, nodes, agg):
    W = B * MID
    with Room(nc, g, name) as r:
        rows, tot = ([r.sb(f"{n}{k}", [P, W]) for k in range(2)] for n in ("rows", "tot"))
        take, put = ([r.sb(f"{n}{k}", [P, B], i32) for k in range(2)] for n in ("take", "put"))
        got, stored = ([r.sem(f"{n}{k}") for k in range(2)] for n in ("got", "stored"))
        free, sum_free, link_s, staged, staged_put, ready, zeroed = (r.sem(n) for n in (
            "free", "sum_free", "link", "staged", "staged_put", "ready", "zeroed"))
        with nc.Block() as block:
            @block.gpsimd
            def _(pool):
                pool.sem_inc(free, 2)
                pool.sem_inc(sum_free, 2)

                def fetch(b):
                    s = b.slot
                    held(pool, free, b.number + 1, g.passed)
                    nc.gpsimd.tensor_copy(take[s][:, :], g.src_rows[:, bass.ds(b.number * B, B)]).then_inc(staged, 1)
                    held(pool, staged, b.number + 1, g.passed)
                    gather(nc, rows[s], nodes, take[s], got[s])

                def send(b):
                    s = b.slot
                    held(pool, ready, b.number + 1, g.passed)
                    nc.gpsimd.tensor_copy(put[s][:, :], g.last_rows[:, bass.ds(b.number * B, B)]).then_inc(staged_put, 1)
                    held(pool, staged_put, b.number + 1, g.passed)
                    scatter_rows(nc, tot[s], agg, put[s], stored[s])

                def landed(b):
                    held(pool, stored[b.slot], 16 * B * b.nth, g.passed)
                    pool.sem_inc(sum_free, 1)
                pipeline(pool, fetch, send, landed)

            @block.vector
            def _(dve):
                link = Link(dve, link_s)
                link(nc.vector.memset(tot[1][:, :], 0.0))
                link.restart()

                def add(b):
                    s = b.slot
                    dve.wait_ge(got[s], 16 * B * b.nth)
                    dve.wait_ge(sum_free, b.number + 1)
                    running_sums(nc, link, tot, s, rows[s], g, b, MID).then_inc(ready, 1)
                    dve.wait_ge(ready, b.number + 1)
                    nc.vector.sem_inc(free, 1)
                pipeline(dve, add)

            if name == "gc1":
                @block.sync
                def _(sp):
                    zero_table(sp, g, g.agg5, NP, zeroed)
        seam(nc, g, r, agg, tot[(STEPS - 1) % 2], MID)


def gcn_middle(nc, g):
    W = J * MID
    with Room(nc, g, "gm") as r:
        t3, agg, o = ([r.sb(f"{n}{k}", [P, W]) for k in range(2)] for n in ("t3", "agg", "o"))
        x_in, stored = ([r.sem(f"{n}{k}") for k in range(2)] for n in ("x_in", "stored"))
        free, link_s, ready = (r.sem(n) for n in ("free", "link", "ready"))
        with nc.Block() as block:
            @block.sync
            def _(sp):
                sp.sem_inc(free, 2)

                def load(b):
                    sp.wait_ge(free, b.number + 1)
                    sp.dma_start(t3[b.slot][:, :], chunk_of(g.t3, b.number)).then_inc(x_in[b.slot], 16)
                    sp.dma_start(agg[b.slot][:, :], chunk_of(g.agg4, b.number)).then_inc(x_in[b.slot], 16)
                pipeline(sp, load)

            @block.vector
            def _(dve):
                link = Link(dve, link_s)

                def close(b):
                    s = b.slot
                    dinv = spread(g.dinv[:, bass.ds(b.number * J, J)], MID)
                    link.restart()
                    dve.wait_ge(x_in[s], 32 * b.nth)
                    link(nc.vector.tensor_tensor(t3[s][:, :], t3[s][:, :], agg[s][:, :], ALU.add))
                    link(nc.vector.tensor_tensor(grouped(t3[s][:, :], MID), grouped(t3[s][:, :], MID), dinv, ALU.mult))
                    link(nc.vector.tensor_tensor(grouped(t3[s][:, :], MID), grouped(t3[s][:, :], MID), each_group(g.w["bg1"][:, 0:MID], J), ALU.add))
                    link(nc.vector.tensor_scalar(t3[s][:, :], t3[s][:, :], 0.0, None, ALU.max))
                    nc.vector.tensor_tensor(grouped(o[s][:, :], MID), grouped(t3[s][:, :], MID), dinv, ALU.mult).then_inc(ready, 1)
                pipeline(dve, close)

            @block.scalar
            def _(act):
                def store(b):
                    act.wait_ge(ready, b.number + 1)
                    act.dma_start(chunk_of(g.t4, b.number), o[b.slot][:, :]).then_inc(stored[b.slot], 16)

                def landed(b):
                    act.wait_ge(stored[b.slot], 16 * b.nth)
                    act.sem_inc(free, 1)
                pipeline(act, store, landed, oldest_first=True)


def gcn_close(nc, g, out):
    W = J * D
    M = J * MID
    with Room(nc, g, "gf") as r:
        x = [r.sb(f"x{k}", [P, W]) for k in range(2)]
        t4, agg, uT = ([r.sb(f"{n}{k}", [P, M]) for k in range(2)] for n in ("t4", "agg", "uT"))
        psT = [r.ps(f"psT{k}", [P, M]) for k in range(2)]
        psH = [r.ps(f"psH{k}", [P, W]) for k in range(2)]
        x_in, stored = ([r.sem(f"{n}{k}") for k in range(2)] for n in ("x_in", "stored"))
        free, link_s, scaled, turned, evac, product, ready = (r.sem(n) for n in (
            "free", "link", "scaled", "turned", "evac", "product", "ready"))
        with nc.Block() as block:
            @block.sync
            def _(sp):
                sp.sem_inc(free, 2)

                def load(b):
                    sp.wait_ge(free, b.number + 1)
                    sp.dma_start(t4[b.slot][:, :], chunk_of(g.t4, b.number)).then_inc(x_in[b.slot], 16)
                    sp.dma_start(agg[b.slot][:, :], chunk_of(g.agg5, b.number)).then_inc(x_in[b.slot], 16)
                    sp.dma_start(x[b.slot][:, :], chunk_of(g.x3, b.number)).then_inc(x_in[b.slot], 16)
                pipeline(sp, load)

            @block.vector
            def _(dve):
                link = Link(dve, link_s)

                def scale(b):
                    s = b.slot
                    link.restart()
                    dve.wait_ge(x_in[s], 48 * b.nth)
                    link(nc.vector.tensor_tensor(t4[s][:, :], t4[s][:, :], agg[s][:, :], ALU.add))
                    nc.vector.tensor_tensor(grouped(t4[s][:, :], MID), grouped(t4[s][:, :], MID),
                                            spread(g.dinv[:, bass.ds(b.number * J, J)], MID), ALU.mult).then_inc(scaled, 1)

                def close(b):
                    s = b.slot
                    dve.wait_ge(product, b.number + 1)
                    link(nc.vector.tensor_tensor(x[s][:, :], x[s][:, :], psH[s][:, :], ALU.add))
                    nc.vector.tensor_tensor(grouped(x[s][:, :], D), grouped(x[s][:, :], D), each_group(g.w["bg2"][:, :], J), ALU.add).then_inc(ready, 1)
                pipeline(dve, scale, close)

            @block.tensor
            def _(pe):
                def turn(b):
                    s = b.slot
                    pe.wait_ge(scaled, b.number + 1)
                    transpose_pairs(nc, psT[s], t4[s], g.ident, J // 4).then_inc(turned, 1)

                def project(b):
                    s = b.slot
                    pe.wait_ge(evac, b.number + 1)
                    times(nc, psH[s], uT[s], g.w["gcn2"], J // 4).then_inc(product, 1)
                pipeline(pe, turn, project)

            @block.scalar
            def _(act):
                def turn(b):
                    act.wait_ge(turned, b.number + 1)
                    nc.scalar.activation(uT[b.slot][:, :], psT[b.slot][:, :], ACT.Copy).then_inc(evac, 1)
                pipeline(act, turn)

            @block.gpsimd
            def _(pool):
                whole = out[0:(STEPS - 1) * CHUNK, :].rearrange("(c p j) d -> c p (j d)", p=P, j=J)

                def store(b):
                    held(pool, ready, b.number + 1, g.passed)
                    if isinstance(b.number, int) and b.number == STEPS - 1:
                        pool.dma_start(out[(STEPS - 1) * CHUNK:N, :].rearrange("(p j) d -> p (j d)", j=J), x[b.slot][0:LASTP, :]).then_inc(stored[b.slot], 16)
                    else:
                        pool.dma_start(whole[b.number], x[b.slot][:, :]).then_inc(stored[b.slot], 16)

                def landed(b):
                    held(pool, stored[b.slot], 16 * b.nth, g.passed)
                    pool.sem_inc(free, 1)
                pipeline(pool, store, landed, oldest_first=True)


NAMES = ["x", "src", "dst", "edge_attr_32", "edge_type_8", "edge_weight1", "L0_gnn_b", "L1_gnn_weight",
         "L2_gnn_q1_w", "L2_gnn_q1_b", "L2_gnn_k1_w", "L2_gnn_k1_b", "L2_gnn_v1_w", "L2_gnn_v1_b", "L2_gnn_e1_w",
         "L2_gnn_s1_w", "L2_gnn_s1_b", "L2_gnn_q2_w", "L2_gnn_q2_b", "L2_gnn_k2_w", "L2_gnn_k2_b", "L2_gnn_v2_w",
         "L2_gnn_v2_b", "L2_gnn_e2_w", "L2_gnn_s2_w", "L2_gnn_s2_b", "L2_gnn_skip_w", "L2_gnn_skip_b",
         "L3_gnn_W1", "L3_gnn_b1", "L3_gnn_W2", "L3_gnn_b2"]


def kernel(**inputs):
    import numpy as _np
    import concourse.bacc as _bacc
    from concourse import mybir as _mybir
    from concourse.bass_utils import run_bass_kernel_spmd as _run

    nc = _bacc.Bacc("TRN2", target_bir_lowering=False, num_devices=1)
    arrays, given = {}, {}
    for name in NAMES + ["W0T"]:
        v = _np.asarray(inputs["L0_gnn_W"]).T if name == "W0T" else _np.asarray(inputs[name])
        v = _np.ascontiguousarray(v)
        arrays[f"in_{name}"] = v
        given[name] = nc.dram_tensor(f"in_{name}", v.shape, _mybir.dt.from_np(v.dtype), kind="ExternalInput").ap()
    out = nc.dram_tensor("out_x", (N, D), _mybir.dt.float32, kind="ExternalOutput").ap()
    build(nc, given, out)
    r = _run(nc, [arrays], core_ids=[0])
    return r.results[0]["out_x"]
```

```python
import numpy as np
import concourse.bass as bass
from concourse import mybir
from contextlib import ExitStack

fp32 = mybir.dt.float32
i32 = mybir.dt.int32
bf16 = mybir.dt.bfloat16
fp16 = mybir.dt.float16
ALU = mybir.AluOpType
ACT = mybir.ActivationFunctionType
AXX = mybir.AxisListType.X

P = 128
D = 64
DE = 32
MID = 32
RELS = 8
N = 100000
E = 50000
J = 16
CHUNK = P * J
STEPS = 49
NP = STEPS * CHUNK
LASTP = (N - (STEPS - 1) * CHUNK) // J
B = 8
T = STEPS * B
SPARE = 2 * B * P
SLOTS = 4
FULL = E // T
REST = E - FULL * T
COLS = STEPS * J
PADROW = NP + P - 1
HUGE = 3.0e38
EPS = 1e-5
assert (N - (STEPS - 1) * CHUNK) % J == 0 and FULL == P - 1 and NP >= N


class Batch:

    def __init__(self, number, slot, nth):
        self.number, self.slot, self.nth = number, slot, nth


def pipeline(eng, *stages, slots=2, oldest_first=False, order=None):
    if order is None:
        order = [(d, stage) for d, stage in enumerate(stages) if stage is not None]
        if oldest_first:
            order.reverse()
    deepest = max(d for d, _ in order)

    def peeled(c):
        for d, stage in order:
            if 0 <= c - d < STEPS:
                stage(Batch(c - d, (c - d) % slots, (c - d) // slots + 1))

    lead = -(-deepest // slots) * slots
    end = STEPS // slots * slots
    for c in range(lead):
        peeled(c)
    with eng.Fori(lead // slots, end // slots) as i:
        for k in range(slots):
            for d, stage in order:
                stage(Batch(i * slots + (k - d), (k - d) % slots, i + ((k - d) // slots + 1)))
    for c in range(end, STEPS + deepest):
        peeled(c)


def nothing(b):
    pass


class Link:

    def __init__(self, eng, sem):
        self.eng, self.sem, self.n = eng, sem, 0

    def __call__(self, ins):
        self.n += 1
        ins.then_inc(self.sem, 1)
        self.eng.wait_ge(self.sem, self.n)

    def restart(self):
        self.eng.sem_clear(self.sem)
        self.n = 0


DMA_SIGNALS = {"loaded", "weights", "attrs", "zeroed", "x_in", "stored", "got", "ea_in", "seam_got", "seam_put",
               ("de", "added"), ("dd", "cleared")}


class Room:

    def __init__(self, nc, g, name):
        self.g = g
        self.nc, self.name, self.stack, self.sems = nc, name, ExitStack(), []

    def __enter__(self):
        return self

    def __exit__(self, *e):
        if self.sems and e[0] is None:
            with self.nc.Block() as block:
                @block.sync
                def _(sp):
                    for sem in self.sems:
                        sp.sem_clear(sem)
        return self.stack.__exit__(*e)

    def sb(self, name, shape, dt=fp32):
        return self.stack.enter_context(self.nc.sbuf_tensor(f"{self.name}_{name}", shape, dt))

    def ps(self, name, shape, dt=fp32):
        return self.stack.enter_context(self.nc.psum_tensor(f"{self.name}_{name}", shape, dt))

    def sem(self, name):
        if (self.name, name) in DMA_SIGNALS or name.rstrip("0123456789") in DMA_SIGNALS:
            return self.g.keeper.enter_context(self.nc.semaphore(f"{self.name}_{name}"))
        self.sems.append(self.stack.enter_context(self.nc.semaphore(f"{self.name}_{name}")))
        return self.sems[-1]


def held(eng, sem, value, passed):
    eng.wait_ge(sem, value)
    eng.sem_inc(passed, 1)


def once_past(eng, sem, b, back):
    if not (isinstance(b.number, int) and b.number < back):
        eng.wait_ge(sem, b.number - (back - 1))


def spread(ap, width):
    return ap.unsqueeze(2).to_broadcast([ap.shape[0], ap.shape[1], width])


def each_group(row, groups):
    return row.unsqueeze(1).to_broadcast([row.shape[0], groups, row.shape[1]])


def grouped(ap, width):
    return ap.rearrange("p (g f) -> p g f", f=width)


def chunk_of(table, c):
    return table[0:NP, :].rearrange("(c p j) d -> c p (j d)", p=P, j=J)[c]


def build(nc, a, out):
    with ExitStack() as ctx:
        def keep(name, shape, dt=fp32):
            return ctx.enter_context(nc.sbuf_tensor(name, shape, dt))

        def table(name, rows, width):
            return nc.dram_tensor(name, (rows, width), fp32, kind="Internal").ap()

        g = Graph()
        g.keeper = ctx
        g.passed = ctx.enter_context(nc.semaphore("passed"))
        g.t0 = table("t0", NP, D)
        g.base0 = table("base0", NP, D)
        g.acc0 = table("acc0", NP + SPARE, D)
        g.x1 = table("x1", NP, D)
        g.x2 = table("x2", NP + SPARE, D)
        g.g1 = table("g1", NP + SPARE, D)
        g.g2 = table("g2", NP + SPARE, D)
        g.skip = table("skip", NP, D)
        g.x3 = table("x3", NP, D)
        g.t3 = table("t3", NP, MID)
        g.acc3 = table("acc3", NP + SPARE, MID)
        g.t4 = table("t4", NP, MID)
        g.acc4 = table("acc4", NP + SPARE, MID)
        g.attr = table("attr", P * T, DE)
        g.ident = keep("ident", [P, P])
        g.ones = keep("ones", [P, P])
        g.zeros = keep("zeros", [P, 1024])
        g.eps = keep("eps", [P, 1])
        g.dummy_row = keep("dummy_row", [P, 1])
        g.src_f = keep("src_f", [P, T])
        g.src_rows = keep("src_rows", [P, T], i32)
        g.dst_rows = keep("dst_rows", [P, T], i32)
        g.last_rows = keep("last_rows", [P, T], i32)
        g.dst_f = keep("dst_f", [P, T])
        g.goes_on = keep("goes_on", [P, T])
        g.etype_f = keep("etype_f", [P, T])
        g.norm = keep("norm", [P, T])
        g.dis = keep("dis", [P, COLS])
        g.dinv = keep("dinv", [P, COLS])
        g.first_first = keep("first_first", [P, P])
        g.first_last = keep("first_last", [P, P])
        g.last_first = keep("last_first", [P, P])
        g.last_last = keep("last_last", [P, P])
        g.seam_sum = keep("seam_sum", [P, P])
        g.one_dst = keep("one_dst", [P, 1])
        g.seam_to = keep("seam_to", [P, 1], i32)
        for name in PAIR_WEIGHTS:
            setw(g, name, keep("w_" + name, [P, P]))
        for name in ("e1", "e2", "gcn2"):
            setw(g, name, keep("w_" + name, [P, 4 * D]))
        setw(g, "gcn1", keep("w_gcn1", [P, 2 * MID]))
        setw(g, "rel", keep("w_rel", [P, RELS * D]))
        for name in BIASES:
            setw(g, name, keep("b_" + name, [P, D]))

        setup(nc, g, a)
        degrees(nc, g)
        diffusion_dense(nc, g, a)
        diffusion_edges(nc, g)
        diffusion_close(nc, g)
        relation_edges(nc, g)
        attention_edges(nc, g, "at1", g.x2, True, ("q1", "k1", "v1", "e1"), ("bq1", "bk1", "bv1"),
                        [("s1", "bs1", g.g1)], g.g1)
        attention_edges(nc, g, "at2", g.g1, False, ("q2", "k2", "v2", "e2"), ("bq2", "bk2", "bv2"),
                        [("s2", "bs2", g.g2), ("skip_a", "bskip", g.skip)], g.g2)
        skip_dense(nc, g)
        gcn_edges(nc, g, "gc1", g.t3, g.acc3)
        gcn_middle(nc, g)
        gcn_edges(nc, g, "gc2", g.t4, g.acc4)
        gcn_close(nc, g, out)


PAIR_WEIGHTS = {"w0": "W0T", "q1": "L2_gnn_q1_w", "k1": "L2_gnn_k1_w", "v1": "L2_gnn_v1_w", "s1": "L2_gnn_s1_w",
                "q2": "L2_gnn_q2_w", "k2": "L2_gnn_k2_w", "v2": "L2_gnn_v2_w", "s2": "L2_gnn_s2_w",
                "skip_a": "L2_gnn_skip_w", "skip_b": "L2_gnn_skip_w"}
BIASES = {"b0": "L0_gnn_b", "bq1": "L2_gnn_q1_b", "bk1": "L2_gnn_k1_b", "bv1": "L2_gnn_v1_b", "bs1": "L2_gnn_s1_b",
          "bq2": "L2_gnn_q2_b", "bk2": "L2_gnn_k2_b", "bv2": "L2_gnn_v2_b", "bs2": "L2_gnn_s2_b",
          "bskip": "L2_gnn_skip_b", "bg1": "L3_gnn_b1", "bg2": "L3_gnn_b2"}


class Graph:

    def __init__(self):
        self.w = {}


def setw(g, name, ap):
    g.w[name] = ap


def edge_load(eng, tile, flat, sem, shift=0):
    eng.dma_start(tile[0:FULL, :], flat[shift:shift + FULL * T].rearrange("(p t) -> p t", t=T)).then_inc(sem, 16)
    eng.dma_start(tile[FULL:P, 0:REST - shift], flat[FULL * T + shift:E].unsqueeze(0)).then_inc(sem, 16)


def setup(nc, g, a):
    w = g.w
    with Room(nc, g, "setup") as r:
        src_i, dst_i, next_i, type_i = (r.sb(n, [P, T], i32) for n in ("src_i", "dst_i", "next_i", "type_i"))
        next_f, ends, pad = r.sb("next_f", [P, T]), r.sb("ends", [P, T]), r.sb("pad", [P, T])
        diag = r.sb("diag", [P, 2, P])
        nowhere = r.sb("nowhere", [P, -(-T // (2 * B)) * 2 * B])
        before, after = r.sb("before", [P, P]), r.sb("after", [P, P])
        tmp = r.sb("tmp", [P, 4])
        ps_rows = r.ps("ps_rows", [P, 2 * P])
        cleared, loaded, weights, link_s, dve_diag, pe_rows, made, attrs = (r.sem(n) for n in (
            "cleared", "loaded", "weights", "link", "dve_diag", "pe_rows", "made", "attrs"))
        with nc.Block() as block:
            @block.vector
            def _(dve):
                link = Link(dve, link_s)
                for t in w:
                    nc.vector.memset(w[t][:, :], 0.0)
                for t, v in ((src_i, PADROW), (dst_i, PADROW), (next_i, PADROW), (type_i, 0)):
                    nc.vector.memset(t[:, :], v)
                nc.vector.memset(g.norm[:, :], 0.0)
                nc.vector.memset(g.eps[:, :], EPS)
                nc.vector.memset(g.ones[:, :], 1.0)
                nc.vector.memset(g.zeros[:, :], 0.0).then_inc(cleared, 1)
                dve.wait_ge(loaded, 5 * 32)
                link(nc.vector.tensor_copy(g.src_f[:, :], src_i[:, :]))
                link(nc.vector.tensor_copy(g.dst_f[:, :], dst_i[:, :]))
                link(nc.vector.tensor_copy(next_f[:, :], next_i[:, :]))
                link(nc.vector.tensor_copy(g.etype_f[:, :], type_i[:, :]))
                link(nc.vector.tensor_scalar(g.src_rows[:, :], g.src_f[:, :], float(N - 1), None, ALU.min))
                link(nc.vector.tensor_scalar(g.dst_rows[:, :], g.dst_f[:, :], float(N - 1), None, ALU.min))
                link(nc.vector.tensor_tensor(ends[:, :], g.dst_f[:, :], next_f[:, :], ALU.is_equal))
                link(nc.vector.memset(g.goes_on[:, 0:1], 0.0))
                link(nc.vector.tensor_copy(g.goes_on[:, 1:T], ends[:, 0:T - 1]))
                link(nc.vector.tensor_scalar(pad[:, :], g.dst_f[:, :], float(N), None, ALU.is_ge))
                link(nc.vector.tensor_tensor(ends[:, :], ends[:, :], pad[:, :], ALU.max))
                dve.wait_ge(made, 1)
                link(nc.vector.tensor_tensor(pad[:, :], nowhere[:, 0:T], g.dst_f[:, :], ALU.subtract))
                link(nc.vector.tensor_tensor(pad[:, :], pad[:, :], ends[:, :], ALU.mult))
                link(nc.vector.tensor_tensor(g.last_rows[:, :], pad[:, :], g.dst_f[:, :], ALU.add))
                dve.wait_ge(made, 4)
                link(nc.vector.tensor_scalar(diag[:, 0, :], g.ident[:, :], g.dst_f[:, 0:1], None, ALU.mult))
                nc.vector.tensor_scalar(diag[:, 1, :], g.ident[:, :], g.dst_f[:, T - 1:T], None, ALU.mult).then_inc(dve_diag, 1)
                dve.wait_ge(pe_rows, 1)
                firsts, lasts = ps_rows[:, 0:P], ps_rows[:, P:2 * P]
                first, last = g.dst_f[:, 0:1], g.dst_f[:, T - 1:T]
                link(nc.vector.tensor_scalar(g.first_first[:, :], firsts, first, None, ALU.is_equal))
                link(nc.vector.tensor_scalar(g.first_last[:, :], lasts, first, None, ALU.is_equal))
                link(nc.vector.tensor_scalar(g.last_first[:, :], firsts, last, None, ALU.is_equal))
                link(nc.vector.tensor_scalar(g.last_last[:, :], lasts, last, None, ALU.is_equal))
                nc.vector.tensor_tensor(g.one_dst[:, :], first, last, ALU.is_equal).then_inc(dve_diag, 1)
                link(nc.vector.tensor_tensor(diag[:, 0, :], g.first_last[:, :], before[:, :], ALU.mult))
                link(nc.vector.tensor_reduce(tmp[:, 2:3], diag[:, 0, :], AXX, ALU.add))
                link(nc.vector.tensor_tensor(diag[:, 0, :], g.first_first[:, :], after[:, :], ALU.mult))
                link(nc.vector.tensor_reduce(tmp[:, 3:4], diag[:, 0, :], AXX, ALU.add))
                link(nc.vector.tensor_scalar(tmp[:, 2:4], tmp[:, 2:4], 1.0, None, ALU.min))
                link(nc.vector.tensor_scalar(tmp[:, 3:4], tmp[:, 3:4], -1.0, 1.0, ALU.mult, ALU.add))
                link(nc.vector.tensor_tensor(tmp[:, 0:1], tmp[:, 2:3], tmp[:, 3:4], ALU.mult))
                link(nc.vector.tensor_tensor(tmp[:, 1:2], first, g.dummy_row[:, :], ALU.subtract))
                link(nc.vector.tensor_tensor(tmp[:, 1:2], tmp[:, 1:2], tmp[:, 0:1], ALU.mult))
                link(nc.vector.tensor_tensor(g.seam_to[:, :], tmp[:, 1:2], g.dummy_row[:, :], ALU.add))

            @block.tensor
            def _(pe):
                pe.wait_ge(dve_diag, 1)
                nc.tensor.matmul(ps_rows[:, 0:P], g.ones[:, :], diag[:, 0, :], start=True, stop=True)
                nc.tensor.matmul(ps_rows[:, P:2 * P], g.ones[:, :], diag[:, 1, :], start=True, stop=True).then_inc(pe_rows, 1)

            @block.gpsimd
            def _(pool):
                nc.gpsimd.iota(g.dummy_row[:, :], pattern=[[0, 1]], base=NP, channel_multiplier=1,
                               allow_small_or_imprecise_dtypes=True)
                nc.gpsimd.iota(nowhere[:, :], pattern=[[0, -(-T // (2 * B))], [P, 2 * B]], base=NP, channel_multiplier=1,
                               allow_small_or_imprecise_dtypes=True).then_inc(made, 1)
                pool.wait_ge(cleared, 1)
                nc.gpsimd.affine_select(out=g.ident[:, :], in_=g.zeros[:, 0:P], compare_op=ALU.not_equal, fill=1.0,
                                        base=0, pattern=[[-1, P]], channel_multiplier=1).then_inc(made, 1)
                for mask, sign in ((before, -1), (after, 1)):
                    nc.gpsimd.affine_select(out=mask[:, :], in_=g.ones[:, :], compare_op=ALU.is_gt, fill=0.0,
                                            base=0, pattern=[[sign, P]], channel_multiplier=-sign).then_inc(made, 1)
                pool.wait_ge(dve_diag, 2)
                nc.gpsimd.affine_select(out=g.seam_sum[:, :], in_=g.last_first[:, :], compare_op=ALU.is_gt, fill=0.0,
                                        base=0, pattern=[[1, P]], channel_multiplier=-1)

            @block.sync
            def _(sp):
                sp.wait_ge(cleared, 1)
                edge_load(sp, src_i, a["src"], loaded)
                edge_load(sp, dst_i, a["dst"], loaded)
                edge_load(sp, next_i, a["dst"], loaded, shift=1)
                edge_load(sp, type_i, a["edge_type_8"], loaded)
                edge_load(sp, g.norm, a["edge_weight1"].rearrange("e o -> (e o)"), loaded)
                sp.dma_start(g.attr[0:E, :].rearrange("(p k) d -> p (k d)", p=80),
                             a["edge_attr_32"].rearrange("(p k) d -> p (k d)", p=80)).then_inc(attrs, 16)
                sp.dma_start(g.attr[E:P * T, :].rearrange("(p k) d -> p (k d)", p=16),
                             g.zeros[0:16, 0:(P * T - E) * DE // 16]).then_inc(attrs, 16)
                for tab in (g.acc0, g.x2, g.g1, g.g2, g.acc3, g.acc4):
                    width = tab.shape[1]
                    sp.dma_start(tab[NP:NP + SPARE, :].rearrange("(p k) d -> p (k d)", p=P),
                                 g.zeros[:, 0:SPARE // P * width]).then_inc(attrs, 16)
                sp.wait_ge(attrs, 32 + 6 * 16)
                sp.wait_ge(loaded, 5 * 32)

            @block.scalar
            def _(act):
                act.wait_ge(cleared, 1)
                count = 0

                def load(dst, src):
                    act.dma_start(dst, src).then_inc(weights, 16)

                for name, given in PAIR_WEIGHTS.items():
                    rows = a[given]
                    rows = rows[D:2 * D, :] if name == "skip_b" else rows[0:D, :]
                    for k in range(2):
                        load(w[name][k * D:(k + 1) * D, k * D:(k + 1) * D], rows)
                        count += 1
                for name, given in (("e1", "L2_gnn_e1_w"), ("e2", "L2_gnn_e2_w"), ("gcn2", "L3_gnn_W2")):
                    for k in range(4):
                        load(w[name][k * DE:(k + 1) * DE, k * D:(k + 1) * D], a[given])
                        count += 1
                for k in range(2):
                    load(w["gcn1"][k * D:(k + 1) * D, k * MID:(k + 1) * MID], a["L3_gnn_W1"])
                    load(w["rel"][k * D:(k + 1) * D, :].rearrange("i (r o) -> i r o", r=RELS),
                         a["L1_gnn_weight"].rearrange("r i o -> i r o"))
                    count += 2
                for name, given in BIASES.items():
                    f = a[given].shape[0]
                    load(w[name][:, 0:f], a[given].unsqueeze(0).to_broadcast([P, f]))
                    count += 1
                act.wait_ge(weights, 16 * count)


def degrees(nc, g):
    with Room(nc, g, "deg") as r:
        as_int, part_i = r.sb("as_int", [P, T], i32), r.sb("part_i", [P, T], i32)
        low_f, chunk_f, part_f = ([r.sb(f"{n}{k}", [P, T]) for k in range(2)] for n in ("low", "chunk", "part"))
        col_f = [r.sb(f"col{k}", [P, T]) for k in range(2)]
        iota = r.sb("iota", [P, COLS], fp16)
        hot_part = r.sb("hot_part", [P, 2, 2, B, P], bf16)
        hot_col = r.sb("hot_col", [P, 2, 2, B, COLS], bf16)
        blank = r.sb("blank", [P, P], bf16)
        counts = [r.ps(f"counts{k}", [P, 1024]) for k in range(2)]
        link_s, ready, hot, used, counted, root, rooted = (r.sem(n) for n in ("link", "ready", "hot", "used", "counted", "root", "rooted"))
        HALVES = ((0, 512), (512, COLS))
        with nc.Block() as block:
            @block.gpsimd
            def _(pool):
                nc.gpsimd.iota(iota[:, :], pattern=[[1, COLS]], base=0, channel_multiplier=0,
                               allow_small_or_imprecise_dtypes=True).then_inc(ready, 1)

            @block.vector
            def _(dve):
                link = Link(dve, link_s)
                link(nc.vector.memset(blank[:, :], 0.0))
                for k, index in enumerate((g.src_f, g.dst_f)):
                    link(nc.vector.tensor_copy(as_int[:, :], index[:, :]))
                    link(nc.vector.tensor_scalar(part_i[:, :], as_int[:, :], 4, 127, ALU.logical_shift_right, ALU.bitwise_and))
                    link(nc.vector.tensor_copy(part_f[k][:, :], part_i[:, :]))
                    link(nc.vector.tensor_scalar(part_i[:, :], as_int[:, :], 15, None, ALU.bitwise_and))
                    link(nc.vector.tensor_copy(low_f[k][:, :], part_i[:, :]))
                    link(nc.vector.tensor_scalar(part_i[:, :], as_int[:, :], 11, None, ALU.logical_shift_right))
                    link(nc.vector.tensor_copy(chunk_f[k][:, :], part_i[:, :]))
                    link(nc.vector.scalar_tensor_tensor(col_f[k][:, :], chunk_f[k][:, :], float(J), low_f[k][:, :], ALU.mult, ALU.add))
                dve.wait_ge(ready, 1)
                nc.vector.sem_inc(used, 2)

                def one_hot(b):
                    dve.wait_ge(used, b.number + 1)
                    last = None
                    for k in range(2):
                        for t in range(B):
                            at = bass.ds(b.number * B + t, 1)
                            nc.vector.tensor_scalar(hot_part[:, b.slot, k, t, :], iota[:, 0:P], part_f[k][:, at], None, ALU.is_equal)
                            last = nc.vector.tensor_scalar(hot_col[:, b.slot, k, t, :], iota[:, :], col_f[k][:, at], None, ALU.is_equal)
                    last.then_inc(hot, 1)
                pipeline(dve, one_hot)
                dve.wait_ge(counted, 1)
                for k, to in enumerate((g.dis, g.dinv)):
                    link(nc.vector.tensor_scalar(to[:, :], counts[k][:, 0:COLS], 1.0, None, ALU.add))
                    link(nc.vector.reciprocal(to[:, :], to[:, :]))
                nc.vector.sem_inc(root, 1)

            @block.tensor
            def _(pe):
                pe.wait_ge(hot, 1)
                for k in range(2):
                    for lo, hi in HALVES:
                        nc.tensor.matmul(counts[k][:, lo:hi], blank[:, :], hot_col[:, 0, k, 0, lo:hi], start=True, stop=False)

                def count(b):
                    pe.wait_ge(hot, b.number + 1)
                    last = None
                    for k in range(2):
                        for t in range(B):
                            for lo, hi in HALVES:
                                last = nc.tensor.matmul(counts[k][:, lo:hi], hot_part[:, b.slot, k, t, :],
                                                        hot_col[:, b.slot, k, t, lo:hi], start=False, stop=False)
                    last.then_inc(used, 1)
                pipeline(pe, count)
                for k in range(2):
                    for lo, hi in HALVES:
                        last = nc.tensor.matmul(counts[k][:, lo:hi], blank[:, :], hot_col[:, 0, k, 0, lo:hi], start=False, stop=True)
                last.then_inc(counted, 1)

            @block.scalar
            def _(act):
                act.wait_ge(root, 1)
                nc.scalar.activation(g.dis[:, :], g.dis[:, :], ACT.Sqrt)
                nc.scalar.activation(g.dinv[:, :], g.dinv[:, :], ACT.Sqrt).then_inc(rooted, 1)
                act.wait_ge(rooted, 1)



def transpose_pairs(nc, to, src, ident, n):
    for k in range(n):
        last = nc.tensor.transpose(to[:, k * P:(k + 1) * P], src[:, k * P:(k + 1) * P], ident[:, :])
    return last


def times(nc, to, left, weight, n, start=True, stop=True):
    wide = weight.shape[1]
    for k in range(n):
        last = nc.tensor.matmul(to[:, k * wide:(k + 1) * wide], left[:, k * P:(k + 1) * P], weight[:, :],
                                start=start, stop=stop, skip_group_check=not (start and stop))
    return last


def mean_off(nc, link, x, centred, sums, groups):
    link(nc.vector.tensor_reduce(sums, grouped(x, D), AXX, ALU.add))
    link(nc.vector.tensor_scalar(sums, sums, -1.0 / D, None, ALU.mult))
    return nc.vector.tensor_tensor(grouped(centred, D), grouped(x, D), spread(sums, D), ALU.add)


def diffusion_dense(nc, g, a):
    W = J * D
    with Room(nc, g, "dd") as r:
        x, cen, lo, hi = ([r.sb(f"{n}{k}", [P, W]) for k in range(SLOTS)] for n in ("x", "cen", "t0", "base"))
        sq, hT, h0, rl = ([r.sb(f"{n}{k}", [P, W]) for k in range(2)] for n in ("sq", "hT", "h0", "rl"))
        sums, sd = r.sb("sums", [P, SLOTS, J]), r.sb("sd", [P, SLOTS, J])
        psT = [r.ps(f"psT{k}", [P, W]) for k in range(2)]
        psH = [r.ps(f"psH{k}", [P, W]) for k in range(2)]
        x_in = [r.sem(f"x_in{k}") for k in range(SLOTS)]
        stored = [r.sem(f"stored{k}") for k in range(SLOTS)]
        x_free, o_free, link_s, squared, centred, summed, rooted, normed, turned, evac, product, h_made, mixed, relued, scaled, ready, cleared = (r.sem(n) for n in (
            "x_free", "o_free", "link", "squared", "centred", "summed", "rooted", "normed", "turned", "evac", "product", "h_made", "mixed", "relued", "scaled", "ready", "cleared"))
        with nc.Block() as block:
            @block.sync
            def _(sp):
                sp.sem_inc(x_free, SLOTS)
                view = a["x"]

                def load(b):
                    sp.wait_ge(x_free, b.number + 1)
                    if isinstance(b.number, int) and b.number == STEPS - 1:
                        sp.dma_start(x[b.slot][LASTP:P, :], g.zeros[LASTP:P, :]).then_inc(cleared, 16)
                        sp.wait_ge(cleared, 16)
                        sp.dma_start(x[b.slot][0:LASTP, :], view[(STEPS - 1) * CHUNK:N, :].rearrange("(p j) d -> p (j d)", j=J)).then_inc(x_in[b.slot], 16)
                    else:
                        whole = view[0:(STEPS - 1) * CHUNK, :].rearrange("(c p j) d -> c p (j d)", p=P, j=J)
                        sp.dma_start(x[b.slot][:, :], whole[b.number]).then_inc(x_in[b.slot], 16)
                pipeline(sp, load, slots=SLOTS)

            @block.vector
            def _(dve):
                link = Link(dve, link_s)

                def centre(b):
                    s = b.slot
                    link.restart()
                    dve.wait_ge(x_in[s], 16 * b.nth)
                    mean_off(nc, link, x[s][:, :], cen[s][:, :], sums[:, s, :], J).then_inc(centred, 1)

                def variance(b):
                    s = b.slot
                    dve.wait_ge(squared, b.number + 1)
                    nc.vector.tensor_reduce(sd[:, s, :], grouped(sq[s % 2][:, :], D), AXX, ALU.add).then_inc(summed, 1)

                def scale(b):
                    s = b.slot
                    dve.wait_ge(rooted, b.number + 1)
                    link(nc.vector.reciprocal(sd[:, s, :], sd[:, s, :]))
                    nc.vector.tensor_tensor(grouped(cen[s][:, :], D), grouped(cen[s][:, :], D), spread(sd[:, s, :], D), ALU.mult).then_inc(normed, 1)

                def close(b):
                    s = b.slot
                    dve.wait_ge(product, b.number + 1)
                    dve.wait_ge(scaled, b.number + 1)
                    dve.wait_ge(o_free, b.number + 1)
                    nc.vector.tensor_tensor(grouped(h0[s % 2][:, :], D), grouped(psH[s % 2][:, :], D), each_group(g.w["b0"][:, :], J), ALU.add).then_inc(h_made, 1)
                    dve.wait_ge(h_made, b.number + 1)
                    nc.vector.scalar_tensor_tensor(hi[s][:, :], h0[s % 2][:, :], 0.95, x[s][:, :], ALU.mult, ALU.add).then_inc(mixed, 1)

                pipeline(dve, centre, variance, scale, close, slots=SLOTS)

            @block.scalar
            def _(act):
                def norm(b):
                    s = b.slot
                    act.wait_ge(centred, b.number + 1)
                    if not (isinstance(b.number, int) and b.number < 2):
                        act.wait_ge(summed, b.number - 1)
                    nc.scalar.activation(sq[s % 2][:, :], cen[s][:, :], ACT.Square).then_inc(squared, 1)

                def root(b):
                    s = b.slot
                    act.wait_ge(summed, b.number + 1)
                    nc.scalar.activation(sd[:, s, :], sd[:, s, :], ACT.Sqrt, bias=g.eps[:, :], scale=1.0 / D).then_inc(rooted, 1)

                def turn(b):
                    s = b.slot
                    act.wait_ge(turned, b.number + 1)
                    nc.scalar.activation(hT[s % 2][:, :], psT[s % 2][:, :], ACT.Relu).then_inc(evac, 1)

                def positive(b):
                    act.wait_ge(h_made, b.number + 1)
                    nc.scalar.activation(rl[b.slot % 2][:, :], h0[b.slot % 2][:, :], ACT.Relu, scale=1.5).then_inc(relued, 1)
                pipeline(act, norm, root, turn, positive, slots=SLOTS)

            @block.tensor
            def _(pe):
                def turn(b):
                    s = b.slot
                    pe.wait_ge(normed, b.number + 1)
                    transpose_pairs(nc, psT[s % 2], cen[s], g.ident, J // 2).then_inc(turned, 1)
                    pe.wait_ge(evac, b.number + 1)
                    pe.wait_ge(scaled, b.number + 1)
                    times(nc, psH[s % 2], hT[s % 2], g.w["w0"], J // 2).then_inc(product, 1)
                pipeline(pe, turn, slots=SLOTS)

            @block.gpsimd
            def _(pool):
                pool.sem_inc(o_free, SLOTS)
                pool.sem_inc(scaled, 2)

                def mix(b):
                    s = b.slot
                    pool.wait_ge(h_made, b.number + 1)
                    dis = g.dis[:, bass.ds(b.number * J, J)]
                    nc.gpsimd.tensor_tensor(grouped(lo[s][:, :], D), grouped(h0[s % 2][:, :], D), spread(dis, D), ALU.mult)
                    held(pool, mixed, b.number + 1, g.passed)
                    held(pool, relued, b.number + 1, g.passed)
                    nc.gpsimd.tensor_tensor(hi[s][:, :], hi[s][:, :], rl[s % 2][:, :], ALU.add).then_inc(ready, 1)
                    held(pool, ready, b.number + 1, g.passed)
                    pool.sem_inc(scaled, 1)
                    pool.sem_inc(x_free, 1)
                    pool.dma_start(chunk_of(g.t0, b.number), lo[s][:, :]).then_inc(stored[s], 16)
                    pool.dma_start(chunk_of(g.acc0, b.number), lo[s][:, :]).then_inc(stored[s], 16)
                    pool.dma_start(chunk_of(g.base0, b.number), hi[s][:, :]).then_inc(stored[s], 16)

                def landed(b):
                    held(pool, stored[b.slot], 48 * b.nth, g.passed)
                    pool.sem_inc(o_free, 1)
                pipeline(pool, mix, None, landed, slots=SLOTS, oldest_first=True)


def gather(nc, buf, table, rows, sem, groups=B):
    width = table.shape[1]
    for t in range(groups):
        nc.gpsimd.indirect_dma_start(buf[:, t * width:(t + 1) * width], None, table,
                                     bass.IndirectOffsetOnAxis(ap=rows[:, t:t + 1], axis=0)).then_inc(sem, 16)


def add_rows(nc, buf, table, rows, sem, groups=B):
    width = table.shape[1]
    for t in range(groups):
        nc.gpsimd.indirect_dma_start(table, bass.IndirectOffsetOnAxis(ap=rows[:, t:t + 1], axis=0),
                                     buf[:, t * width:(t + 1) * width], None, compute_op=ALU.add).then_inc(sem, 16)


def diffusion_edges(nc, g):
    W = B * D
    with Room(nc, g, "de") as r:
        rows = [r.sb(f"rows{k}", [P, W]) for k in range(2)]
        summed = [r.sb(f"summed{k}", [P, W]) for k in range(2)]
        take = [r.sb(f"take{k}", [P, B], i32) for k in range(2)]
        put = [r.sb(f"put{k}", [P, B], i32) for k in range(2)]
        diag = r.sb("diag", [P, B, P])
        same = [r.sb(f"same{k}", [P, B, P]) for k in range(2)]
        later = r.sb("later", [P, P])
        dup, toward = r.sb("dup", [P, B]), r.sb("toward", [P, B])
        ps_src = r.ps("ps_src", [P, B * P])
        ps_sum = [r.ps(f"ps_sum{k}", [P, W]) for k in range(2)]
        got = [r.sem(f"got{k}") for k in range(2)]
        free, link_s, staged, mask, dve_diag, src_rows, same_made, product, ready, added, zeroed = (r.sem(n) for n in (
            "free", "link", "staged", "mask", "dve_diag", "src_rows", "same_made", "product", "ready", "added", "zeroed"))
        with nc.Block() as block:
            @block.gpsimd
            def _(pool):
                nc.gpsimd.affine_select(out=later[:, :], in_=g.ones[:, :], compare_op=ALU.is_gt, fill=0.0,
                                        base=0, pattern=[[1, P]], channel_multiplier=-1).then_inc(mask, 1)
                pool.sem_inc(free, 2)

                def fetch(b):
                    s = b.slot
                    held(pool, free, b.number + 1, g.passed)
                    nc.gpsimd.tensor_copy(take[s][:, :], g.dst_rows[:, bass.ds(b.number * B, B)]).then_inc(staged, 1)
                    held(pool, staged, b.number + 1, g.passed)

                def add(b):
                    held(pool, ready, b.number + 1, g.passed)

                def both(f, d):
                    for t in range(B):
                        if f is not None:
                            s = f.slot
                            nc.gpsimd.indirect_dma_start(rows[s][:, t * D:(t + 1) * D], None, g.t0,
                                                         bass.IndirectOffsetOnAxis(ap=take[s][:, t:t + 1], axis=0)).then_inc(got[s], 16)
                        if d is not None:
                            s = d.slot
                            if not (isinstance(d.number, int) and d.number == 0 and t == 0):
                                held(pool, added, 16 * (d.number * B + t), g.passed)
                            nc.gpsimd.indirect_dma_start(g.acc0, bass.IndirectOffsetOnAxis(ap=put[s][:, t:t + 1], axis=0),
                                                         summed[s][:, t * D:(t + 1) * D], None, compute_op=ALU.add).then_inc(added, 16)

                for c in (0, 1):
                    fetch(Batch(c, c, 1))
                    both(Batch(c, c, 1), None)
                with pool.Fori(1, STEPS // 2) as i:
                    for k in range(2):
                        f, d = Batch(i * 2 + k, k, i + 1), Batch(i * 2 + k - 2, k, i)
                        add(d)
                        fetch(f)
                        both(f, d)
                last, d = Batch(STEPS - 1, 0, STEPS // 2 + 1), Batch(STEPS - 3, 0, STEPS // 2)
                add(d)
                fetch(last)
                both(last, d)
                for d in (Batch(STEPS - 2, 1, 0), Batch(STEPS - 1, 0, 0)):
                    add(d)
                    both(None, d)
                pool.wait_ge(added, 16 * T)

            @block.vector
            def _(dve):
                link = Link(dve, link_s)
                dve.wait_ge(mask, 1)

                def equal(b):
                    s = b.slot
                    src = g.src_f[:, bass.ds(b.number * B, B)]
                    nc.vector.tensor_tensor(diag[:, :, :], each_group(g.ident[:, :], B), spread(src, P), ALU.mult).then_inc(dve_diag, 1)
                    dve.wait_ge(src_rows, b.number + 1)
                    link(nc.vector.tensor_tensor(same[s][:, :, :], ps_src[:, :].rearrange("p (b q) -> p b q", q=P), spread(src, P), ALU.is_equal))
                    nc.vector.sem_inc(same_made, 1)
                    link(nc.vector.tensor_tensor(diag[:, :, :], same[s][:, :, :], each_group(later[:, :], B), ALU.mult))
                    link(nc.vector.tensor_reduce(dup[:, :], diag[:, :, :], AXX, ALU.max))
                    link(nc.vector.tensor_scalar(toward[:, :], src, -1.0, g.dummy_row[:, :], ALU.mult, ALU.add))
                    link(nc.vector.tensor_tensor(toward[:, :], toward[:, :], dup[:, :], ALU.mult))
                    if not (isinstance(b.number, int) and b.number < 2):
                        dve.wait_ge(added, 16 * B * (b.number - 1))
                    link(nc.vector.tensor_tensor(put[s][:, :], toward[:, :], src, ALU.add))
                    link.restart()

                def carry(b):
                    s = b.slot
                    dve.wait_ge(product, b.number + 1)
                    nc.vector.tensor_copy(summed[s][:, :], ps_sum[s][:, :]).then_inc(ready, 1)
                    dve.wait_ge(ready, b.number + 1)
                pipeline_from_two(dve, equal, carry)

            @block.tensor
            def _(pe):
                def turn(b):
                    pe.wait_ge(dve_diag, b.number + 1)
                    for h in range(2):
                        last = nc.tensor.matmul(ps_src[:, h * 512:(h + 1) * 512], g.ones[:, :],
                                                diag[:, :, :].rearrange("p b q -> p (b q)")[:, h * 512:(h + 1) * 512], start=True, stop=True)
                    last.then_inc(src_rows, 1)

                def merge(b):
                    s = b.slot
                    pe.wait_ge(same_made, b.number + 1)
                    pe.wait_ge(got[s], 16 * B * b.nth)
                    for t in range(B):
                        last = nc.tensor.matmul(ps_sum[s][:, t * D:(t + 1) * D], same[s][:, t, :],
                                                rows[s][:, t * D:(t + 1) * D], start=True, stop=True)
                    last.then_inc(product, 1)
                    pe.wait_ge(product, b.number + 1)
                    pe.sem_inc(free, 1)
                pipeline(pe, turn, merge)


def pipeline_from_two(eng, *stages):
    first, second = stages

    def at(c, k=None):
        return Batch(c, c % 2, c // 2 + 1)
    first(at(0))
    first(at(1))
    second(at(0))
    with eng.Fori(1, STEPS // 2) as i:
        first(Batch(i * 2, 0, i + 1))
        second(Batch(i * 2 - 1, 1, i))
        first(Batch(i * 2 + 1, 1, i + 1))
        second(Batch(i * 2, 0, i + 1))
    first(at(STEPS - 1))
    second(at(STEPS - 2))
    second(at(STEPS - 1))


def diffusion_close(nc, g):
    W = J * D
    with Room(nc, g, "dc") as r:
        base, acc = ([r.sb(f"{n}{k}", [P, W]) for k in range(SLOTS)] for n in ("base", "acc"))
        tiny = r.sb("tiny", [P, COLS])
        x_in, stored = ([r.sem(f"{n}{k}") for k in range(SLOTS)] for n in ("x_in", "stored"))
        free, link_s, ready = (r.sem(n) for n in ("free", "link", "ready"))
        with nc.Block() as block:
            @block.sync
            def _(sp):
                sp.sem_inc(free, SLOTS)

                def load(b):
                    sp.wait_ge(free, b.number + 1)
                    sp.dma_start(base[b.slot][:, :], chunk_of(g.base0, b.number)).then_inc(x_in[b.slot], 16)
                    sp.dma_start(acc[b.slot][:, :], chunk_of(g.acc0, b.number)).then_inc(x_in[b.slot], 16)
                pipeline(sp, load, slots=SLOTS)

            @block.vector
            def _(dve):
                link = Link(dve, link_s)
                link(nc.vector.tensor_scalar(tiny[:, :], g.dis[:, :], 0.05, None, ALU.mult))

                def close(b):
                    s = b.slot
                    link.restart()
                    dve.wait_ge(x_in[s], 32 * b.nth)
                    link(nc.vector.tensor_tensor(grouped(acc[s][:, :], D), grouped(acc[s][:, :], D), spread(tiny[:, bass.ds(b.number * J, J)], D), ALU.mult))
                    nc.vector.tensor_tensor(base[s][:, :], base[s][:, :], acc[s][:, :], ALU.add).then_inc(ready, 1)
                pipeline(dve, close, slots=SLOTS)

            @block.scalar
            def _(act):
                def store(b):
                    s = b.slot
                    act.wait_ge(ready, b.number + 1)
                    act.dma_start(chunk_of(g.x1, b.number), base[s][:, :]).then_inc(stored[s], 16)
                    act.dma_start(chunk_of(g.x2, b.number), base[s][:, :]).then_inc(stored[s], 16)

                def landed(b):
                    act.wait_ge(stored[b.slot], 32 * b.nth)
                    act.sem_inc(free, 1)
                pipeline(act, store, None, landed, slots=SLOTS, oldest_first=True)



def running_sums(nc, link, tot, slot, msg, g, b, width):
    for t in range(B):
        if t == B - 1:
            link.restart()
        before = tot[slot][:, (t - 1) * width:t * width] if t else tot[1 - slot][:, (B - 1) * width:B * width]
        ins = nc.vector.scalar_tensor_tensor(tot[slot][:, t * width:(t + 1) * width], before,
                                             g.goes_on[:, bass.ds(b.number * B + t, 1)],
                                             msg[:, t * width:(t + 1) * width], ALU.mult, ALU.add)
        if t < B - 1:
            link(ins)
    return ins


def seam(nc, g, r, agg, tot, width):
    carried = r.sb("seam_carried", [P, width])
    ps = r.ps("seam_ps", [P, width])
    product, summed, put = (r.sem("seam_" + n) for n in ("product", "summed", "put"))
    with nc.Block() as block:
        @block.tensor
        def _(pe):
            nc.tensor.matmul(ps[:, :], g.seam_sum[:, :], tot[:, (B - 1) * width:B * width], start=True, stop=True).then_inc(product, 1)

        @block.gpsimd
        def _(pool):
            pool.wait_ge(summed, 1)
            add_rows(nc, carried, agg, g.seam_to, put, groups=1)
            pool.wait_ge(put, 16)

        @block.vector
        def _(dve):
            dve.wait_ge(product, 1)
            nc.vector.tensor_copy(carried[:, :], ps[:, :]).then_inc(summed, 1)


def relation_edges(nc, g):
    W = B * D
    with Room(nc, g, "re") as r:
        rows, hT, tot, cen = ([r.sb(f"{n}{k}", [P, W]) for k in range(2)] for n in ("rows", "hT", "tot", "cen"))
        take, put = ([r.sb(f"{n}{k}", [P, B], i32) for k in range(2)] for n in ("take", "put"))
        sq, msg = (r.sb(n, [P, W]) for n in ("sq", "msg"))
        sums, sd = r.sb("sums", [P, B]), r.sb("sd", [P, B])
        rel = r.sb("rel", [P, RELS])
        coef = r.sb("coef", [P, B, RELS])
        picked = [r.sb(f"picked{k}", [P, RELS * D]) for k in range(2)]
        psT = r.ps("psT", [P, W])
        psR = [r.ps(f"psR{k}", [P, RELS * D]) for k in range(4)]
        got, stored = ([r.sem(f"{n}{k}") for k in range(2)] for n in ("got", "stored"))
        free, sum_free, link_s, relno, staged, staged_put, centred, squared, summed, rooted, normed, turned, evac, product, read, reduced, ready = (r.sem(n) for n in (
            "free", "sum_free", "link", "relno", "staged", "staged_put", "centred", "squared", "summed", "rooted", "normed", "turned", "evac", "product", "read", "reduced", "ready"))
        with nc.Block() as block:
            @block.gpsimd
            def _(pool):
                nc.gpsimd.iota(rel[:, :], pattern=[[1, RELS]], base=0, channel_multiplier=0,
                               allow_small_or_imprecise_dtypes=True).then_inc(relno, 1)
                pool.sem_inc(free, 2)
                pool.sem_inc(sum_free, 2)

                def fetch(b):
                    s = b.slot
                    held(pool, free, b.number + 1, g.passed)
                    nc.gpsimd.tensor_copy(take[s][:, :], g.src_rows[:, bass.ds(b.number * B, B)]).then_inc(staged, 1)
                    held(pool, staged, b.number + 1, g.passed)
                    gather(nc, rows[s], g.x1, take[s], got[s])

                def send(b):
                    s = b.slot
                    held(pool, ready, b.number + 1, g.passed)
                    nc.gpsimd.tensor_copy(put[s][:, :], g.last_rows[:, bass.ds(b.number * B, B)]).then_inc(staged_put, 1)
                    held(pool, staged_put, b.number + 1, g.passed)
                    add_rows(nc, tot[s], g.x2, put[s], stored[s])

                def landed(b):
                    held(pool, stored[b.slot], 16 * B * b.nth, g.passed)
                    pool.sem_inc(sum_free, 1)

                pipeline(pool, fetch, None, send, landed)

            @block.vector
            def _(dve):
                link = Link(dve, link_s)
                dve.wait_ge(relno, 1)
                link(nc.vector.memset(tot[1][:, :], 0.0))
                link.restart()

                def norm(b):
                    s = b.slot
                    dve.wait_ge(got[s], 16 * B * b.nth)
                    mean_off(nc, link, rows[s][:, :], cen[s][:, :], sums[:, :], B).then_inc(centred, 1)
                    dve.wait_ge(centred, b.number + 1)
                    nc.vector.sem_inc(free, 1)
                    dve.wait_ge(squared, b.number + 1)
                    nc.vector.tensor_reduce(sd[:, :], grouped(sq[:, :], D), AXX, ALU.add).then_inc(summed, 1)
                    dve.wait_ge(rooted, b.number + 1)
                    link(nc.vector.reciprocal(sd[:, :], sd[:, :]))
                    nc.vector.tensor_tensor(grouped(cen[s][:, :], D), grouped(cen[s][:, :], D), spread(sd[:, :], D), ALU.mult).then_inc(normed, 1)

                def pick(b):
                    s = b.slot
                    at = bass.ds(b.number * B, B)
                    link(nc.vector.tensor_tensor(coef[:, :, :], each_group(rel[:, :], B), spread(g.etype_f[:, at], RELS), ALU.is_equal))
                    link(nc.vector.tensor_tensor(coef[:, :, :], coef[:, :, :], spread(g.norm[:, at], RELS), ALU.mult))
                    def own(t):
                        dve.wait_ge(product, b.number * B + t + 1)
                        if t >= 2:
                            dve.wait_ge(reduced, b.number * B + (t - 1))
                        nc.vector.tensor_tensor(grouped(picked[t % 2][:, :], D), grouped(psR[t % 4][:, :], D),
                                                spread(coef[:, t, :], D), ALU.mult).then_inc(read, 1)
                    own(0)
                    for t in range(B):
                        if t + 1 < B:
                            own(t + 1)
                        dve.wait_ge(read, b.number * B + t + 1)
                        nc.vector.tensor_reduce(msg[:, t * D:(t + 1) * D], picked[t % 2][:, :].rearrange("p (r o) -> p o r", r=RELS), AXX, ALU.add).then_inc(reduced, 1)
                    dve.wait_ge(reduced, b.number * B + B)
                    dve.wait_ge(sum_free, b.number + 1)
                    running_sums(nc, link, tot, s, msg, g, b, D).then_inc(ready, 1)
                    dve.wait_ge(ready, b.number + 1)
                pipeline(dve, norm, pick)

            @block.scalar
            def _(act):
                def norm(b):
                    act.wait_ge(centred, b.number + 1)
                    nc.scalar.activation(sq[:, :], cen[b.slot][:, :], ACT.Square).then_inc(squared, 1)
                    act.wait_ge(summed, b.number + 1)
                    nc.scalar.activation(sd[:, :], sd[:, :], ACT.Sqrt, bias=g.eps[:, :], scale=1.0 / D).then_inc(rooted, 1)
                    act.wait_ge(turned, b.number + 1)
                    nc.scalar.activation(hT[b.slot][:, :], psT[:, :], ACT.Relu).then_inc(evac, 1)
                pipeline(act, norm)

            @block.tensor
            def _(pe):
                def turn(b):
                    pe.wait_ge(normed, b.number + 1)
                    transpose_pairs(nc, psT, cen[b.slot], g.ident, B // 2).then_inc(turned, 1)

                def relate(b):
                    s = b.slot
                    pe.wait_ge(evac, b.number + 1)
                    for t in range(B):
                        if not (isinstance(b.number, int) and b.number == 0 and t < 4):
                            pe.wait_ge(read, b.number * B + (t - 3))
                        h = (t % 2) * D
                        nc.tensor.matmul(psR[t % 4][:, :], hT[s][h:h + D, (t // 2) * P:(t // 2 + 1) * P],
                                         g.w["rel"][h:h + D, :], start=True, stop=True).then_inc(product, 1)
                turn(Batch(0, 0, 1))
                relate(Batch(0, 0, 1))
                with pe.Fori(0, STEPS // 2) as i:
                    for k in range(2):
                        turn(Batch(i * 2 + (k + 1), (k + 1) % 2, None))
                        relate(Batch(i * 2 + (k + 1), (k + 1) % 2, None))
        seam(nc, g, r, g.x2, tot[(STEPS - 1) % 2], D)


def attention_edges(nc, g, name, nodes, normalise, weights, biases, dense, acc):
    with Room(nc, g, name) as r:
        scores = r.sb("scores", [P, T])
        values = r.sb("values", [P, T * D])
        attention_scores(nc, g, name, nodes, normalise, weights, biases, dense, scores, values)
        segment_softmax(nc, g, name, scores)
        attention_sums(nc, g, name, acc, scores, values)


def attention_scores(nc, g, name, nodes, normalise, weights, biases, dense, scores, values):
    W = B * D
    C = J * D
    wq, wk, wv, we = (g.w[n] for n in weights)
    bq, bk, bv = (g.w[n] for n in biases)
    pieces = [(h, n) for n in range(len(dense)) for h in range(2)]
    M = len(pieces)
    with Room(nc, g, name + "s") as r:
        ends, xd = ([r.sb(f"{n}{k}", [P, C]) for k in range(2)] for n in ("ends", "xd"))
        ea = [r.sb(f"ea{k}", [P, B * DE]) for k in range(2)]
        outs = [[r.sb(f"out{n}{k}", [P, C]) for k in range(2)] for n in range(len(dense))]
        take_s, take_d = ([r.sb(f"{n}{k}", [P, B], i32) for k in range(2)] for n in ("take_s", "take_d"))
        hsT, hdT, eaT, xT = ([r.sb(f"{n}{k}", [P, w]) for k in range(2)] for n, w in (("hsT", W), ("hdT", W), ("eaT", B * DE), ("xT", C)))
        q, k_ = r.sb("q", [P, W]), r.sb("k", [P, W])
        if normalise:
            cen_e, cen_d = r.sb("cen_e", [P, C]), r.sb("cen_d", [P, C])
            sq = r.sb("sq", [P, C])
            sums, sd = r.sb("sums", [P, 2, J]), r.sb("sd", [P, 2, J])
        psS, psD, psE, psQ, psK, psV, psX, psY = (r.ps(n, [P, 512]) for n in ("psS", "psD", "psE", "psQ", "psK", "psV", "psX", "psY"))
        got, ea_in, stored = ([r.sem(f"{n}{k}") for k in range(2)] for n in ("got", "ea_in", "stored"))
        (free, o_free, staged, link_s, centred, squared, summed, rooted, normed, turned, evac, turned_h, evac_h, product, used,
         piece, piece_read) = (r.sem(n) for n in (
             "free", "o_free", "staged", "link", "centred", "squared", "summed", "rooted", "normed", "turned", "evac",
             "turned_h", "evac_h", "product", "used", "piece", "piece_read"))
        with nc.Block() as block:
            @block.gpsimd
            def _(pool):
                def fetch(b):
                    s = b.slot
                    held(pool, free, b.number + 1, g.passed)
                    nc.gpsimd.tensor_copy(take_s[s][:, :], g.src_rows[:, bass.ds(b.number * B, B)])
                    nc.gpsimd.tensor_copy(take_d[s][:, :], g.dst_rows[:, bass.ds(b.number * B, B)]).then_inc(staged, 1)
                    held(pool, staged, b.number + 1, g.passed)
                    gather(nc, ends[s][:, 0:W], nodes, take_s[s], got[s])
                    gather(nc, ends[s][:, W:C], nodes, take_d[s], got[s])
                pipeline(pool, fetch)

            @block.sync
            def _(sp):
                rows = g.attr.rearrange("(p c t) d -> c p (t d)", p=P, t=B)
                sp.sem_inc(o_free, 2)

                def load(b):
                    sp.wait_ge(free, b.number + 1)
                    sp.dma_start(ea[b.slot][:, :], rows[b.number]).then_inc(ea_in[b.slot], 16)
                    sp.dma_start(xd[b.slot][:, :], chunk_of(nodes, b.number)).then_inc(ea_in[b.slot], 16)

                def store(b):
                    sp.wait_ge(piece_read, b.number * M + M)
                    for n, (_, _, to) in enumerate(dense):
                        sp.dma_start(chunk_of(to, b.number), outs[n][b.slot][:, :]).then_inc(stored[b.slot], 16)

                def landed(b):
                    sp.wait_ge(stored[b.slot], 16 * len(dense) * b.nth)
                    sp.sem_inc(o_free, 1)
                pipeline(sp, load, None, store, landed, oldest_first=True)

            def inputs_ready(eng, b):
                eng.wait_ge(got[b.slot], 16 * 2 * B * b.nth)
                eng.wait_ge(ea_in[b.slot], 32 * b.nth)

            @block.tensor
            def _(pe):
                pe.sem_inc(free, 2)

                def turn(b):
                    s = b.slot
                    if normalise:
                        pe.wait_ge(normed, b.number + 1)
                        pe.wait_ge(ea_in[s], 32 * b.nth)
                        e, x = cen_e, cen_d
                    else:
                        inputs_ready(pe, b)
                        e, x = ends[s], xd[s]
                    once_past(pe, evac_h, b, 1)
                    transpose_pairs(nc, psS, e[:, 0:W], g.ident, B // 2)
                    transpose_pairs(nc, psD, e[:, W:C], g.ident, B // 2)
                    transpose_pairs(nc, psE, ea[s], g.ident, B // 4)
                    transpose_pairs(nc, psX, x[:, 0:W], g.ident, B // 2).then_inc(turned, 1)
                    pe.wait_ge(evac, b.number + 1)
                    transpose_pairs(nc, psX, x[:, W:C], g.ident, B // 2).then_inc(turned_h, 1)
                    pe.wait_ge(turned_h, b.number + 1)
                    pe.sem_inc(free, 1)

                def project(b):
                    s = b.slot
                    pe.wait_ge(evac, b.number + 1)
                    once_past(pe, used, b, 1)
                    times(nc, psQ, hdT[s], wq, B // 2)
                    for to, w in ((psK, wk), (psV, wv)):
                        for h in range(2):
                            nc.tensor.matmul(to[:, h * 256:(h + 1) * 256], eaT[s][:, h * P:(h + 1) * P], we[:, :], start=True, stop=False,
                                             skip_group_check=True)
                            for k in range(2):
                                j = 2 * h + k
                                last = nc.tensor.matmul(to[:, j * P:(j + 1) * P], hsT[s][:, j * P:(j + 1) * P], w[:, :], start=False, stop=(k == 1),
                                                        skip_group_check=True)
                    last.then_inc(product, 1)

                def own(b):
                    s = b.slot
                    pe.wait_ge(evac_h, b.number + 1)
                    for m, (h, n) in enumerate(pieces):
                        if not (isinstance(b.number, int) and b.number == 0 and m == 0):
                            pe.wait_ge(piece_read, b.number * M + m)
                        times(nc, psY, xT[s][:, h * W:(h + 1) * W], g.w[dense[n][0]], B // 2).then_inc(piece, 1)
                pipeline(pe, order=[(1, project), (0, turn), (1, own)])

            @block.scalar
            def _(act):
                def norm(b):
                    for e, cen in ((0, cen_e), (1, cen_d)):
                        act.wait_ge(centred, b.number * 2 + (e + 1))
                        if not (isinstance(b.number, int) and b.number == 0 and e == 0):
                            act.wait_ge(summed, b.number * 2 + e)
                        nc.scalar.activation(sq[:, :], cen[:, :], ACT.Square).then_inc(squared, 1)
                    act.wait_ge(summed, b.number * 2 + 2)
                    nc.scalar.activation(sd[:, :, :], sd[:, :, :], ACT.Sqrt, bias=g.eps[:, :], scale=1.0 / D).then_inc(rooted, 1)

                def turn(b):
                    s = b.slot
                    act.wait_ge(turned, b.number + 1)
                    once_past(act, product, b, 2)
                    nc.scalar.activation(hsT[s][:, :], psS[:, :], ACT.Relu)
                    nc.scalar.activation(hdT[s][:, :], psD[:, :], ACT.Relu)
                    nc.scalar.activation(eaT[s][:, :], psE[:, 0:B * DE], ACT.Copy)
                    if not (isinstance(b.number, int) and b.number < 2):
                        act.wait_ge(piece, (b.number - 1) * M)
                    nc.scalar.activation(xT[s][:, 0:W], psX[:, :], ACT.Relu).then_inc(evac, 1)
                    act.wait_ge(turned_h, b.number + 1)
                    nc.scalar.activation(xT[s][:, W:C], psX[:, :], ACT.Relu).then_inc(evac_h, 1)
                if normalise:
                    pipeline(act, order=[(0, norm), (0, turn), (2, nothing)])
                else:
                    pipeline(act, order=[(0, turn), (2, nothing)])

            @block.vector
            def _(dve):
                link = Link(dve, link_s)

                def norm(b):
                    s = b.slot
                    inputs_ready(dve, b)
                    once_past(dve, turned_h, b, 1)
                    for e, (x, cen) in enumerate(((ends[s], cen_e), (xd[s], cen_d))):
                        mean_off(nc, link, x[:, :], cen[:, :], sums[:, e, :], J).then_inc(centred, 1)
                    for e in range(2):
                        dve.wait_ge(squared, b.number * 2 + (e + 1))
                        nc.vector.tensor_reduce(sd[:, e, :], grouped(sq[:, :], D), AXX, ALU.add).then_inc(summed, 1)
                    dve.wait_ge(rooted, b.number + 1)
                    link(nc.vector.reciprocal(sd[:, :, :], sd[:, :, :]))
                    for e, cen in enumerate((cen_e, cen_d)):
                        last = nc.vector.tensor_tensor(grouped(cen[:, :], D), grouped(cen[:, :], D), spread(sd[:, e, :], D), ALU.mult)
                    last.then_inc(normed, 1)

                def score(b):
                    s = b.slot
                    dve.wait_ge(product, b.number + 1)
                    nc.vector.tensor_tensor(grouped(q[:, :], D), grouped(psQ[:, :], D), each_group(bq[:, :], B), ALU.add)
                    nc.vector.tensor_tensor(grouped(values[:, bass.ds(b.number * W, W)], D), grouped(psV[:, :], D), each_group(bv[:, :], B), ALU.add)
                    nc.vector.tensor_tensor(grouped(k_[:, :], D), grouped(psK[:, :], D), each_group(bk[:, :], B), ALU.add).then_inc(used, 1)
                    dve.wait_ge(used, b.number + 1)
                    link(nc.vector.tensor_tensor(q[:, :], q[:, :], k_[:, :], ALU.mult))
                    link(nc.vector.tensor_reduce(scores[:, bass.ds(b.number * B, B)], grouped(q[:, :], D), AXX, ALU.add))
                    link.restart()
                    dve.wait_ge(o_free, b.number + 1)
                    for m, (h, n) in enumerate(pieces):
                        dve.wait_ge(piece, b.number * M + (m + 1))
                        nc.vector.tensor_tensor(grouped(outs[n][s][:, h * W:(h + 1) * W], D), grouped(psY[:, :], D),
                                                each_group(g.w[dense[n][1]][:, :], B), ALU.add).then_inc(piece_read, 1)
                if normalise:
                    pipeline(dve, norm, score)
                else:
                    pipeline(dve, None, score)


def segment_softmax(nc, g, name, scores):
    with Room(nc, g, name + "m") as r:
        fence, fence_back, keep_back, last = (r.sb(n, [P, T]) for n in ("fence", "fence_back", "keep_back", "last"))
        fwd, full, at_first, at_last, ends = (r.sb(n, [P, T]) for n in ("fwd", "full", "at_first", "at_last", "ends"))
        diag = r.sb("diag", [P, 2, P])
        near_first, near_last = r.sb("near_first", [P, 2, P]), r.sb("near_last", [P, 2, P])
        masks = r.sb("masks", [P, 2, 2, P])
        both = r.sb("both", [P, 2])
        tail = r.sb("tail", [P, 1])
        two = r.sb("two", [P, 1])
        ps = r.ps("ps", [P, 2 * P])
        link_s, spread_s, rows_s, shifted, exped = (r.sem(n) for n in ("link", "diag", "rows", "shifted", "exped"))
        rev = slice(None, None, -1)
        with nc.Block() as block:
            @block.tensor
            def _(pe):
                for n in range(2):
                    pe.wait_ge(spread_s, n + 1)
                    nc.tensor.matmul(ps[:, :], g.ones[:, :], diag[:, :, :].rearrange("p a q -> p (a q)"), start=True, stop=True).then_inc(rows_s, 1)

            @block.scalar
            def _(act):
                act.wait_ge(shifted, 1)
                nc.scalar.activation(scores[:, :], scores[:, :], ACT.Exp, scale=0.125).then_inc(exped, 1)

            @block.vector
            def _(dve):
                link = Link(dve, link_s)
                v = nc.vector
                link(v.tensor_scalar(fence[:, :], g.goes_on[:, :], HUGE, -HUGE, ALU.mult, ALU.add))
                link(v.memset(keep_back[:, T - 1:T], 0.0))
                link(v.tensor_copy(keep_back[:, 0:T - 1], g.goes_on[:, 1:T]))
                link(v.tensor_scalar(fence_back[:, :], keep_back[:, :], HUGE, -HUGE, ALU.mult, ALU.add))
                link(v.tensor_scalar(last[:, :], keep_back[:, :], -1.0, 1.0, ALU.mult, ALU.add))
                link(v.tensor_scalar(at_first[:, :], g.dst_f[:, :], g.dst_f[:, 0:1], None, ALU.is_equal))
                link(v.tensor_scalar(at_last[:, :], g.dst_f[:, :], g.dst_f[:, T - 1:T], None, ALU.is_equal))
                link(v.tensor_tensor(tail[:, :], g.dst_f[:, 0:1], g.dst_f[:, T - 1:T], ALU.not_equal))
                for k, m in enumerate((g.first_first, g.first_last, g.last_first, g.last_last)):
                    link(v.tensor_copy(masks[:, k // 2, k % 2, :], m[:, :]))

                def ends_of(a, z, n):
                    link(v.tensor_scalar(diag[:, 0, :], g.ident[:, :], a, None, ALU.mult))
                    v.tensor_scalar(diag[:, 1, :], g.ident[:, :], z, None, ALU.mult).then_inc(spread_s, 1)
                    dve.wait_ge(rows_s, n)

                rows = ps[:, :].rearrange("p (a q) -> p a q", q=P)
                link(v.tensor_tensor_scan(fwd[:, :], fence[:, :], scores[:, :], 0.0, ALU.add, ALU.max))
                link(v.tensor_tensor_scan(full[:, rev], fence_back[:, rev], fwd[:, rev], 0.0, ALU.add, ALU.max))
                ends_of(full[:, 0:1], fwd[:, T - 1:T], 1)
                for k, near in enumerate((near_first, near_last)):
                    link(v.tensor_scalar(near[:, :, :], masks[:, k, :, :], HUGE, -HUGE, ALU.mult, ALU.add))
                    link(v.tensor_tensor(near[:, :, :], near[:, :, :], rows, ALU.add))
                    link(v.tensor_reduce(both[:, k:k + 1], near[:, :, :].rearrange("p a q -> p (a q)"), AXX, ALU.max))
                for k, at in enumerate((at_first, at_last)):
                    link(v.tensor_scalar(ends[:, :], at[:, :], HUGE, -HUGE, ALU.mult, ALU.add))
                    link(v.scalar_tensor_tensor(full[:, :], ends[:, :], both[:, k:k + 1], full[:, :], ALU.add, ALU.max))
                v.tensor_tensor(scores[:, :], scores[:, :], full[:, :], ALU.subtract).then_inc(shifted, 1)
                dve.wait_ge(exped, 1)
                link(v.tensor_tensor_scan(fwd[:, :], g.goes_on[:, :], scores[:, :], 0.0, ALU.mult, ALU.add))
                link(v.tensor_tensor(last[:, :], last[:, :], fwd[:, :], ALU.mult))
                link(v.tensor_tensor_scan(full[:, rev], keep_back[:, rev], last[:, rev], 0.0, ALU.mult, ALU.add))
                link(v.tensor_tensor(two[:, :], fwd[:, T - 1:T], tail[:, :], ALU.mult))
                ends_of(full[:, 0:1], two[:, :], 2)
                for k, near in enumerate((near_first, near_last)):
                    link(v.tensor_tensor(near[:, :, :], masks[:, k, :, :], rows, ALU.mult))
                    link(v.tensor_reduce(both[:, k:k + 1], near[:, :, :].rearrange("p a q -> p (a q)"), AXX, ALU.add))
                for k, at in enumerate((at_first, at_last)):
                    link(v.scalar_tensor_tensor(full[:, :], at[:, :], both[:, k:k + 1], full[:, :], ALU.mult, ALU.max))
                link(v.reciprocal(full[:, :], full[:, :]))
                link(v.tensor_tensor(scores[:, :], scores[:, :], full[:, :], ALU.mult))


def attention_sums(nc, g, name, agg, alpha, values):
    W = B * D
    with Room(nc, g, name + "w") as r:
        tot = [r.sb(f"tot{k}", [P, W]) for k in range(2)]
        put = [r.sb(f"put{k}", [P, B], i32) for k in range(2)]
        msg = r.sb("msg", [P, W])
        stored = [r.sem(f"stored{k}") for k in range(2)]
        sum_free, link_s, staged, ready = (r.sem(n) for n in ("sum_free", "link", "staged", "ready"))
        with nc.Block() as block:
            @block.vector
            def _(dve):
                link = Link(dve, link_s)
                link(nc.vector.memset(tot[1][:, :], 0.0))
                link.restart()

                def add(b):
                    s = b.slot
                    dve.wait_ge(sum_free, b.number + 1)
                    link(nc.vector.tensor_tensor(grouped(msg[:, :], D), grouped(values[:, bass.ds(b.number * W, W)], D),
                                                 spread(alpha[:, bass.ds(b.number * B, B)], D), ALU.mult))
                    running_sums(nc, link, tot, s, msg, g, b, D).then_inc(ready, 1)
                    dve.wait_ge(ready, b.number + 1)
                pipeline(dve, add)

            @block.gpsimd
            def _(pool):
                pool.sem_inc(sum_free, 2)
                scatter_pipeline(nc, pool, g, tot, put, agg, ready, staged, stored, sum_free)
        seam(nc, g, r, agg, tot[(STEPS - 1) % 2], D)


def scatter_pipeline(nc, pool, g, tot, put, agg, ready, staged, stored, sum_free):
    def send(b):
        s = b.slot
        held(pool, ready, b.number + 1, g.passed)
        nc.gpsimd.tensor_copy(put[s][:, :], g.last_rows[:, bass.ds(b.number * B, B)]).then_inc(staged, 1)
        held(pool, staged, b.number + 1, g.passed)
        add_rows(nc, tot[s], agg, put[s], stored[s])

    def landed(b):
        held(pool, stored[b.slot], 16 * B * b.nth, g.passed)
        pool.sem_inc(sum_free, 1)
    pipeline(pool, send, landed)


def skip_dense(nc, g):
    W = J * D
    with Room(nc, g, "sk") as r:
        x, g2, sk = ([r.sb(f"{n}{k}", [P, W]) for k in range(SLOTS)] for n in ("x", "g2", "sk"))
        g2T, cen, hT, sq = ([r.sb(f"{n}{k}", [P, W]) for k in range(2)] for n in ("g2T", "cen", "hT", "sq"))
        o = [r.sb(f"o{k}", [P, J * MID]) for k in range(SLOTS)]
        sums, sd = r.sb("sums", [P, SLOTS, J]), r.sb("sd", [P, SLOTS, J])
        psA, psB, psT = (r.ps(n, [P, W]) for n in ("psA", "psB", "psT"))
        psO = [r.ps(f"psO{k}", [P, J * MID]) for k in range(2)]
        x_in, stored = ([r.sem(f"{n}{k}") for k in range(SLOTS)] for n in ("x_in", "stored"))
        names = ("free", "link", "turned2", "evac2", "made2", "mixed", "added", "centred", "squared",
                 "summed", "rooted", "normed", "turned3", "evac3", "made3", "ready")
        (free, link_s, turned2, evac2, made2, mixed, added, centred, squared,
         summed, rooted, normed, turned3, evac3, made3, ready) = (r.sem(n) for n in names)
        with nc.Block() as block:
            @block.sync
            def _(sp):
                sp.sem_inc(free, SLOTS)

                def load(b):
                    sp.wait_ge(free, b.number + 1)
                    sp.dma_start(g2[b.slot][:, :], chunk_of(g.g2, b.number)).then_inc(x_in[b.slot], 16)
                    sp.dma_start(sk[b.slot][:, :], chunk_of(g.skip, b.number)).then_inc(x_in[b.slot], 16)
                    sp.dma_start(x[b.slot][:, :], chunk_of(g.x2, b.number)).then_inc(x_in[b.slot], 16)
                pipeline(sp, load, slots=SLOTS)

            @block.tensor
            def _(pe):
                def skip(b):
                    s = b.slot
                    pe.wait_ge(x_in[s], 48 * b.nth)
                    once_past(pe, evac2, b, 1)
                    transpose_pairs(nc, psA, g2[s], g.ident, J // 2).then_inc(turned2, 1)
                    pe.wait_ge(evac2, b.number + 1)
                    once_past(pe, mixed, b, 1)
                    times(nc, psB, g2T[s % 2], g.w["skip_b"], J // 2).then_inc(made2, 1)

                def narrow(b):
                    s = b.slot
                    pe.wait_ge(normed, b.number + 1)
                    once_past(pe, evac3, b, 1)
                    transpose_pairs(nc, psT, cen[s % 2], g.ident, J // 2).then_inc(turned3, 1)

                def project(b):
                    s = b.slot
                    pe.wait_ge(evac3, b.number + 1)
                    once_past(pe, ready, b, 2)
                    times(nc, psO[s % 2], hT[s % 2], g.w["gcn1"], J // 2).then_inc(made3, 1)
                pipeline(pe, order=[(3, project), (2, narrow), (0, skip)], slots=SLOTS)

            @block.scalar
            def _(act):
                def out2(b):
                    s = b.slot
                    act.wait_ge(turned2, b.number + 1)
                    nc.scalar.activation(g2T[s % 2][:, :], psA[:, :], ACT.Relu).then_inc(evac2, 1)

                def square(b):
                    s = b.slot
                    act.wait_ge(centred, b.number + 1)
                    once_past(act, summed, b, 2)
                    nc.scalar.activation(sq[s % 2][:, :], cen[s % 2][:, :], ACT.Square).then_inc(squared, 1)

                def root(b):
                    s = b.slot
                    act.wait_ge(summed, b.number + 1)
                    nc.scalar.activation(sd[:, s, :], sd[:, s, :], ACT.Sqrt, bias=g.eps[:, :], scale=1.0 / D).then_inc(rooted, 1)

                def out3(b):
                    s = b.slot
                    act.wait_ge(turned3, b.number + 1)
                    once_past(act, made3, b, 2)
                    nc.scalar.activation(hT[s % 2][:, :], psT[:, :], ACT.Relu).then_inc(evac3, 1)
                pipeline(act, order=[(2, root), (2, out3), (0, out2), (1, square)], slots=SLOTS)

            @block.vector
            def _(dve):
                link = Link(dve, link_s)

                def add(b):
                    s = b.slot
                    link.restart()
                    dve.wait_ge(made2, b.number + 1)
                    nc.vector.tensor_tensor(sk[s][:, :], sk[s][:, :], psB[:, :], ALU.add).then_inc(mixed, 1)
                    dve.wait_ge(mixed, b.number + 1)
                    nc.vector.scalar_tensor_tensor(x[s][:, :], sk[s][:, :], 0.0, x[s][:, :], ALU.max, ALU.add).then_inc(added, 1)
                    dve.wait_ge(added, b.number + 1)
                    once_past(dve, turned3, b, 2)
                    mean_off(nc, link, x[s][:, :], cen[s % 2][:, :], sums[:, s, :], J).then_inc(centred, 1)

                def variance(b):
                    s = b.slot
                    dve.wait_ge(squared, b.number + 1)
                    nc.vector.tensor_reduce(sd[:, s, :], grouped(sq[s % 2][:, :], D), AXX, ALU.add).then_inc(summed, 1)

                def scale(b):
                    s = b.slot
                    dve.wait_ge(rooted, b.number + 1)
                    link(nc.vector.reciprocal(sd[:, s, :], sd[:, s, :]))
                    nc.vector.tensor_tensor(grouped(cen[s % 2][:, :], D), grouped(cen[s % 2][:, :], D), spread(sd[:, s, :], D), ALU.mult).then_inc(normed, 1)

                def close(b):
                    s = b.slot
                    dve.wait_ge(made3, b.number + 1)
                    nc.vector.tensor_tensor(grouped(o[s][:, :], MID), grouped(psO[s % 2][:, :], MID),
                                            spread(g.dinv[:, bass.ds(b.number * J, J)], MID), ALU.mult).then_inc(ready, 1)
                pipeline(dve, order=[(2, scale), (1, add), (3, close), (1, variance)], slots=SLOTS)

            @block.gpsimd
            def _(pool):
                def store(b):
                    s = b.slot
                    held(pool, ready, b.number + 1, g.passed)
                    pool.dma_start(chunk_of(g.x3, b.number), x[s][:, :]).then_inc(stored[s], 16)
                    pool.dma_start(chunk_of(g.t3, b.number), o[s][:, :]).then_inc(stored[s], 16)
                    pool.dma_start(chunk_of(g.acc3, b.number), o[s][:, :]).then_inc(stored[s], 16)

                def landed(b):
                    held(pool, stored[b.slot], 48 * b.nth, g.passed)
                    pool.sem_inc(free, 1)
                pipeline(pool, store, landed, slots=SLOTS, oldest_first=True)


def gcn_edges(nc, g, name, nodes, agg):
    W = B * MID
    with Room(nc, g, name) as r:
        rows, tot = ([r.sb(f"{n}{k}", [P, W]) for k in range(2)] for n in ("rows", "tot"))
        take, put = ([r.sb(f"{n}{k}", [P, B], i32) for k in range(2)] for n in ("take", "put"))
        got, stored = ([r.sem(f"{n}{k}") for k in range(2)] for n in ("got", "stored"))
        free, sum_free, link_s, staged, staged_put, ready = (r.sem(n) for n in (
            "free", "sum_free", "link", "staged", "staged_put", "ready"))
        with nc.Block() as block:
            @block.gpsimd
            def _(pool):
                pool.sem_inc(free, 2)
                pool.sem_inc(sum_free, 2)

                def fetch(b):
                    s = b.slot
                    held(pool, free, b.number + 1, g.passed)
                    nc.gpsimd.tensor_copy(take[s][:, :], g.src_rows[:, bass.ds(b.number * B, B)]).then_inc(staged, 1)
                    held(pool, staged, b.number + 1, g.passed)
                    gather(nc, rows[s], nodes, take[s], got[s])

                def send(b):
                    s = b.slot
                    held(pool, ready, b.number + 1, g.passed)
                    nc.gpsimd.tensor_copy(put[s][:, :], g.last_rows[:, bass.ds(b.number * B, B)]).then_inc(staged_put, 1)
                    held(pool, staged_put, b.number + 1, g.passed)
                    add_rows(nc, tot[s], agg, put[s], stored[s])

                def landed(b):
                    held(pool, stored[b.slot], 16 * B * b.nth, g.passed)
                    pool.sem_inc(sum_free, 1)
                pipeline(pool, fetch, send, landed)

            @block.vector
            def _(dve):
                link = Link(dve, link_s)
                link(nc.vector.memset(tot[1][:, :], 0.0))
                link.restart()

                def add(b):
                    s = b.slot
                    dve.wait_ge(got[s], 16 * B * b.nth)
                    dve.wait_ge(sum_free, b.number + 1)
                    running_sums(nc, link, tot, s, rows[s], g, b, MID).then_inc(ready, 1)
                    dve.wait_ge(ready, b.number + 1)
                    nc.vector.sem_inc(free, 1)
                pipeline(dve, add)
        seam(nc, g, r, agg, tot[(STEPS - 1) % 2], MID)


def gcn_middle(nc, g):
    W = J * MID
    with Room(nc, g, "gm") as r:
        t3, o = ([r.sb(f"{n}{k}", [P, W]) for k in range(SLOTS)] for n in ("t3", "o"))
        x_in, stored = ([r.sem(f"{n}{k}") for k in range(SLOTS)] for n in ("x_in", "stored"))
        free, link_s, ready = (r.sem(n) for n in ("free", "link", "ready"))
        with nc.Block() as block:
            @block.sync
            def _(sp):
                sp.sem_inc(free, SLOTS)

                def load(b):
                    sp.wait_ge(free, b.number + 1)
                    sp.dma_start(t3[b.slot][:, :], chunk_of(g.acc3, b.number)).then_inc(x_in[b.slot], 16)
                pipeline(sp, load, slots=SLOTS)

            @block.vector
            def _(dve):
                link = Link(dve, link_s)

                def close(b):
                    s = b.slot
                    dinv = spread(g.dinv[:, bass.ds(b.number * J, J)], MID)
                    link.restart()
                    dve.wait_ge(x_in[s], 16 * b.nth)
                    link(nc.vector.tensor_tensor(grouped(t3[s][:, :], MID), grouped(t3[s][:, :], MID), dinv, ALU.mult))
                    link(nc.vector.tensor_tensor(grouped(t3[s][:, :], MID), grouped(t3[s][:, :], MID), each_group(g.w["bg1"][:, 0:MID], J), ALU.add))
                    link(nc.vector.tensor_scalar(t3[s][:, :], t3[s][:, :], 0.0, None, ALU.max))
                    nc.vector.tensor_tensor(grouped(o[s][:, :], MID), grouped(t3[s][:, :], MID), dinv, ALU.mult).then_inc(ready, 1)
                pipeline(dve, close, slots=SLOTS)

            @block.scalar
            def _(act):
                def store(b):
                    act.wait_ge(ready, b.number + 1)
                    act.dma_start(chunk_of(g.t4, b.number), o[b.slot][:, :]).then_inc(stored[b.slot], 16)
                    act.dma_start(chunk_of(g.acc4, b.number), o[b.slot][:, :]).then_inc(stored[b.slot], 16)

                def landed(b):
                    act.wait_ge(stored[b.slot], 32 * b.nth)
                    act.sem_inc(free, 1)
                pipeline(act, store, None, landed, slots=SLOTS, oldest_first=True)


def gcn_close(nc, g, out):
    W = J * D
    M = J * MID
    with Room(nc, g, "gf") as r:
        x = [r.sb(f"x{k}", [P, W]) for k in range(SLOTS)]
        acc = [r.sb(f"acc{k}", [P, M]) for k in range(SLOTS)]
        uT = [r.sb(f"uT{k}", [P, M]) for k in range(2)]
        psT = [r.ps(f"psT{k}", [P, M]) for k in range(2)]
        psH = [r.ps(f"psH{k}", [P, W]) for k in range(2)]
        x_in, stored = ([r.sem(f"{n}{k}") for k in range(SLOTS)] for n in ("x_in", "stored"))
        free, biased, scaled, turned, evac, product, ready = (r.sem(n) for n in (
            "free", "biased", "scaled", "turned", "evac", "product", "ready"))
        with nc.Block() as block:
            @block.sync
            def _(sp):
                sp.sem_inc(free, SLOTS)

                def load(b):
                    sp.wait_ge(free, b.number + 1)
                    sp.dma_start(acc[b.slot][:, :], chunk_of(g.acc4, b.number)).then_inc(x_in[b.slot], 16)
                    sp.dma_start(x[b.slot][:, :], chunk_of(g.x3, b.number)).then_inc(x_in[b.slot], 16)
                pipeline(sp, load, slots=SLOTS)

            @block.vector
            def _(dve):
                def scale(b):
                    s = b.slot
                    dve.wait_ge(x_in[s], 32 * b.nth)
                    nc.vector.tensor_tensor(grouped(acc[s][:, :], MID), grouped(acc[s][:, :], MID),
                                            spread(g.dinv[:, bass.ds(b.number * J, J)], MID), ALU.mult).then_inc(scaled, 1)

                def close(b):
                    s = b.slot
                    dve.wait_ge(product, b.number + 1)
                    dve.wait_ge(biased, b.number + 1)
                    nc.vector.tensor_tensor(x[s][:, :], x[s][:, :], psH[s % 2][:, :], ALU.add).then_inc(ready, 1)
                pipeline(dve, scale, close, slots=SLOTS)

            @block.tensor
            def _(pe):
                def turn(b):
                    s = b.slot
                    pe.wait_ge(scaled, b.number + 1)
                    transpose_pairs(nc, psT[s % 2], acc[s], g.ident, J // 4).then_inc(turned, 1)
                    pe.wait_ge(evac, b.number + 1)
                    once_past(pe, ready, b, 2)
                    times(nc, psH[s % 2], uT[s % 2], g.w["gcn2"], J // 4).then_inc(product, 1)
                pipeline(pe, order=[(0, turn), (2, nothing)], slots=SLOTS)

            @block.scalar
            def _(act):
                def turn(b):
                    act.wait_ge(turned, b.number + 1)
                    nc.scalar.activation(uT[b.slot % 2][:, :], psT[b.slot % 2][:, :], ACT.Copy).then_inc(evac, 1)
                pipeline(act, turn, slots=SLOTS)

            @block.gpsimd
            def _(pool):
                whole = out[0:(STEPS - 1) * CHUNK, :].rearrange("(c p j) d -> c p (j d)", p=P, j=J)

                def bias(b):
                    s = b.slot
                    held(pool, x_in[s], 32 * b.nth, g.passed)
                    nc.gpsimd.tensor_tensor(grouped(x[s][:, :], D), grouped(x[s][:, :], D), each_group(g.w["bg2"][:, :], J), ALU.add).then_inc(biased, 1)

                def store(b):
                    held(pool, ready, b.number + 1, g.passed)
                    if isinstance(b.number, int) and b.number == STEPS - 1:
                        pool.dma_start(out[(STEPS - 1) * CHUNK:N, :].rearrange("(p j) d -> p (j d)", j=J), x[b.slot][0:LASTP, :]).then_inc(stored[b.slot], 16)
                    else:
                        pool.dma_start(whole[b.number], x[b.slot][:, :]).then_inc(stored[b.slot], 16)

                def landed(b):
                    held(pool, stored[b.slot], 16 * b.nth, g.passed)
                    pool.sem_inc(free, 1)
                pipeline(pool, bias, store, None, landed, slots=SLOTS, oldest_first=True)


NAMES = ["x", "src", "dst", "edge_attr_32", "edge_type_8", "edge_weight1", "L0_gnn_b", "L1_gnn_weight",
         "L2_gnn_q1_w", "L2_gnn_q1_b", "L2_gnn_k1_w", "L2_gnn_k1_b", "L2_gnn_v1_w", "L2_gnn_v1_b", "L2_gnn_e1_w",
         "L2_gnn_s1_w", "L2_gnn_s1_b", "L2_gnn_q2_w", "L2_gnn_q2_b", "L2_gnn_k2_w", "L2_gnn_k2_b", "L2_gnn_v2_w",
         "L2_gnn_v2_b", "L2_gnn_e2_w", "L2_gnn_s2_w", "L2_gnn_s2_b", "L2_gnn_skip_w", "L2_gnn_skip_b",
         "L3_gnn_W1", "L3_gnn_b1", "L3_gnn_W2", "L3_gnn_b2"]


def kernel(**inputs):
    import numpy as _np
    import concourse.bacc as _bacc
    from concourse import mybir as _mybir
    from concourse.bass_utils import run_bass_kernel_spmd as _run

    nc = _bacc.Bacc("TRN2", target_bir_lowering=False, num_devices=1)
    arrays, given = {}, {}
    for name in NAMES + ["W0T"]:
        v = _np.asarray(inputs["L0_gnn_W"]).T if name == "W0T" else _np.asarray(inputs[name])
        v = _np.ascontiguousarray(v)
        arrays[f"in_{name}"] = v
        given[name] = nc.dram_tensor(f"in_{name}", v.shape, _mybir.dt.from_np(v.dtype), kind="ExternalInput").ap()
    out = nc.dram_tensor("out_x", (N, D), _mybir.dt.float32, kind="ExternalOutput").ap()
    build(nc, given, out)
    r = _run(nc, [arrays], core_ids=[0])
    return r.results[0]["out_x"]
```

```python
import numpy as np
import concourse.bass as bass
from concourse import mybir
from contextlib import ExitStack

fp32 = mybir.dt.float32
i32 = mybir.dt.int32
bf16 = mybir.dt.bfloat16
fp16 = mybir.dt.float16
ALU = mybir.AluOpType
ACT = mybir.ActivationFunctionType
AXX = mybir.AxisListType.X

P = 128
D = 64
DE = 32
MID = 32
RELS = 8
N = 100000
E = 50000
J = 16
CHUNK = P * J
STEPS = 49
NP = STEPS * CHUNK
LASTP = (N - (STEPS - 1) * CHUNK) // J
B = 8
T = STEPS * B
SPARE = 2 * B * P
SLOTS = 4
DEEP = 6
FULL = E // T
REST = E - FULL * T
COLS = STEPS * J
PADROW = NP + P - 1
HUGE = 3.0e38
EPS = 1e-5
assert (N - (STEPS - 1) * CHUNK) % J == 0 and FULL == P - 1 and NP >= N


class Batch:

    def __init__(self, number, slot, nth):
        self.number, self.slot, self.nth = number, slot, nth


def pipeline(eng, *stages, slots=2, oldest_first=False, order=None):
    if order is None:
        order = [(d, stage) for d, stage in enumerate(stages) if stage is not None]
        if oldest_first:
            order.reverse()
    deepest = max(d for d, _ in order)

    def peeled(c):
        for d, stage in order:
            if 0 <= c - d < STEPS:
                stage(Batch(c - d, (c - d) % slots, (c - d) // slots + 1))

    lead = -(-deepest // slots) * slots
    end = STEPS // slots * slots
    for c in range(lead):
        peeled(c)
    with eng.Fori(lead // slots, end // slots) as i:
        for k in range(slots):
            for d, stage in order:
                stage(Batch(i * slots + (k - d), (k - d) % slots, i + ((k - d) // slots + 1)))
    for c in range(end, STEPS + deepest):
        peeled(c)


def nothing(b):
    pass


class Link:

    def __init__(self, eng, sem):
        self.eng, self.sem, self.n = eng, sem, 0

    def __call__(self, ins):
        self.n += 1
        ins.then_inc(self.sem, 1)
        self.eng.wait_ge(self.sem, self.n)

    def restart(self):
        self.eng.sem_clear(self.sem)
        self.n = 0


DMA_SIGNALS = {"loaded", "weights", "attrs", "zeroed", "o_stored", "x_in", "stored", "got", "ea_in", "seam_got", "seam_put",
               ("de", "added0"), ("de", "added1"), ("dd", "cleared")}


class Room:

    def __init__(self, nc, g, name):
        self.g = g
        self.nc, self.name, self.stack, self.sems = nc, name, ExitStack(), []

    def __enter__(self):
        return self

    def __exit__(self, *e):
        if self.sems and e[0] is None:
            with self.nc.Block() as block:
                @block.sync
                def _(sp):
                    for sem in self.sems:
                        sp.sem_clear(sem)
        return self.stack.__exit__(*e)

    def sb(self, name, shape, dt=fp32):
        return self.stack.enter_context(self.nc.sbuf_tensor(f"{self.name}_{name}", shape, dt))

    def ps(self, name, shape, dt=fp32):
        return self.stack.enter_context(self.nc.psum_tensor(f"{self.name}_{name}", shape, dt))

    def sem(self, name):
        if (self.name, name) in DMA_SIGNALS or name.rstrip("0123456789") in DMA_SIGNALS:
            return self.g.keeper.enter_context(self.nc.semaphore(f"{self.name}_{name}"))
        self.sems.append(self.stack.enter_context(self.nc.semaphore(f"{self.name}_{name}")))
        return self.sems[-1]


def held(eng, sem, value, passed):
    eng.wait_ge(sem, value)
    eng.sem_inc(passed, 1)


def once_past(eng, sem, b, back):
    if not (isinstance(b.number, int) and b.number < back):
        eng.wait_ge(sem, b.number - (back - 1))


def spread(ap, width):
    return ap.unsqueeze(2).to_broadcast([ap.shape[0], ap.shape[1], width])


def each_group(row, groups):
    return row.unsqueeze(1).to_broadcast([row.shape[0], groups, row.shape[1]])


def grouped(ap, width):
    return ap.rearrange("p (g f) -> p g f", f=width)


def chunk_of(table, c):
    return table[0:NP, :].rearrange("(c p j) d -> c p (j d)", p=P, j=J)[c]


def build(nc, a, out):
    with ExitStack() as ctx:
        def keep(name, shape, dt=fp32):
            return ctx.enter_context(nc.sbuf_tensor(name, shape, dt))

        def table(name, rows, width):
            return nc.dram_tensor(name, (rows, width), fp32, kind="Internal").ap()

        g = Graph()
        g.keeper = ctx
        g.passed = ctx.enter_context(nc.semaphore("passed"))
        g.t0 = table("t0", NP, D)
        g.acc0 = [table(f"acc0{k}", NP + SPARE, D) for k in range(2)]
        g.x1 = table("x1", NP, D)
        g.x2 = table("x2", NP + SPARE, D)
        g.g1 = table("g1", NP + SPARE, D)
        g.g2 = table("g2", NP + SPARE, D)
        g.skip = table("skip", NP, D)
        g.x3 = table("x3", NP, D)
        g.t3 = table("t3", NP, MID)
        g.acc3 = table("acc3", NP + SPARE, MID)
        g.t4 = table("t4", NP, MID)
        g.acc4 = table("acc4", NP + SPARE, MID)
        g.attr = table("attr", P * T, DE)
        g.near = table("near", P * T, D)
        g.sums = table("sums", P * T, D)
        g.ident = keep("ident", [P, P])
        g.ones = keep("ones", [P, P])
        g.zeros = keep("zeros", [P, 1024])
        g.eps = keep("eps", [P, 1])
        g.dummy_row = keep("dummy_row", [P, 1])
        g.src_f = keep("src_f", [P, T])
        g.src_rows = keep("src_rows", [P, T], i32)
        g.dst_rows = keep("dst_rows", [P, T], i32)
        g.last_rows = keep("last_rows", [P, T], i32)
        g.dst_f = keep("dst_f", [P, T])
        g.goes_on = keep("goes_on", [P, T])
        g.etype_f = keep("etype_f", [P, T])
        g.norm = keep("norm", [P, T])
        g.dis = keep("dis", [P, COLS])
        g.dinv = keep("dinv", [P, COLS])
        g.first_first = keep("first_first", [P, P])
        g.fix_first = keep("fix_first", [P, D])
        g.fix_last = keep("fix_last", [P, D])
        g.first_last = keep("first_last", [P, P])
        g.last_first = keep("last_first", [P, P])
        g.last_last = keep("last_last", [P, P])
        g.seam_sum = keep("seam_sum", [P, P])
        g.one_dst = keep("one_dst", [P, 1])
        g.seam_to = keep("seam_to", [P, 1], i32)
        for name in PAIR_WEIGHTS:
            setw(g, name, keep("w_" + name, [P, P]))
        for name in ("e1", "e2", "gcn2"):
            setw(g, name, keep("w_" + name, [P, 4 * D]))
        setw(g, "gcn1", keep("w_gcn1", [P, 2 * MID]))
        setw(g, "rel", keep("w_rel", [P, RELS * D]))
        for name in BIASES:
            setw(g, name, keep("b_" + name, [P, D]))

        setup(nc, g, a)
        out_degrees(nc, g)
        diffusion_dense(nc, g, a)
        diffusion_edges(nc, g)
        diffusion_close(nc, g)
        relation_edges(nc, g)
        attention_edges(nc, g, "at1", g.x2, True, ("q1", "k1", "v1", "e1"), ("bq1", "bk1", "bv1"),
                        [("s1", "bs1", g.g1)], g.g1)
        attention_edges(nc, g, "at2", g.g1, False, ("q2", "k2", "v2", "e2"), ("bq2", "bk2", "bv2"),
                        [("s2", "bs2", g.g2)], g.g2, ("skip_a", "bskip", g.g1, g.skip))
        skip_dense(nc, g)
        gcn_edges(nc, g, "gc1", g.t3, g.acc3)
        gcn_middle(nc, g)
        gcn_edges(nc, g, "gc2", g.t4, g.acc4)
        gcn_close(nc, g, out)


PAIR_WEIGHTS = {"w0": "W0T", "q1": "L2_gnn_q1_w", "k1": "L2_gnn_k1_w", "v1": "L2_gnn_v1_w", "s1": "L2_gnn_s1_w",
                "q2": "L2_gnn_q2_w", "k2": "L2_gnn_k2_w", "v2": "L2_gnn_v2_w", "s2": "L2_gnn_s2_w",
                "skip_a": "L2_gnn_skip_w", "skip_b": "L2_gnn_skip_w"}
BIASES = {"b0": "L0_gnn_b", "bq1": "L2_gnn_q1_b", "bk1": "L2_gnn_k1_b", "bv1": "L2_gnn_v1_b", "bs1": "L2_gnn_s1_b",
          "bq2": "L2_gnn_q2_b", "bk2": "L2_gnn_k2_b", "bv2": "L2_gnn_v2_b", "bs2": "L2_gnn_s2_b",
          "bskip": "L2_gnn_skip_b", "bg1": "L3_gnn_b1", "bg2": "L3_gnn_b2"}


class Graph:

    def __init__(self):
        self.w = {}


def setw(g, name, ap):
    g.w[name] = ap


def edge_load(eng, tile, flat, sem, shift=0):
    eng.dma_start(tile[0:FULL, :], flat[shift:shift + FULL * T].rearrange("(p t) -> p t", t=T)).then_inc(sem, 16)
    eng.dma_start(tile[FULL:P, 0:REST - shift], flat[FULL * T + shift:E].unsqueeze(0)).then_inc(sem, 16)


def setup(nc, g, a):
    w = g.w
    with Room(nc, g, "setup") as r:
        src_i, dst_i, next_i, type_i = (r.sb(n, [P, T], i32) for n in ("src_i", "dst_i", "next_i", "type_i"))
        next_f, ends, pad = r.sb("next_f", [P, T]), r.sb("ends", [P, T]), r.sb("pad", [P, T])
        diag = r.sb("diag", [P, 2, P])
        nowhere = r.sb("nowhere", [P, -(-T // (2 * B)) * 2 * B])
        before, after = r.sb("before", [P, P]), r.sb("after", [P, P])
        tmp = r.sb("tmp", [P, 4])
        ps_rows = r.ps("ps_rows", [P, 2 * P])
        cleared, loaded, weights, link_s, dve_diag, pe_rows, made, attrs = (r.sem(n) for n in (
            "cleared", "loaded", "weights", "link", "dve_diag", "pe_rows", "made", "attrs"))
        with nc.Block() as block:
            @block.vector
            def _(dve):
                link = Link(dve, link_s)
                for t in w:
                    nc.vector.memset(w[t][:, :], 0.0)
                for t, v in ((src_i, PADROW), (dst_i, PADROW), (next_i, PADROW), (type_i, 0)):
                    nc.vector.memset(t[:, :], v)
                nc.vector.memset(g.norm[:, :], 0.0)
                nc.vector.memset(g.eps[:, :], EPS)
                nc.vector.memset(g.ones[:, :], 1.0)
                nc.vector.memset(g.zeros[:, :], 0.0).then_inc(cleared, 1)
                dve.wait_ge(loaded, 5 * 32)
                link(nc.vector.tensor_copy(g.src_f[:, :], src_i[:, :]))
                link(nc.vector.tensor_copy(g.dst_f[:, :], dst_i[:, :]))
                link(nc.vector.tensor_copy(next_f[:, :], next_i[:, :]))
                link(nc.vector.tensor_copy(g.etype_f[:, :], type_i[:, :]))
                link(nc.vector.tensor_scalar(g.src_rows[:, :], g.src_f[:, :], float(N - 1), None, ALU.min))
                link(nc.vector.tensor_scalar(g.dst_rows[:, :], g.dst_f[:, :], float(N - 1), None, ALU.min))
                link(nc.vector.tensor_tensor(ends[:, :], g.dst_f[:, :], next_f[:, :], ALU.is_equal))
                link(nc.vector.memset(g.goes_on[:, 0:1], 0.0))
                link(nc.vector.tensor_copy(g.goes_on[:, 1:T], ends[:, 0:T - 1]))
                link(nc.vector.tensor_scalar(pad[:, :], g.dst_f[:, :], float(N), None, ALU.is_ge))
                link(nc.vector.tensor_tensor(ends[:, :], ends[:, :], pad[:, :], ALU.max))
                dve.wait_ge(made, 1)
                link(nc.vector.tensor_tensor(pad[:, :], nowhere[:, 0:T], g.dst_f[:, :], ALU.subtract))
                link(nc.vector.tensor_tensor(pad[:, :], pad[:, :], ends[:, :], ALU.mult))
                link(nc.vector.tensor_tensor(g.last_rows[:, :], pad[:, :], g.dst_f[:, :], ALU.add))
                dve.wait_ge(made, 4)
                link(nc.vector.tensor_scalar(diag[:, 0, :], g.ident[:, :], g.dst_f[:, 0:1], None, ALU.mult))
                nc.vector.tensor_scalar(diag[:, 1, :], g.ident[:, :], g.dst_f[:, T - 1:T], None, ALU.mult).then_inc(dve_diag, 1)
                dve.wait_ge(pe_rows, 1)
                firsts, lasts = ps_rows[:, 0:P], ps_rows[:, P:2 * P]
                first, last = g.dst_f[:, 0:1], g.dst_f[:, T - 1:T]
                link(nc.vector.tensor_scalar(g.first_first[:, :], firsts, first, None, ALU.is_equal))
                link(nc.vector.tensor_scalar(g.first_last[:, :], lasts, first, None, ALU.is_equal))
                link(nc.vector.tensor_scalar(g.last_first[:, :], firsts, last, None, ALU.is_equal))
                link(nc.vector.tensor_scalar(g.last_last[:, :], lasts, last, None, ALU.is_equal))
                nc.vector.tensor_tensor(g.one_dst[:, :], first, last, ALU.is_equal).then_inc(dve_diag, 1)
                link(nc.vector.tensor_tensor(diag[:, 0, :], g.first_last[:, :], before[:, :], ALU.mult))
                link(nc.vector.tensor_reduce(tmp[:, 2:3], diag[:, 0, :], AXX, ALU.add))
                link(nc.vector.tensor_tensor(diag[:, 0, :], g.first_first[:, :], after[:, :], ALU.mult))
                link(nc.vector.tensor_reduce(tmp[:, 3:4], diag[:, 0, :], AXX, ALU.add))
                link(nc.vector.tensor_scalar(tmp[:, 2:4], tmp[:, 2:4], 1.0, None, ALU.min))
                link(nc.vector.tensor_scalar(tmp[:, 3:4], tmp[:, 3:4], -1.0, 1.0, ALU.mult, ALU.add))
                link(nc.vector.tensor_tensor(tmp[:, 0:1], tmp[:, 2:3], tmp[:, 3:4], ALU.mult))
                link(nc.vector.tensor_tensor(tmp[:, 1:2], first, g.dummy_row[:, :], ALU.subtract))
                link(nc.vector.tensor_tensor(tmp[:, 1:2], tmp[:, 1:2], tmp[:, 0:1], ALU.mult))
                link(nc.vector.tensor_tensor(g.seam_to[:, :], tmp[:, 1:2], g.dummy_row[:, :], ALU.add))

            @block.tensor
            def _(pe):
                pe.wait_ge(dve_diag, 1)
                nc.tensor.matmul(ps_rows[:, 0:P], g.ones[:, :], diag[:, 0, :], start=True, stop=True)
                nc.tensor.matmul(ps_rows[:, P:2 * P], g.ones[:, :], diag[:, 1, :], start=True, stop=True).then_inc(pe_rows, 1)

            @block.gpsimd
            def _(pool):
                nc.gpsimd.iota(g.dummy_row[:, :], pattern=[[0, 1]], base=NP, channel_multiplier=1,
                               allow_small_or_imprecise_dtypes=True)
                nc.gpsimd.iota(nowhere[:, :], pattern=[[0, -(-T // (2 * B))], [P, 2 * B]], base=NP, channel_multiplier=1,
                               allow_small_or_imprecise_dtypes=True).then_inc(made, 1)
                pool.wait_ge(cleared, 1)
                nc.gpsimd.affine_select(out=g.ident[:, :], in_=g.zeros[:, 0:P], compare_op=ALU.not_equal, fill=1.0,
                                        base=0, pattern=[[-1, P]], channel_multiplier=1).then_inc(made, 1)
                for mask, sign in ((before, -1), (after, 1)):
                    nc.gpsimd.affine_select(out=mask[:, :], in_=g.ones[:, :], compare_op=ALU.is_gt, fill=0.0,
                                            base=0, pattern=[[sign, P]], channel_multiplier=-sign).then_inc(made, 1)
                pool.wait_ge(dve_diag, 2)
                nc.gpsimd.affine_select(out=g.seam_sum[:, :], in_=g.last_first[:, :], compare_op=ALU.is_gt, fill=0.0,
                                        base=0, pattern=[[1, P]], channel_multiplier=-1)

            @block.sync
            def _(sp):
                sp.wait_ge(cleared, 1)
                edge_load(sp, src_i, a["src"], loaded)
                edge_load(sp, dst_i, a["dst"], loaded)
                edge_load(sp, next_i, a["dst"], loaded, shift=1)
                edge_load(sp, type_i, a["edge_type_8"], loaded)
                edge_load(sp, g.norm, a["edge_weight1"].rearrange("e o -> (e o)"), loaded)
                sp.dma_start(g.attr[0:E, :].rearrange("(p k) d -> p (k d)", p=80),
                             a["edge_attr_32"].rearrange("(p k) d -> p (k d)", p=80)).then_inc(attrs, 16)
                sp.dma_start(g.attr[E:P * T, :].rearrange("(p k) d -> p (k d)", p=16),
                             g.zeros[0:16, 0:(P * T - E) * DE // 16]).then_inc(attrs, 16)
                for tab in (*g.acc0, g.x2, g.g1, g.g2, g.acc3, g.acc4):
                    width = tab.shape[1]
                    sp.dma_start(tab[NP:NP + SPARE, :].rearrange("(p k) d -> p (k d)", p=P),
                                 g.zeros[:, 0:SPARE // P * width]).then_inc(attrs, 16)
                sp.wait_ge(attrs, 32 + 7 * 16)
                sp.wait_ge(loaded, 5 * 32)

            @block.scalar
            def _(act):
                act.wait_ge(cleared, 1)
                count = 0

                def load(dst, src):
                    act.dma_start(dst, src).then_inc(weights, 16)

                for name, given in PAIR_WEIGHTS.items():
                    rows = a[given]
                    rows = rows[D:2 * D, :] if name == "skip_b" else rows[0:D, :]
                    for k in range(2):
                        load(w[name][k * D:(k + 1) * D, k * D:(k + 1) * D], rows)
                        count += 1
                for name, given in (("e1", "L2_gnn_e1_w"), ("e2", "L2_gnn_e2_w"), ("gcn2", "L3_gnn_W2")):
                    for k in range(4):
                        load(w[name][k * DE:(k + 1) * DE, k * D:(k + 1) * D], a[given])
                        count += 1
                for k in range(2):
                    load(w["gcn1"][k * D:(k + 1) * D, k * MID:(k + 1) * MID], a["L3_gnn_W1"])
                    load(w["rel"][k * D:(k + 1) * D, :].rearrange("i (r o) -> i r o", r=RELS),
                         a["L1_gnn_weight"].rearrange("r i o -> i r o"))
                    count += 2
                for name, given in BIASES.items():
                    f = a[given].shape[0]
                    load(w[name][:, 0:f], a[given].unsqueeze(0).to_broadcast([P, f]))
                    count += 1
                act.wait_ge(weights, 16 * count)


class Counter:

    HALVES = ((0, 512), (512, COLS))

    def __init__(self, nc, r):
        self.nc = nc
        self.as_int, self.part_i = r.sb("as_int", [P, T], i32), r.sb("part_i", [P, T], i32)
        self.low_f, self.chunk_f, self.part_f, self.col_f = (r.sb(n, [P, T]) for n in ("low", "chunk", "part", "col"))
        self.iota = r.sb("iota", [P, COLS], fp16)
        self.hot_part = r.sb("hot_part", [P, 2, B, P], bf16)
        self.hot_col = r.sb("hot_col", [P, 2, B, COLS], bf16)
        self.blank = r.sb("blank", [P, 512], bf16)
        self.counts = r.ps("counts", [P, 1024])
        self.columns, self.blanked, self.hot, self.used, self.counted, self.root, self.rooted = (r.sem(n) for n in (
            "columns", "blanked", "hot", "used", "counted", "root", "rooted"))

    def number_columns(self):
        self.nc.gpsimd.iota(self.iota[:, :], pattern=[[1, COLS]], base=0, channel_multiplier=0,
                            allow_small_or_imprecise_dtypes=True).then_inc(self.columns, 1)

    def split(self, dve, link, index):
        nc = self.nc
        nc.vector.memset(self.blank[:, :], 0.0).then_inc(self.blanked, 1)
        link(nc.vector.tensor_copy(self.as_int[:, :], index[:, :]))
        link(nc.vector.tensor_scalar(self.part_i[:, :], self.as_int[:, :], 4, 127, ALU.logical_shift_right, ALU.bitwise_and))
        link(nc.vector.tensor_copy(self.part_f[:, :], self.part_i[:, :]))
        link(nc.vector.tensor_scalar(self.part_i[:, :], self.as_int[:, :], 15, None, ALU.bitwise_and))
        link(nc.vector.tensor_copy(self.low_f[:, :], self.part_i[:, :]))
        link(nc.vector.tensor_scalar(self.part_i[:, :], self.as_int[:, :], 11, None, ALU.logical_shift_right))
        link(nc.vector.tensor_copy(self.chunk_f[:, :], self.part_i[:, :]))
        link(nc.vector.scalar_tensor_tensor(self.col_f[:, :], self.chunk_f[:, :], float(J), self.low_f[:, :], ALU.mult, ALU.add))
        dve.wait_ge(self.columns, 1)
        nc.vector.sem_inc(self.used, 2)

    def one_hot(self, dve, b):
        dve.wait_ge(self.used, b.number + 1)
        for t in range(B):
            at = bass.ds(b.number * B + t, 1)
            self.nc.vector.tensor_scalar(self.hot_part[:, b.slot, t, :], self.iota[:, 0:P], self.part_f[:, at], None, ALU.is_equal)
            last = self.nc.vector.tensor_scalar(self.hot_col[:, b.slot, t, :], self.iota[:, :], self.col_f[:, at], None, ALU.is_equal)
        last.then_inc(self.hot, 1)

    def begin(self, pe):
        pe.wait_ge(self.blanked, 1)
        for lo, hi in self.HALVES:
            self.nc.tensor.matmul(self.counts[:, lo:hi], self.blank[:, 0:P], self.blank[:, 0:hi - lo], start=True, stop=False,
                                  skip_group_check=True)

    def count(self, pe, b):
        pe.wait_ge(self.hot, b.number + 1)
        for t in range(B):
            for lo, hi in self.HALVES:
                last = self.nc.tensor.matmul(self.counts[:, lo:hi], self.hot_part[:, b.slot, t, :],
                                             self.hot_col[:, b.slot, t, lo:hi], start=False, stop=False, skip_group_check=True)
        last.then_inc(self.used, 1)

    def end(self, pe):
        for lo, hi in self.HALVES:
            last = self.nc.tensor.matmul(self.counts[:, lo:hi], self.blank[:, 0:P], self.blank[:, 0:hi - lo], start=False, stop=True,
                                         skip_group_check=True)
        last.then_inc(self.counted, 1)

    def invert(self, dve, link, to):
        dve.wait_ge(self.counted, 1)
        link(self.nc.vector.tensor_scalar(to[:, :], self.counts[:, 0:COLS], 1.0, None, ALU.add))
        link(self.nc.vector.reciprocal(to[:, :], to[:, :]))
        self.nc.vector.sem_inc(self.root, 1)

    def take_root(self, act, to):
        act.wait_ge(self.root, 1)
        self.nc.scalar.activation(to[:, :], to[:, :], ACT.Sqrt).then_inc(self.rooted, 1)
        act.wait_ge(self.rooted, 1)


def out_degrees(nc, g):
    with Room(nc, g, "deg") as r:
        counter = Counter(nc, r)
        link_s = r.sem("link")
        with nc.Block() as block:
            @block.gpsimd
            def _(pool):
                counter.number_columns()

            @block.vector
            def _(dve):
                link = Link(dve, link_s)
                counter.split(dve, link, g.src_f)
                pipeline(dve, lambda b: counter.one_hot(dve, b))
                counter.invert(dve, link, g.dis)

            @block.tensor
            def _(pe):
                counter.begin(pe)
                pipeline(pe, lambda b: counter.count(pe, b))
                counter.end(pe)

            @block.scalar
            def _(act):
                counter.take_root(act, g.dis)


def transpose_pairs(nc, to, src, ident, n):
    for k in range(n):
        last = nc.tensor.transpose(to[:, k * P:(k + 1) * P], src[:, k * P:(k + 1) * P], ident[:, :])
    return last


def times(nc, to, left, weight, n, start=True, stop=True):
    wide = weight.shape[1]
    for k in range(n):
        last = nc.tensor.matmul(to[:, k * wide:(k + 1) * wide], left[:, k * P:(k + 1) * P], weight[:, :],
                                start=start, stop=stop, skip_group_check=not (start and stop))
    return last


def mean_off(nc, link, x, centred, sums, groups):
    link(nc.vector.tensor_reduce(sums, grouped(x, D), AXX, ALU.add))
    link(nc.vector.tensor_scalar(sums, sums, -1.0 / D, None, ALU.mult))
    return nc.vector.tensor_tensor(grouped(centred, D), grouped(x, D), spread(sums, D), ALU.add)


def diffusion_dense(nc, g, a):
    W = J * D
    with Room(nc, g, "dd") as r:
        x, cen, lo, hi = ([r.sb(f"{n}{k}", [P, W]) for k in range(DEEP)] for n in ("x", "cen", "t0", "base"))
        sq, hT, h0, rl = ([r.sb(f"{n}{k}", [P, W]) for k in range(2)] for n in ("sq", "hT", "h0", "rl"))
        sums, sd = r.sb("sums", [P, DEEP, J]), r.sb("sd", [P, DEEP, J])
        psT = [r.ps(f"psT{k}", [P, W]) for k in range(2)]
        psH = [r.ps(f"psH{k}", [P, W]) for k in range(2)]
        x_in = [r.sem(f"x_in{k}") for k in range(DEEP)]
        stored = [r.sem(f"stored{k}") for k in range(DEEP)]
        grow = r.sb("grow", [P, COLS])
        x_free, o_free, link_s, squared, centred, summed, rooted, normed, turned, evac, product, h_made, mixed, relued, scaled, ready, cleared, lo_made, blended = (r.sem(n) for n in (
            "x_free", "o_free", "link", "squared", "centred", "summed", "rooted", "normed", "turned", "evac", "product", "h_made", "mixed", "relued", "scaled", "ready", "cleared", "lo_made", "blended"))
        with nc.Block() as block:
            @block.sync
            def _(sp):
                sp.sem_inc(x_free, DEEP)
                view = a["x"]

                def load(b):
                    sp.wait_ge(x_free, b.number + 1)
                    if isinstance(b.number, int) and b.number == STEPS - 1:
                        sp.dma_start(x[b.slot][LASTP:P, :], g.zeros[LASTP:P, :]).then_inc(cleared, 16)
                        sp.wait_ge(cleared, 16)
                        sp.dma_start(x[b.slot][0:LASTP, :], view[(STEPS - 1) * CHUNK:N, :].rearrange("(p j) d -> p (j d)", j=J)).then_inc(x_in[b.slot], 16)
                    else:
                        whole = view[0:(STEPS - 1) * CHUNK, :].rearrange("(c p j) d -> c p (j d)", p=P, j=J)
                        sp.dma_start(x[b.slot][:, :], whole[b.number]).then_inc(x_in[b.slot], 16)
                pipeline(sp, load, slots=DEEP)

            @block.vector
            def _(dve):
                link = Link(dve, link_s)

                def centre(b):
                    s = b.slot
                    link.restart()
                    dve.wait_ge(x_in[s], 16 * b.nth)
                    mean_off(nc, link, x[s][:, :], cen[s][:, :], sums[:, s, :], J).then_inc(centred, 1)

                def variance(b):
                    s = b.slot
                    dve.wait_ge(squared, b.number + 1)
                    nc.vector.tensor_reduce(sd[:, s, :], grouped(sq[s % 2][:, :], D), AXX, ALU.add).then_inc(summed, 1)

                def scale(b):
                    s = b.slot
                    dve.wait_ge(rooted, b.number + 1)
                    link(nc.vector.reciprocal(sd[:, s, :], sd[:, s, :]))
                    nc.vector.tensor_tensor(grouped(cen[s][:, :], D), grouped(cen[s][:, :], D), spread(sd[:, s, :], D), ALU.mult).then_inc(normed, 1)

                def close(b):
                    s = b.slot
                    dve.wait_ge(product, b.number + 1)
                    dve.wait_ge(scaled, b.number + 1)
                    dve.wait_ge(o_free, b.number + 1)
                    nc.vector.tensor_tensor(grouped(h0[s % 2][:, :], D), grouped(psH[s % 2][:, :], D), each_group(g.w["b0"][:, :], J), ALU.add).then_inc(h_made, 1)
                    dve.wait_ge(h_made, b.number + 1)
                    nc.vector.scalar_tensor_tensor(hi[s][:, :], h0[s % 2][:, :], 0.95, x[s][:, :], ALU.mult, ALU.add).then_inc(blended, 1)

                link(nc.vector.reciprocal(grow[:, :], g.dis[:, :]))
                link(nc.vector.tensor_scalar(grow[:, :], grow[:, :], 20.0, None, ALU.mult))
                pipeline(dve, order=[(2, scale), (1, variance), (3, close), (0, centre)], slots=DEEP)

            @block.scalar
            def _(act):
                def norm(b):
                    s = b.slot
                    act.wait_ge(centred, b.number + 1)
                    if not (isinstance(b.number, int) and b.number < 2):
                        act.wait_ge(summed, b.number - 1)
                    nc.scalar.activation(sq[s % 2][:, :], cen[s][:, :], ACT.Square).then_inc(squared, 1)

                def root(b):
                    s = b.slot
                    act.wait_ge(summed, b.number + 1)
                    nc.scalar.activation(sd[:, s, :], sd[:, s, :], ACT.Sqrt, bias=g.eps[:, :], scale=1.0 / D).then_inc(rooted, 1)

                def turn(b):
                    s = b.slot
                    act.wait_ge(turned, b.number + 1)
                    nc.scalar.activation(hT[s % 2][:, :], psT[s % 2][:, :], ACT.Relu).then_inc(evac, 1)

                def positive(b):
                    act.wait_ge(h_made, b.number + 1)
                    once_past(act, mixed, b, 2)
                    nc.scalar.activation(rl[b.slot % 2][:, :], h0[b.slot % 2][:, :], ACT.Relu, scale=1.5).then_inc(relued, 1)

                def store(b):
                    s = b.slot
                    act.wait_ge(ready, b.number + 1)
                    act.dma_start(chunk_of(g.t0, b.number), lo[s][:, :]).then_inc(stored[s], 16)
                    act.dma_start(chunk_of(g.acc0[0], b.number), lo[s][:, :]).then_inc(stored[s], 16)
                    act.dma_start(chunk_of(g.acc0[1], b.number), hi[s][:, :]).then_inc(stored[s], 16)

                def landed(b):
                    act.wait_ge(stored[b.slot], 48 * b.nth)
                    act.sem_inc(o_free, 1)
                act.sem_inc(o_free, DEEP)
                pipeline(act, order=[(1, norm), (1, root), (2, turn), (3, positive), (5, store), (6, landed)], slots=DEEP)

            @block.tensor
            def _(pe):
                def turn(b):
                    s = b.slot
                    pe.wait_ge(normed, b.number + 1)
                    transpose_pairs(nc, psT[s % 2], cen[s], g.ident, J // 2).then_inc(turned, 1)
                    pe.wait_ge(evac, b.number + 1)
                    once_past(pe, h_made, b, 2)
                    times(nc, psH[s % 2], hT[s % 2], g.w["w0"], J // 2).then_inc(product, 1)
                pipeline(pe, order=[(0, turn), (2, nothing)], slots=DEEP)

            @block.gpsimd
            def _(pool):
                pool.sem_inc(scaled, 2)

                def mix(b):
                    s = b.slot
                    at = bass.ds(b.number * J, J)
                    held(pool, h_made, b.number + 1, g.passed)
                    nc.gpsimd.tensor_tensor(grouped(lo[s][:, :], D), grouped(h0[s % 2][:, :], D), spread(g.dis[:, at], D), ALU.mult).then_inc(lo_made, 1)
                    held(pool, blended, b.number + 1, g.passed)
                    pool.sem_inc(x_free, 1)
                    held(pool, relued, b.number + 1, g.passed)
                    held(pool, lo_made, b.number + 1, g.passed)
                    pool.sem_inc(scaled, 1)
                    nc.gpsimd.tensor_tensor(hi[s][:, :], hi[s][:, :], rl[s % 2][:, :], ALU.add).then_inc(mixed, 1)
                    held(pool, mixed, b.number + 1, g.passed)
                    nc.gpsimd.tensor_tensor(grouped(hi[s][:, :], D), grouped(hi[s][:, :], D), spread(grow[:, at], D), ALU.mult).then_inc(ready, 1)
                pipeline(pool, mix, slots=DEEP)


def gather(nc, buf, table, rows, sem, groups=B):
    width = table.shape[1]
    for t in range(groups):
        nc.gpsimd.indirect_dma_start(buf[:, t * width:(t + 1) * width], None, table,
                                     bass.IndirectOffsetOnAxis(ap=rows[:, t:t + 1], axis=0)).then_inc(sem, 16)


def add_rows(nc, buf, table, rows, sem, groups=B):
    width = table.shape[1]
    for t in range(groups):
        nc.gpsimd.indirect_dma_start(table, bass.IndirectOffsetOnAxis(ap=rows[:, t:t + 1], axis=0),
                                     buf[:, t * width:(t + 1) * width], None, compute_op=ALU.add).then_inc(sem, 16)


def diffusion_edges(nc, g):
    W = B * D
    with Room(nc, g, "de") as r:
        rows = [r.sb(f"rows{k}", [P, W]) for k in range(2)]
        summed = [r.sb(f"summed{k}", [P, W]) for k in range(2)]
        take = [r.sb(f"take{k}", [P, B], i32) for k in range(2)]
        put = [r.sb(f"put{k}", [P, B], i32) for k in range(2)]
        diag = r.sb("diag", [P, B, P])
        same = [r.sb(f"same{k}", [P, B, P]) for k in range(2)]
        later = r.sb("later", [P, P])
        dup, toward = r.sb("dup", [P, B]), r.sb("toward", [P, B])
        ps_src = r.ps("ps_src", [P, B * P])
        ps_sum = [r.ps(f"ps_sum{k}", [P, W]) for k in range(2)]
        got = [r.sem(f"got{k}") for k in range(2)]
        added = [r.sem(f"added{k}") for k in range(2)]
        free, link_s, staged, mask, dve_diag, src_rows, same_made, product, ready = (r.sem(n) for n in (
            "free", "link", "staged", "mask", "dve_diag", "src_rows", "same_made", "product", "ready"))
        counter = Counter(nc, r)
        with nc.Block() as block:
            @block.gpsimd
            def _(pool):
                nc.gpsimd.affine_select(out=later[:, :], in_=g.ones[:, :], compare_op=ALU.is_gt, fill=0.0,
                                        base=0, pattern=[[1, P]], channel_multiplier=-1).then_inc(mask, 1)
                counter.number_columns()
                pool.sem_inc(free, 2)

                def fetch(b):
                    s = b.slot
                    held(pool, free, b.number + 1, g.passed)
                    nc.gpsimd.tensor_copy(take[s][:, :], g.dst_rows[:, bass.ds(b.number * B, B)]).then_inc(staged, 1)
                    held(pool, staged, b.number + 1, g.passed)

                def add(b):
                    held(pool, ready, b.number + 1, g.passed)

                def both(f, d):
                    for t in range(B):
                        if f is not None:
                            s = f.slot
                            nc.gpsimd.indirect_dma_start(rows[s][:, t * D:(t + 1) * D], None, g.t0,
                                                         bass.IndirectOffsetOnAxis(ap=take[s][:, t:t + 1], axis=0)).then_inc(got[s], 16)
                        if d is not None:
                            s = d.slot
                            if not (isinstance(d.number, int) and d.number == 0 and t < 2):
                                held(pool, added[t % 2], 16 * (d.number * (B // 2) + t // 2), g.passed)
                            nc.gpsimd.indirect_dma_start(g.acc0[t % 2], bass.IndirectOffsetOnAxis(ap=put[s][:, t:t + 1], axis=0),
                                                         summed[s][:, t * D:(t + 1) * D], None, compute_op=ALU.add).then_inc(added[t % 2], 16)

                for c in (0, 1):
                    fetch(Batch(c, c, 1))
                    both(Batch(c, c, 1), None)
                with pool.Fori(1, STEPS // 2) as i:
                    for k in range(2):
                        f, d = Batch(i * 2 + k, k, i + 1), Batch(i * 2 + k - 2, k, i)
                        add(d)
                        fetch(f)
                        both(f, d)
                last, d = Batch(STEPS - 1, 0, STEPS // 2 + 1), Batch(STEPS - 3, 0, STEPS // 2)
                add(d)
                fetch(last)
                both(last, d)
                for d in (Batch(STEPS - 2, 1, 0), Batch(STEPS - 1, 0, 0)):
                    add(d)
                    both(None, d)
                for k in range(2):
                    pool.wait_ge(added[k], 16 * (T // 2))

            @block.vector
            def _(dve):
                link = Link(dve, link_s)
                dve.wait_ge(mask, 1)
                counter.split(dve, link, g.dst_f)
                link.restart()

                def equal(b):
                    s = b.slot
                    src = g.src_f[:, bass.ds(b.number * B, B)]
                    nc.vector.tensor_tensor(diag[:, :, :], each_group(g.ident[:, :], B), spread(src, P), ALU.mult).then_inc(dve_diag, 1)
                    dve.wait_ge(src_rows, b.number + 1)
                    link(nc.vector.tensor_tensor(same[s][:, :, :], ps_src[:, :].rearrange("p (b q) -> p b q", q=P), spread(src, P), ALU.is_equal))
                    nc.vector.sem_inc(same_made, 1)
                    link(nc.vector.tensor_tensor(diag[:, :, :], same[s][:, :, :], each_group(later[:, :], B), ALU.mult))
                    link(nc.vector.tensor_reduce(dup[:, :], diag[:, :, :], AXX, ALU.max))
                    link(nc.vector.tensor_scalar(toward[:, :], src, -1.0, g.dummy_row[:, :], ALU.mult, ALU.add))
                    link(nc.vector.tensor_tensor(toward[:, :], toward[:, :], dup[:, :], ALU.mult))

                def point(b):
                    s = b.slot
                    src = g.src_f[:, bass.ds(b.number * B, B)]
                    if not (isinstance(b.number, int) and b.number < 2):
                        for k in range(2):
                            dve.wait_ge(added[k], 16 * (B // 2) * (b.number - 1))
                    link(nc.vector.tensor_tensor(put[s][:, :], toward[:, :], src, ALU.add))
                    link.restart()

                def carry(b):
                    s = b.slot
                    dve.wait_ge(product, b.number + 1)
                    nc.vector.tensor_copy(summed[s][:, :], ps_sum[s][:, :]).then_inc(ready, 1)
                    dve.wait_ge(ready, b.number + 1)
                pipeline(dve, order=[(0, equal), (1, carry), (0, point), (1, lambda b: counter.one_hot(dve, b)), (2, nothing)])
                counter.invert(dve, link, g.dinv)

            @block.tensor
            def _(pe):
                def turn(b):
                    pe.wait_ge(dve_diag, b.number + 1)
                    for h in range(2):
                        last = nc.tensor.matmul(ps_src[:, h * 512:(h + 1) * 512], g.ones[:, :],
                                                diag[:, :, :].rearrange("p b q -> p (b q)")[:, h * 512:(h + 1) * 512], start=True, stop=True)
                    last.then_inc(src_rows, 1)

                def merge(b):
                    s = b.slot
                    pe.wait_ge(same_made, b.number + 1)
                    pe.wait_ge(got[s], 16 * B * b.nth)
                    for t in range(B):
                        last = nc.tensor.matmul(ps_sum[s][:, t * D:(t + 1) * D], same[s][:, t, :],
                                                rows[s][:, t * D:(t + 1) * D], start=True, stop=True)
                    last.then_inc(product, 1)
                    pe.wait_ge(product, b.number + 1)
                    pe.sem_inc(free, 1)
                counter.begin(pe)
                pipeline(pe, order=[(0, turn), (1, merge), (1, lambda b: counter.count(pe, b))])
                counter.end(pe)

            @block.scalar
            def _(act):
                counter.take_root(act, g.dinv)


def diffusion_close(nc, g):
    W = J * D
    with Room(nc, g, "dc") as r:
        base, acc = ([r.sb(f"{n}{k}", [P, W]) for k in range(SLOTS)] for n in ("base", "acc"))
        tiny = r.sb("tiny", [P, COLS])
        x_in, stored = ([r.sem(f"{n}{k}") for k in range(SLOTS)] for n in ("x_in", "stored"))
        free, link_s, ready = (r.sem(n) for n in ("free", "link", "ready"))
        with nc.Block() as block:
            @block.sync
            def _(sp):
                sp.sem_inc(free, SLOTS)

                def load(b):
                    sp.wait_ge(free, b.number + 1)
                    sp.dma_start(base[b.slot][:, :], chunk_of(g.acc0[1], b.number)).then_inc(x_in[b.slot], 16)
                    sp.dma_start(acc[b.slot][:, :], chunk_of(g.acc0[0], b.number)).then_inc(x_in[b.slot], 16)
                pipeline(sp, load, slots=SLOTS)

            @block.vector
            def _(dve):
                link = Link(dve, link_s)
                link(nc.vector.tensor_scalar(tiny[:, :], g.dis[:, :], 0.05, None, ALU.mult))

                def close(b):
                    s = b.slot
                    link.restart()
                    dve.wait_ge(x_in[s], 32 * b.nth)
                    link(nc.vector.tensor_tensor(base[s][:, :], base[s][:, :], acc[s][:, :], ALU.add))
                    nc.vector.tensor_tensor(grouped(base[s][:, :], D), grouped(base[s][:, :], D), spread(tiny[:, bass.ds(b.number * J, J)], D), ALU.mult).then_inc(ready, 1)
                pipeline(dve, close, slots=SLOTS)

            @block.scalar
            def _(act):
                def store(b):
                    s = b.slot
                    act.wait_ge(ready, b.number + 1)
                    act.dma_start(chunk_of(g.x1, b.number), base[s][:, :]).then_inc(stored[s], 16)
                    act.dma_start(chunk_of(g.x2, b.number), base[s][:, :]).then_inc(stored[s], 16)

                def landed(b):
                    act.wait_ge(stored[b.slot], 32 * b.nth)
                    act.sem_inc(free, 1)
                pipeline(act, store, None, landed, slots=SLOTS, oldest_first=True)



def running_sums(nc, link, tot, slot, msg, g, b, width):
    for t in range(B):
        if t == B - 1:
            link.restart()
        before = tot[slot][:, (t - 1) * width:t * width] if t else tot[1 - slot][:, (B - 1) * width:B * width]
        ins = nc.vector.scalar_tensor_tensor(tot[slot][:, t * width:(t + 1) * width], before,
                                             g.goes_on[:, bass.ds(b.number * B + t, 1)],
                                             msg[:, t * width:(t + 1) * width], ALU.mult, ALU.add)
        if t < B - 1:
            link(ins)
    return ins


def seam(nc, g, r, agg, tot, width):
    carried = r.sb("seam_carried", [P, width])
    ps = r.ps("seam_ps", [P, width])
    product, summed, put = (r.sem("seam_" + n) for n in ("product", "summed", "put"))
    with nc.Block() as block:
        @block.tensor
        def _(pe):
            nc.tensor.matmul(ps[:, :], g.seam_sum[:, :], tot[:, (B - 1) * width:B * width], start=True, stop=True).then_inc(product, 1)

        @block.gpsimd
        def _(pool):
            pool.wait_ge(summed, 1)
            add_rows(nc, carried, agg, g.seam_to, put, groups=1)
            pool.wait_ge(put, 16)

        @block.vector
        def _(dve):
            dve.wait_ge(product, 1)
            nc.vector.tensor_copy(carried[:, :], ps[:, :]).then_inc(summed, 1)


def relation_edges(nc, g):
    W = B * D
    with Room(nc, g, "re") as r:
        rows, hT, tot, cen = ([r.sb(f"{n}{k}", [P, W]) for k in range(2)] for n in ("rows", "hT", "tot", "cen"))
        take, put = ([r.sb(f"{n}{k}", [P, B], i32) for k in range(2)] for n in ("take", "put"))
        sq, msg = (r.sb(n, [P, W]) for n in ("sq", "msg"))
        sums, sd = r.sb("sums", [P, B]), [r.sb(f"sd{k}", [P, B]) for k in range(2)]
        rel = r.sb("rel", [P, RELS])
        coef = r.sb("coef", [P, B, RELS])
        picked = [r.sb(f"picked{k}", [P, RELS * D]) for k in range(2)]
        psT = r.ps("psT", [P, W])
        psR = [r.ps(f"psR{k}", [P, RELS * D]) for k in range(4)]
        got, stored = ([r.sem(f"{n}{k}") for k in range(2)] for n in ("got", "stored"))
        free, sum_free, link_s, relno, staged, staged_put, centred, squared, summed, rooted, turned, evac, product, read, reduced, ready = (r.sem(n) for n in (
            "free", "sum_free", "link", "relno", "staged", "staged_put", "centred", "squared", "summed", "rooted", "turned", "evac", "product", "read", "reduced", "ready"))
        with nc.Block() as block:
            @block.gpsimd
            def _(pool):
                nc.gpsimd.iota(rel[:, :], pattern=[[1, RELS]], base=0, channel_multiplier=0,
                               allow_small_or_imprecise_dtypes=True).then_inc(relno, 1)
                pool.sem_inc(free, 2)
                pool.sem_inc(sum_free, 2)

                def fetch(b):
                    s = b.slot
                    held(pool, free, b.number + 1, g.passed)
                    nc.gpsimd.tensor_copy(take[s][:, :], g.src_rows[:, bass.ds(b.number * B, B)]).then_inc(staged, 1)
                    held(pool, staged, b.number + 1, g.passed)
                    gather(nc, rows[s], g.x1, take[s], got[s])

                def send(b):
                    s = b.slot
                    held(pool, ready, b.number + 1, g.passed)
                    nc.gpsimd.tensor_copy(put[s][:, :], g.last_rows[:, bass.ds(b.number * B, B)]).then_inc(staged_put, 1)
                    held(pool, staged_put, b.number + 1, g.passed)
                    add_rows(nc, tot[s], g.x2, put[s], stored[s])

                def landed(b):
                    held(pool, stored[b.slot], 16 * B * b.nth, g.passed)
                    pool.sem_inc(sum_free, 1)

                pipeline(pool, order=[(0, fetch), (4, landed), (3, send)])

            @block.vector
            def _(dve):
                link = Link(dve, link_s)
                dve.wait_ge(relno, 1)
                link(nc.vector.memset(tot[1][:, :], 0.0))
                link.restart()

                def centre(b):
                    s = b.slot
                    dve.wait_ge(got[s], 16 * B * b.nth)
                    once_past(dve, turned, b, 2)
                    mean_off(nc, link, rows[s][:, :], cen[s][:, :], sums[:, :], B).then_inc(centred, 1)
                    dve.wait_ge(centred, b.number + 1)
                    nc.vector.sem_inc(free, 1)

                def variance(b):
                    dve.wait_ge(squared, b.number + 1)
                    nc.vector.tensor_reduce(sd[b.slot][:, :], grouped(sq[:, :], D), AXX, ALU.add).then_inc(summed, 1)

                def pick(b):
                    s = b.slot
                    at = bass.ds(b.number * B, B)
                    link(nc.vector.tensor_tensor(coef[:, :, :], each_group(rel[:, :], B), spread(g.etype_f[:, at], RELS), ALU.is_equal))
                    dve.wait_ge(rooted, b.number + 1)
                    link(nc.vector.reciprocal(sd[s][:, :], sd[s][:, :]))
                    link(nc.vector.tensor_tensor(sd[s][:, :], sd[s][:, :], g.norm[:, at], ALU.mult))
                    link(nc.vector.tensor_tensor(coef[:, :, :], coef[:, :, :], spread(sd[s][:, :], RELS), ALU.mult))
                    def own(t):
                        dve.wait_ge(product, b.number * B + t + 1)
                        if t >= 2:
                            dve.wait_ge(reduced, b.number * B + (t - 1))
                        nc.vector.tensor_tensor(grouped(picked[t % 2][:, :], D), grouped(psR[t % 4][:, :], D),
                                                spread(coef[:, t, :], D), ALU.mult).then_inc(read, 1)
                    own(0)
                    for t in range(B):
                        if t + 1 < B:
                            own(t + 1)
                        dve.wait_ge(read, b.number * B + t + 1)
                        nc.vector.tensor_reduce(msg[:, t * D:(t + 1) * D], picked[t % 2][:, :].rearrange("p (r o) -> p o r", r=RELS), AXX, ALU.add).then_inc(reduced, 1)
                    dve.wait_ge(reduced, b.number * B + B)
                    dve.wait_ge(sum_free, b.number + 1)
                    running_sums(nc, link, tot, s, msg, g, b, D).then_inc(ready, 1)
                    dve.wait_ge(ready, b.number + 1)
                pipeline(dve, order=[(1, variance), (2, pick), (0, centre), (4, nothing)])

            @block.scalar
            def _(act):
                def square(b):
                    act.wait_ge(centred, b.number + 1)
                    once_past(act, summed, b, 1)
                    nc.scalar.activation(sq[:, :], cen[b.slot][:, :], ACT.Square).then_inc(squared, 1)

                def root(b):
                    act.wait_ge(summed, b.number + 1)
                    nc.scalar.activation(sd[b.slot][:, :], sd[b.slot][:, :], ACT.Sqrt, bias=g.eps[:, :], scale=1.0 / D).then_inc(rooted, 1)

                def turn(b):
                    act.wait_ge(turned, b.number + 1)
                    nc.scalar.activation(hT[b.slot][:, :], psT[:, :], ACT.Relu).then_inc(evac, 1)
                pipeline(act, order=[(1, root), (1, turn), (0, square)])

            @block.tensor
            def _(pe):
                def turn(b):
                    pe.wait_ge(centred, b.number + 1)
                    transpose_pairs(nc, psT, cen[b.slot], g.ident, B // 2).then_inc(turned, 1)

                def relate(b):
                    s = b.slot
                    pe.wait_ge(evac, b.number + 1)
                    for t in range(B):
                        if not (isinstance(b.number, int) and b.number == 0 and t < 4):
                            pe.wait_ge(read, b.number * B + (t - 3))
                        h = (t % 2) * D
                        nc.tensor.matmul(psR[t % 4][:, :], hT[s][h:h + D, (t // 2) * P:(t // 2 + 1) * P],
                                         g.w["rel"][h:h + D, :], start=True, stop=True).then_inc(product, 1)
                pipeline(pe, order=[(2, relate), (1, turn), (4, nothing)])
        seam(nc, g, r, g.x2, tot[(STEPS - 1) % 2], D)


def attention_edges(nc, g, name, nodes, normalise, weights, biases, dense, acc, beside=None):
    with Room(nc, g, name) as r:
        scores = r.sb("scores", [P, T])
        values = r.sb("values", [P, T * D])
        attention_scores(nc, g, name, nodes, normalise, weights, biases, dense, scores, values)
        segment_softmax(nc, g, name, scores)
        attention_sums(nc, g, name, acc, scores, values, normalise, beside)


def attention_scores(nc, g, name, nodes, normalise, weights, biases, dense, scores, values):
    W = B * D
    C = J * D
    wq, wk, wv, we = (g.w[n] for n in weights)
    bq, bk, bv = (g.w[n] for n in biases)
    pieces = [(h, n) for n in range(len(dense)) for h in range(2)]
    if normalise:
        pieces.append((None, 0))
    M = len(pieces)
    with Room(nc, g, name + "s") as r:
        ends = [r.sb(f"ends{k}", [P, C if normalise else W]) for k in range(SLOTS)]
        near = [r.sb(f"near{k}", [P, W]) for k in range(2)]
        xd = [r.sb(f"xd{k}", [P, C]) for k in range(2)]
        ea = [r.sb(f"ea{k}", [P, B * DE]) for k in range(2)]
        outs = [[r.sb(f"out{n}{k}", [P, C]) for k in range(2)] for n in range(len(dense))]
        take_s, take_d = ([r.sb(f"{n}{k}", [P, B], i32) for k in range(SLOTS)] for n in ("take_s", "take_d"))
        hsT, hdT, eaT, xT = ([r.sb(f"{n}{k}", [P, w]) for k in range(2)] for n, w in (("hsT", W), ("hdT", W), ("eaT", B * DE), ("xT", C)))
        q, k_ = g.zeros[:, 0:W], g.zeros[:, W:2 * W]
        if not normalise:
            more = [r.sb(f"more{k}", [P, W]) for k in range(2)]
            at_first, at_last = r.sb("at_first", [P, T]), r.sb("at_last", [P, T])
        if normalise:
            sq = [r.sb(f"sq{k}", [P, C]) for k in range(2)]
            sums, sd = r.sb("sums", [P, 2, J]), [r.sb(f"sd{k}", [P, 2, J]) for k in range(2)]
        psS, psD, psE, psQ, psK, psV, psX, psY = (r.ps(n, [P, 512]) for n in ("psS", "psD", "psE", "psQ", "psK", "psV", "psX", "psY"))
        got, ea_in, stored = ([r.sem(f"{n}{k}") for k in range(SLOTS)] for n in ("got", "ea_in", "stored"))
        (o_free, staged, link_s, centred, squared, summed, rooted, normed, turned, evac, turned_h, evac_h, product, used,
         piece, piece_read) = (r.sem(n) for n in (
             "o_free", "staged", "link", "centred", "squared", "summed", "rooted", "normed", "turned", "evac",
             "turned_h", "evac_h", "product", "used", "piece", "piece_read"))
        with nc.Block() as block:
            @block.gpsimd
            def _(pool):
                def fetch(b):
                    s = b.slot
                    if not (isinstance(b.number, int) and b.number < SLOTS):
                        held(pool, turned_h, b.number - (SLOTS - 1), g.passed)
                    if normalise:
                        nc.gpsimd.tensor_copy(take_d[s][:, :], g.dst_rows[:, bass.ds(b.number * B, B)])
                    nc.gpsimd.tensor_copy(take_s[s][:, :], g.src_rows[:, bass.ds(b.number * B, B)]).then_inc(staged, 1)
                    held(pool, staged, b.number + 1, g.passed)
                    gather(nc, ends[s][:, 0:W], nodes, take_s[s], got[s])
                    if normalise:
                        gather(nc, ends[s][:, W:C], nodes, take_d[s], got[s])
                pipeline(pool, order=[(0, fetch), (SLOTS, nothing)], slots=SLOTS)

            @block.sync
            def _(sp):
                rows = g.attr.rearrange("(p c t) d -> c p (t d)", p=P, t=B)
                near_rows, sum_rows = (tab.rearrange("(p c t) d -> c p (t d)", p=P, t=B) for tab in (g.near, g.sums))
                sp.sem_inc(o_free, 2)

                def load(b):
                    once_past(sp, turned_h, b, 2)
                    sp.dma_start(ea[b.slot % 2][:, :], rows[b.number]).then_inc(ea_in[b.slot], 16)
                    sp.dma_start(xd[b.slot % 2][:, :], chunk_of(nodes, b.number)).then_inc(ea_in[b.slot], 16)
                    if not normalise:
                        sp.dma_start(near[b.slot % 2][:, :], near_rows[b.number]).then_inc(ea_in[b.slot], 16)
                        sp.dma_start(more[b.slot % 2][:, :], sum_rows[b.number]).then_inc(ea_in[b.slot], 16)

                def store(b):
                    sp.wait_ge(piece_read, b.number * M + M)
                    for n, (_, _, to) in enumerate(dense):
                        sp.dma_start(chunk_of(to, b.number), outs[n][b.slot % 2][:, :]).then_inc(stored[b.slot], 16)
                    if normalise:
                        sp.dma_start(near_rows[b.number], near[b.slot % 2][:, :]).then_inc(stored[b.slot], 16)

                def landed(b):
                    sp.wait_ge(stored[b.slot], 16 * (len(dense) + normalise) * b.nth)
                    sp.sem_inc(o_free, 1)
                pipeline(sp, order=[(0, load), (3, store), (4, landed)], slots=SLOTS)

            def inputs_ready(eng, b):
                eng.wait_ge(got[b.slot], 16 * (1 + normalise) * B * b.nth)
                eng.wait_ge(ea_in[b.slot], (32 if normalise else 64) * b.nth)

            @block.tensor
            def _(pe):
                def turn(b):
                    s = b.slot
                    pe.wait_ge(normed, b.number + 1)
                    inputs_ready(pe, b)
                    e, x = ends[s], xd[s % 2]
                    once_past(pe, evac_h, b, 1)
                    transpose_pairs(nc, psS, e[:, 0:W], g.ident, B // 2)
                    transpose_pairs(nc, psD, e[:, W:C] if normalise else near[s % 2], g.ident, B // 2)
                    transpose_pairs(nc, psE, ea[s % 2], g.ident, B // 4)
                    transpose_pairs(nc, psX, x[:, 0:W], g.ident, B // 2).then_inc(turned, 1)

                def turn_rest(b):
                    pe.wait_ge(evac, b.number + 1)
                    transpose_pairs(nc, psX, xd[b.slot % 2][:, W:C], g.ident, B // 2).then_inc(turned_h, 1)

                def project(b):
                    s = b.slot
                    pe.wait_ge(evac, b.number + 1)
                    once_past(pe, used, b, 1)
                    times(nc, psQ, hdT[s % 2], wq, B // 2)
                    for to, w in ((psK, wk), (psV, wv)):
                        for h in range(2):
                            nc.tensor.matmul(to[:, h * 256:(h + 1) * 256], eaT[s % 2][:, h * P:(h + 1) * P], we[:, :], start=True, stop=False,
                                             skip_group_check=True)
                            for k in range(2):
                                j = 2 * h + k
                                last = nc.tensor.matmul(to[:, j * P:(j + 1) * P], hsT[s % 2][:, j * P:(j + 1) * P], w[:, :], start=False, stop=(k == 1),
                                                        skip_group_check=True)
                    last.then_inc(product, 1)

                def own(*some):
                    def stage(b):
                        s = b.slot
                        pe.wait_ge(evac_h, b.number + 1)
                        for m in some:
                            h, n = pieces[m]
                            if not (isinstance(b.number, int) and b.number == 0 and m == 0):
                                pe.wait_ge(piece_read, b.number * M + m)
                            left = hdT[s % 2] if h is None else xT[s % 2][:, h * W:(h + 1) * W]
                            times(nc, psY, left, g.w[dense[n][0]], B // 2).then_inc(piece, 1)
                    return stage
                if normalise:
                    order = [(2, project), (2, own(0)), (1, turn), (1, turn_rest), (2, own(1, 2))]
                else:
                    order = [(2, own(0)), (1, turn), (2, own(1)), (1, turn_rest), (1, project)]
                pipeline(pe, order=order, slots=SLOTS)

            @block.scalar
            def _(act):
                def square(b):
                    for e, x in enumerate((ends[b.slot], xd[b.slot % 2])):
                        act.wait_ge(centred, b.number * 2 + (e + 1))
                        once_past(act, rooted, b, 1)
                        nc.scalar.activation(sq[e][:, :], x[:, :], ACT.Square).then_inc(squared, 1)

                def root(b):
                    act.wait_ge(summed, b.number * 2 + 2)
                    nc.scalar.activation(sd[b.slot % 2][:, :, :], sd[b.slot % 2][:, :, :], ACT.Sqrt, bias=g.eps[:, :], scale=1.0 / D).then_inc(rooted, 1)

                def turn(b):
                    s = b.slot
                    act.wait_ge(turned, b.number + 1)
                    once_past(act, product, b, 2)
                    if not (isinstance(b.number, int) and b.number < 2):
                        act.wait_ge(piece, (b.number - 1) * M)
                    nc.scalar.activation(hsT[s % 2][:, :], psS[:, :], ACT.Relu)
                    nc.scalar.activation(hdT[s % 2][:, :], psD[:, :], ACT.Relu)
                    nc.scalar.activation(eaT[s % 2][:, :], psE[:, 0:B * DE], ACT.Copy)
                    nc.scalar.activation(xT[s % 2][:, 0:W], psX[:, :], ACT.Relu).then_inc(evac, 1)
                    act.wait_ge(turned_h, b.number + 1)
                    nc.scalar.activation(xT[s % 2][:, W:C], psX[:, :], ACT.Relu).then_inc(evac_h, 1)
                if normalise:
                    pipeline(act, order=[(1, root), (1, turn), (0, square), (4, nothing)], slots=SLOTS)
                else:
                    pipeline(act, order=[(1, turn), (4, nothing)], slots=SLOTS)

            @block.vector
            def _(dve):
                link = Link(dve, link_s)

                def centre(b):
                    s = b.slot
                    inputs_ready(dve, b)
                    for e, x in enumerate((ends[s], xd[s % 2])):
                        mean_off(nc, link, x[:, :], x[:, :], sums[:, e, :], J).then_inc(centred, 1)

                def variance(b):
                    for e in range(2):
                        dve.wait_ge(squared, b.number * 2 + (e + 1))
                        nc.vector.tensor_reduce(sd[b.slot % 2][:, e, :], grouped(sq[e][:, :], D), AXX, ALU.add).then_inc(summed, 1)

                def scale(b):
                    s = b.slot
                    root = sd[s % 2]
                    dve.wait_ge(rooted, b.number + 1)
                    link(nc.vector.reciprocal(root[:, :, :], root[:, :, :]))
                    for e, x in enumerate((ends[s], xd[s % 2])):
                        last = nc.vector.tensor_tensor(grouped(x[:, :], D), grouped(x[:, :], D), spread(root[:, e, :], D), ALU.mult)
                    last.then_inc(normed, 1)

                def expand(b):
                    here = near[b.slot % 2]
                    inputs_ready(dve, b)
                    link(nc.vector.tensor_tensor(here[:, :], here[:, :], more[b.slot % 2][:, :], ALU.add))
                    for fix, at in ((g.fix_first, at_first), (g.fix_last, at_last)):
                        for t in range(B):
                            part = here[:, t * D:(t + 1) * D]
                            last = nc.vector.scalar_tensor_tensor(part, fix[:, :], at[:, bass.ds(b.number * B + t, 1)], part, ALU.mult, ALU.add)
                        if at is at_first:
                            link(last)
                    last.then_inc(normed, 1)

                def score(b):
                    s = b.slot
                    dve.wait_ge(product, b.number + 1)
                    nc.vector.tensor_tensor(grouped(q[:, :], D), grouped(psQ[:, :], D), each_group(bq[:, :], B), ALU.add)
                    nc.vector.tensor_tensor(grouped(values[:, bass.ds(b.number * W, W)], D), grouped(psV[:, :], D), each_group(bv[:, :], B), ALU.add)
                    nc.vector.tensor_tensor(grouped(k_[:, :], D), grouped(psK[:, :], D), each_group(bk[:, :], B), ALU.add).then_inc(used, 1)
                    dve.wait_ge(used, b.number + 1)
                    link(nc.vector.tensor_tensor(q[:, :], q[:, :], k_[:, :], ALU.mult))
                    link(nc.vector.tensor_reduce(scores[:, bass.ds(b.number * B, B)], grouped(q[:, :], D), AXX, ALU.add))
                    link.restart()

                def take(*some):
                    def stage(b):
                        s = b.slot % 2
                        if 0 in some:
                            dve.wait_ge(o_free, b.number + 1)
                        for m in some:
                            h, n = pieces[m]
                            dve.wait_ge(piece, b.number * M + (m + 1))
                            to = near[s][:, :] if h is None else outs[n][s][:, h * W:(h + 1) * W]
                            nc.vector.tensor_tensor(grouped(to, D), grouped(psY[:, :], D),
                                                    each_group(g.w[dense[n][1]][:, :], B), ALU.add).then_inc(piece_read, 1)
                    return stage
                if normalise:
                    pipeline(dve, order=[(1, variance), (1, scale), (2, score), (2, take(0)), (0, centre), (2, take(1, 2))], slots=SLOTS)
                else:
                    link(nc.vector.tensor_scalar(at_first[:, :], g.dst_f[:, :], g.dst_f[:, 0:1], None, ALU.is_equal))
                    link(nc.vector.tensor_scalar(at_last[:, :], g.dst_f[:, :], g.dst_f[:, T - 1:T], None, ALU.is_equal))
                    pipeline(dve, order=[(2, score), (2, take(0)), (0, expand), (2, take(1))], slots=SLOTS)


def segment_softmax(nc, g, name, scores):
    with Room(nc, g, name + "m") as r:
        fence, fence_back, keep_back, last = (r.sb(n, [P, T]) for n in ("fence", "fence_back", "keep_back", "last"))
        fwd, full, at_first, at_last, ends = (r.sb(n, [P, T]) for n in ("fwd", "full", "at_first", "at_last", "ends"))
        diag = r.sb("diag", [P, 2, P])
        near_first, near_last = r.sb("near_first", [P, 2, P]), r.sb("near_last", [P, 2, P])
        masks = r.sb("masks", [P, 2, 2, P])
        both = r.sb("both", [P, 2])
        tail = r.sb("tail", [P, 1])
        two = r.sb("two", [P, 1])
        ps = r.ps("ps", [P, 2 * P])
        link_s, spread_s, rows_s, shifted, exped = (r.sem(n) for n in ("link", "diag", "rows", "shifted", "exped"))
        rev = slice(None, None, -1)
        with nc.Block() as block:
            @block.tensor
            def _(pe):
                for n in range(2):
                    pe.wait_ge(spread_s, n + 1)
                    nc.tensor.matmul(ps[:, :], g.ones[:, :], diag[:, :, :].rearrange("p a q -> p (a q)"), start=True, stop=True).then_inc(rows_s, 1)

            @block.scalar
            def _(act):
                act.wait_ge(shifted, 1)
                nc.scalar.activation(scores[:, :], scores[:, :], ACT.Exp, scale=0.125).then_inc(exped, 1)

            @block.vector
            def _(dve):
                link = Link(dve, link_s)
                v = nc.vector
                link(v.tensor_scalar(fence[:, :], g.goes_on[:, :], HUGE, -HUGE, ALU.mult, ALU.add))
                link(v.memset(keep_back[:, T - 1:T], 0.0))
                link(v.tensor_copy(keep_back[:, 0:T - 1], g.goes_on[:, 1:T]))
                link(v.tensor_scalar(fence_back[:, :], keep_back[:, :], HUGE, -HUGE, ALU.mult, ALU.add))
                link(v.tensor_scalar(last[:, :], keep_back[:, :], -1.0, 1.0, ALU.mult, ALU.add))
                link(v.tensor_scalar(at_first[:, :], g.dst_f[:, :], g.dst_f[:, 0:1], None, ALU.is_equal))
                link(v.tensor_scalar(at_last[:, :], g.dst_f[:, :], g.dst_f[:, T - 1:T], None, ALU.is_equal))
                link(v.tensor_tensor(tail[:, :], g.dst_f[:, 0:1], g.dst_f[:, T - 1:T], ALU.not_equal))
                for k, m in enumerate((g.first_first, g.first_last, g.last_first, g.last_last)):
                    link(v.tensor_copy(masks[:, k // 2, k % 2, :], m[:, :]))

                def ends_of(a, z, n):
                    link(v.tensor_scalar(diag[:, 0, :], g.ident[:, :], a, None, ALU.mult))
                    v.tensor_scalar(diag[:, 1, :], g.ident[:, :], z, None, ALU.mult).then_inc(spread_s, 1)
                    dve.wait_ge(rows_s, n)

                rows = ps[:, :].rearrange("p (a q) -> p a q", q=P)
                link(v.tensor_tensor_scan(fwd[:, :], fence[:, :], scores[:, :], 0.0, ALU.add, ALU.max))
                link(v.tensor_tensor_scan(full[:, rev], fence_back[:, rev], fwd[:, rev], 0.0, ALU.add, ALU.max))
                ends_of(full[:, 0:1], fwd[:, T - 1:T], 1)
                for k, near in enumerate((near_first, near_last)):
                    link(v.tensor_scalar(near[:, :, :], masks[:, k, :, :], HUGE, -HUGE, ALU.mult, ALU.add))
                    link(v.tensor_tensor(near[:, :, :], near[:, :, :], rows, ALU.add))
                    link(v.tensor_reduce(both[:, k:k + 1], near[:, :, :].rearrange("p a q -> p (a q)"), AXX, ALU.max))
                for k, at in enumerate((at_first, at_last)):
                    link(v.tensor_scalar(ends[:, :], at[:, :], HUGE, -HUGE, ALU.mult, ALU.add))
                    link(v.scalar_tensor_tensor(full[:, :], ends[:, :], both[:, k:k + 1], full[:, :], ALU.add, ALU.max))
                v.tensor_tensor(scores[:, :], scores[:, :], full[:, :], ALU.subtract).then_inc(shifted, 1)
                dve.wait_ge(exped, 1)
                link(v.tensor_tensor_scan(fwd[:, :], g.goes_on[:, :], scores[:, :], 0.0, ALU.mult, ALU.add))
                link(v.tensor_tensor(last[:, :], last[:, :], fwd[:, :], ALU.mult))
                link(v.tensor_tensor_scan(full[:, rev], keep_back[:, rev], last[:, rev], 0.0, ALU.mult, ALU.add))
                link(v.tensor_tensor(two[:, :], fwd[:, T - 1:T], tail[:, :], ALU.mult))
                ends_of(full[:, 0:1], two[:, :], 2)
                for k, near in enumerate((near_first, near_last)):
                    link(v.tensor_tensor(near[:, :, :], masks[:, k, :, :], rows, ALU.mult))
                    link(v.tensor_reduce(both[:, k:k + 1], near[:, :, :].rearrange("p a q -> p (a q)"), AXX, ALU.add))
                for k, at in enumerate((at_first, at_last)):
                    link(v.scalar_tensor_tensor(full[:, :], at[:, :], both[:, k:k + 1], full[:, :], ALU.mult, ALU.max))
                link(v.reciprocal(full[:, :], full[:, :]))
                link(v.tensor_tensor(scores[:, :], scores[:, :], full[:, :], ALU.mult))


def attention_sums(nc, g, name, agg, alpha, values, spread_out, beside):
    W = B * D
    with Room(nc, g, name + "w") as r:
        tot = [r.sb(f"tot{k}", [P, W]) for k in range(2)]
        put = [r.sb(f"put{k}", [P, B], i32) for k in range(2)]
        msg = r.sb("msg", [P, W])
        if spread_out:
            ends, keep_back = r.sb("ends", [P, T]), r.sb("keep_back", [P, T])
            two, tail = r.sb("two", [P, D]), r.sb("tail", [P, 1])
            fixes = [r.ps(f"fix{k}", [P, D]) for k in range(2)]
            scanned, fixed, fix_put = r.sem("scanned"), r.sem("fixed"), r.sem("stored2")
        stored = [r.sem(f"stored{k}") for k in range(2)]
        if beside:
            weight, bias, nodes, to = g.w[beside[0]], g.w[beside[1]], beside[2], beside[3]
            x, xT, o = ([r.sb(f"{n}{k}", [P, J * D]) for k in range(2)] for n in ("x", "xT", "o"))
            psT, psO = r.ps("psT", [P, J * D]), r.ps("psO", [P, J * D])
            x_in, o_stored = ([r.sem(f"{n}{k}") for k in range(2)] for n in ("x_in", "o_stored"))
            turned, evac, product, taken, o_free = (r.sem(n) for n in ("turned", "evac", "product", "taken", "o_free"))
        sum_free, link_s, staged, ready = (r.sem(n) for n in ("sum_free", "link", "staged", "ready"))
        with nc.Block() as block:
            @block.vector
            def _(dve):
                link = Link(dve, link_s)
                link(nc.vector.memset(tot[1][:, :], 0.0))
                link.restart()
                if spread_out:
                    v = nc.vector
                    link(v.memset(keep_back[:, T - 1:T], 0.0))
                    link(v.tensor_copy(keep_back[:, 0:T - 1], g.goes_on[:, 1:T]))
                    link(v.tensor_scalar(ends[:, :], keep_back[:, :], -1.0, 1.0, ALU.mult, ALU.add))
                    link(v.tensor_tensor(tail[:, :], g.dst_f[:, 0:1], g.dst_f[:, T - 1:T], ALU.not_equal))
                    link.restart()

                def add(b):
                    s = b.slot
                    dve.wait_ge(sum_free, b.number + 1)
                    link(nc.vector.tensor_tensor(grouped(msg[:, :], D), grouped(values[:, bass.ds(b.number * W, W)], D),
                                                 spread(alpha[:, bass.ds(b.number * B, B)], D), ALU.mult))
                    running_sums(nc, link, tot, s, msg, g, b, D).then_inc(ready, 1)
                    dve.wait_ge(ready, b.number + 1)
                    if spread_out:
                        nc.vector.tensor_tensor(grouped(values[:, bass.ds(b.number * W, W)], D), grouped(tot[s][:, :], D),
                                                spread(ends[:, bass.ds(b.number * B, B)], D), ALU.mult)

                def take(b):
                    dve.wait_ge(product, b.number + 1)
                    dve.wait_ge(o_free, b.number + 1)
                    nc.vector.tensor_tensor(grouped(o[b.slot][:, :], D), grouped(psO[:, :], D), each_group(bias[:, :], J), ALU.add).then_inc(taken, 1)
                pipeline(dve, order=[(0, add)] + ([(1, take)] if beside else []))
                if spread_out:
                    dve.drain()
                    by_feature = values[:, :].rearrange("p (t d) -> p d t", d=D)
                    back = slice(None, None, -1)
                    link(v.tensor_tensor(two[:, :], tot[(STEPS - 1) % 2][:, (B - 1) * D:B * D], tail[:, :].to_broadcast([P, D]), ALU.mult))
                    for d in range(D):
                        column = by_feature[:, d, back]
                        last = v.tensor_tensor_scan(column, keep_back[:, back], column, 0.0, ALU.mult, ALU.add)
                    last.then_inc(scanned, 1)
                    dve.wait_ge(fixed, 1)
                    link(v.tensor_tensor(g.fix_first[:, :], fixes[0][:, :], values[:, 0:D], ALU.subtract))
                    link(v.tensor_tensor(g.fix_last[:, :], fixes[1][:, :], two[:, :], ALU.subtract))
                    link(v.tensor_tensor(g.fix_last[:, :], g.fix_last[:, :], tail[:, :].to_broadcast([P, D]), ALU.mult))

            if beside:
                @block.tensor
                def _(pe):
                    def multiply(b):
                        pe.wait_ge(x_in[b.slot], 16 * b.nth)
                        once_past(pe, evac, b, 1)
                        transpose_pairs(nc, psT, x[b.slot], g.ident, J // 2).then_inc(turned, 1)
                        pe.wait_ge(evac, b.number + 1)
                        once_past(pe, taken, b, 1)
                        times(nc, psO, xT[b.slot], weight, J // 2).then_inc(product, 1)
                    pipeline(pe, order=[(0, multiply), (2, nothing)])

                @block.scalar
                def _(act):
                    def copy_out(b):
                        act.wait_ge(turned, b.number + 1)
                        nc.scalar.activation(xT[b.slot][:, :], psT[:, :], ACT.Relu).then_inc(evac, 1)
                    pipeline(act, copy_out)

                @block.sync
                def _(sp):
                    sp.sem_inc(o_free, 2)

                    def load(b):
                        once_past(sp, turned, b, 2)
                        sp.dma_start(x[b.slot][:, :], chunk_of(nodes, b.number)).then_inc(x_in[b.slot], 16)

                    def store(b):
                        sp.wait_ge(taken, b.number + 1)
                        sp.dma_start(chunk_of(to, b.number), o[b.slot][:, :]).then_inc(o_stored[b.slot], 16)

                    def landed(b):
                        sp.wait_ge(o_stored[b.slot], 16 * b.nth)
                        sp.sem_inc(o_free, 1)
                    pipeline(sp, order=[(0, load), (2, store), (3, landed)])

            if spread_out:
                @block.tensor
                def _(pe):
                    pe.wait_ge(scanned, 1)
                    for fix, of_first, of_last in ((fixes[0], g.first_first, g.last_first), (fixes[1], g.first_last, g.last_last)):
                        nc.tensor.matmul(fix[:, :], of_first[:, :], values[:, 0:D], start=True, stop=False)
                        last = nc.tensor.matmul(fix[:, :], of_last[:, :], two[:, :], start=False, stop=True)
                    last.then_inc(fixed, 1)

                @block.sync
                def _(sp):
                    sp.wait_ge(scanned, 1)
                    sp.dma_start(g.sums.rearrange("(p t) d -> p (t d)", p=P), values[:, :]).then_inc(fix_put, 16)
                    sp.wait_ge(fix_put, 16)

            @block.gpsimd
            def _(pool):
                pool.sem_inc(sum_free, 2)
                scatter_pipeline(nc, pool, g, tot, put, agg, ready, staged, stored, sum_free)
        seam(nc, g, r, agg, tot[(STEPS - 1) % 2], D)


def scatter_pipeline(nc, pool, g, tot, put, agg, ready, staged, stored, sum_free):
    def send(b):
        s = b.slot
        held(pool, ready, b.number + 1, g.passed)
        nc.gpsimd.tensor_copy(put[s][:, :], g.last_rows[:, bass.ds(b.number * B, B)]).then_inc(staged, 1)
        held(pool, staged, b.number + 1, g.passed)
        add_rows(nc, tot[s], agg, put[s], stored[s])

    def landed(b):
        held(pool, stored[b.slot], 16 * B * b.nth, g.passed)
        pool.sem_inc(sum_free, 1)
    pipeline(pool, send, landed)


def skip_dense(nc, g):
    W = J * D
    with Room(nc, g, "sk") as r:
        x, g2, sk = ([r.sb(f"{n}{k}", [P, W]) for k in range(DEEP)] for n in ("x", "g2", "sk"))
        g2T, cen, hT, sq = ([r.sb(f"{n}{k}", [P, W]) for k in range(2)] for n in ("g2T", "cen", "hT", "sq"))
        o = [r.sb(f"o{k}", [P, J * MID]) for k in range(DEEP)]
        sums, sd = r.sb("sums", [P, DEEP, J]), r.sb("sd", [P, DEEP, J])
        psA, psB, psT = (r.ps(n, [P, W]) for n in ("psA", "psB", "psT"))
        psO = [r.ps(f"psO{k}", [P, J * MID]) for k in range(2)]
        x_in, stored, o_stored = ([r.sem(f"{n}{k}") for k in range(DEEP)] for n in ("x_in", "stored", "o_stored"))
        names = ("free", "link", "turned2", "evac2", "made2", "mixed", "added", "centred", "squared",
                 "summed", "rooted", "turned3", "evac3", "made3", "ready", "o_free")
        (free, link_s, turned2, evac2, made2, mixed, added, centred, squared,
         summed, rooted, turned3, evac3, made3, ready, o_free) = (r.sem(n) for n in names)
        with nc.Block() as block:
            @block.sync
            def _(sp):
                sp.sem_inc(free, DEEP)

                def load(b):
                    sp.wait_ge(free, b.number + 1)
                    sp.dma_start(g2[b.slot][:, :], chunk_of(g.g2, b.number)).then_inc(x_in[b.slot], 16)
                    sp.dma_start(sk[b.slot][:, :], chunk_of(g.skip, b.number)).then_inc(x_in[b.slot], 16)
                    sp.dma_start(x[b.slot][:, :], chunk_of(g.x2, b.number)).then_inc(x_in[b.slot], 16)
                pipeline(sp, load, slots=DEEP)

            @block.tensor
            def _(pe):
                def skip(b):
                    s = b.slot
                    pe.wait_ge(x_in[s], 48 * b.nth)
                    once_past(pe, evac2, b, 1)
                    transpose_pairs(nc, psA, g2[s], g.ident, J // 2).then_inc(turned2, 1)

                def mix(b):
                    pe.wait_ge(evac2, b.number + 1)
                    once_past(pe, mixed, b, 1)
                    times(nc, psB, g2T[b.slot % 2], g.w["skip_b"], J // 2).then_inc(made2, 1)

                def narrow(b):
                    s = b.slot
                    pe.wait_ge(centred, b.number + 1)
                    once_past(pe, evac3, b, 1)
                    transpose_pairs(nc, psT, cen[s % 2], g.ident, J // 2).then_inc(turned3, 1)

                def project(b):
                    s = b.slot
                    pe.wait_ge(evac3, b.number + 1)
                    once_past(pe, ready, b, 2)
                    times(nc, psO[s % 2], hT[s % 2], g.w["gcn1"], J // 2).then_inc(made3, 1)
                pipeline(pe, order=[(0, skip), (2, narrow), (2, project), (0, mix)], slots=DEEP)

            @block.scalar
            def _(act):
                def out2(b):
                    s = b.slot
                    act.wait_ge(turned2, b.number + 1)
                    nc.scalar.activation(g2T[s % 2][:, :], psA[:, :], ACT.Relu).then_inc(evac2, 1)

                def square(b):
                    s = b.slot
                    act.wait_ge(centred, b.number + 1)
                    once_past(act, summed, b, 2)
                    nc.scalar.activation(sq[s % 2][:, :], cen[s % 2][:, :], ACT.Square).then_inc(squared, 1)

                def root(b):
                    s = b.slot
                    act.wait_ge(summed, b.number + 1)
                    nc.scalar.activation(sd[:, s, :], sd[:, s, :], ACT.Sqrt, bias=g.eps[:, :], scale=1.0 / D).then_inc(rooted, 1)

                def out3(b):
                    s = b.slot
                    act.wait_ge(turned3, b.number + 1)
                    once_past(act, made3, b, 2)
                    nc.scalar.activation(hT[s % 2][:, :], psT[:, :], ACT.Relu).then_inc(evac3, 1)
                act.sem_inc(o_free, DEEP)

                def store_x(b):
                    act.wait_ge(centred, b.number + 1)
                    act.dma_start(chunk_of(g.x3, b.number), x[b.slot][:, :]).then_inc(stored[b.slot], 16)

                def landed_x(b):
                    act.wait_ge(stored[b.slot], 16 * b.nth)
                    act.sem_inc(free, 1)

                def store(b):
                    s = b.slot
                    act.wait_ge(ready, b.number + 1)
                    act.dma_start(chunk_of(g.t3, b.number), o[s][:, :]).then_inc(o_stored[s], 16)
                    act.dma_start(chunk_of(g.acc3, b.number), o[s][:, :]).then_inc(o_stored[s], 16)

                def landed(b):
                    act.wait_ge(o_stored[b.slot], 32 * b.nth)
                    act.sem_inc(o_free, 1)
                pipeline(act, order=[(2, square), (2, store_x), (0, out2), (2, out3), (4, landed_x), (2, root), (4, store), (6, landed)],
                         slots=DEEP)

            @block.vector
            def _(dve):
                link = Link(dve, link_s)

                def add(b):
                    s = b.slot
                    dve.wait_ge(made2, b.number + 1)
                    nc.vector.tensor_tensor(sk[s][:, :], sk[s][:, :], psB[:, :], ALU.add).then_inc(mixed, 1)
                    dve.wait_ge(mixed, b.number + 1)
                    nc.vector.scalar_tensor_tensor(x[s][:, :], sk[s][:, :], 0.0, x[s][:, :], ALU.max, ALU.add).then_inc(added, 1)
                    dve.wait_ge(added, b.number + 1)
                    once_past(dve, turned3, b, 2)
                    mean_off(nc, link, x[s][:, :], cen[s % 2][:, :], sums[:, s, :], J).then_inc(centred, 1)

                def variance(b):
                    s = b.slot
                    dve.wait_ge(squared, b.number + 1)
                    nc.vector.tensor_reduce(sd[:, s, :], grouped(sq[s % 2][:, :], D), AXX, ALU.add).then_inc(summed, 1)

                def close(b):
                    s = b.slot
                    dve.wait_ge(rooted, b.number + 1)
                    link(nc.vector.reciprocal(sd[:, s, :], sd[:, s, :]))
                    link(nc.vector.tensor_tensor(sd[:, s, :], sd[:, s, :], g.dinv[:, bass.ds(b.number * J, J)], ALU.mult))
                    link.restart()
                    dve.wait_ge(made3, b.number + 1)
                    dve.wait_ge(o_free, b.number + 1)
                    nc.vector.tensor_tensor(grouped(o[s][:, :], MID), grouped(psO[s % 2][:, :], MID),
                                            spread(sd[:, s, :], MID), ALU.mult).then_inc(ready, 1)
                pipeline(dve, order=[(3, close), (2, variance), (1, add)], slots=DEEP)


def gcn_edges(nc, g, name, nodes, agg):
    W = B * MID
    with Room(nc, g, name) as r:
        rows, tot = ([r.sb(f"{n}{k}", [P, W]) for k in range(2)] for n in ("rows", "tot"))
        take, put = ([r.sb(f"{n}{k}", [P, B], i32) for k in range(2)] for n in ("take", "put"))
        got, stored = ([r.sem(f"{n}{k}") for k in range(2)] for n in ("got", "stored"))
        free, sum_free, link_s, staged, staged_put, ready = (r.sem(n) for n in (
            "free", "sum_free", "link", "staged", "staged_put", "ready"))
        with nc.Block() as block:
            @block.gpsimd
            def _(pool):
                pool.sem_inc(free, 2)
                pool.sem_inc(sum_free, 2)

                def fetch(b):
                    s = b.slot
                    held(pool, free, b.number + 1, g.passed)
                    nc.gpsimd.tensor_copy(take[s][:, :], g.src_rows[:, bass.ds(b.number * B, B)]).then_inc(staged, 1)
                    held(pool, staged, b.number + 1, g.passed)
                    gather(nc, rows[s], nodes, take[s], got[s])

                def send(b):
                    s = b.slot
                    held(pool, ready, b.number + 1, g.passed)
                    nc.gpsimd.tensor_copy(put[s][:, :], g.last_rows[:, bass.ds(b.number * B, B)]).then_inc(staged_put, 1)
                    held(pool, staged_put, b.number + 1, g.passed)
                    add_rows(nc, tot[s], agg, put[s], stored[s])

                def landed(b):
                    held(pool, stored[b.slot], 16 * B * b.nth, g.passed)
                    pool.sem_inc(sum_free, 1)
                pipeline(pool, fetch, send, landed)

            @block.vector
            def _(dve):
                link = Link(dve, link_s)
                link(nc.vector.memset(tot[1][:, :], 0.0))
                link.restart()

                def add(b):
                    s = b.slot
                    dve.wait_ge(got[s], 16 * B * b.nth)
                    dve.wait_ge(sum_free, b.number + 1)
                    running_sums(nc, link, tot, s, rows[s], g, b, MID).then_inc(ready, 1)
                    dve.wait_ge(ready, b.number + 1)
                    nc.vector.sem_inc(free, 1)
                pipeline(dve, add)
        seam(nc, g, r, agg, tot[(STEPS - 1) % 2], MID)


def gcn_middle(nc, g):
    W = J * MID
    with Room(nc, g, "gm") as r:
        t3, o = ([r.sb(f"{n}{k}", [P, W]) for k in range(SLOTS)] for n in ("t3", "o"))
        x_in, stored = ([r.sem(f"{n}{k}") for k in range(SLOTS)] for n in ("x_in", "stored"))
        free, link_s, ready = (r.sem(n) for n in ("free", "link", "ready"))
        with nc.Block() as block:
            @block.sync
            def _(sp):
                sp.sem_inc(free, SLOTS)

                def load(b):
                    sp.wait_ge(free, b.number + 1)
                    sp.dma_start(t3[b.slot][:, :], chunk_of(g.acc3, b.number)).then_inc(x_in[b.slot], 16)
                pipeline(sp, load, slots=SLOTS)

            @block.vector
            def _(dve):
                link = Link(dve, link_s)

                def close(b):
                    s = b.slot
                    dinv = spread(g.dinv[:, bass.ds(b.number * J, J)], MID)
                    link.restart()
                    dve.wait_ge(x_in[s], 16 * b.nth)
                    link(nc.vector.tensor_tensor(grouped(t3[s][:, :], MID), grouped(t3[s][:, :], MID), dinv, ALU.mult))
                    link(nc.vector.tensor_tensor(grouped(t3[s][:, :], MID), grouped(t3[s][:, :], MID), each_group(g.w["bg1"][:, 0:MID], J), ALU.add))
                    link(nc.vector.tensor_scalar(t3[s][:, :], t3[s][:, :], 0.0, None, ALU.max))
                    nc.vector.tensor_tensor(grouped(o[s][:, :], MID), grouped(t3[s][:, :], MID), dinv, ALU.mult).then_inc(ready, 1)
                pipeline(dve, close, slots=SLOTS)

            @block.scalar
            def _(act):
                def store(b):
                    act.wait_ge(ready, b.number + 1)
                    act.dma_start(chunk_of(g.t4, b.number), o[b.slot][:, :]).then_inc(stored[b.slot], 16)
                    act.dma_start(chunk_of(g.acc4, b.number), o[b.slot][:, :]).then_inc(stored[b.slot], 16)

                def landed(b):
                    act.wait_ge(stored[b.slot], 32 * b.nth)
                    act.sem_inc(free, 1)
                pipeline(act, store, None, landed, slots=SLOTS, oldest_first=True)


def gcn_close(nc, g, out):
    W = J * D
    M = J * MID
    with Room(nc, g, "gf") as r:
        x = [r.sb(f"x{k}", [P, W]) for k in range(DEEP)]
        acc = [r.sb(f"acc{k}", [P, M]) for k in range(DEEP)]
        uT = [r.sb(f"uT{k}", [P, M]) for k in range(2)]
        psT = [r.ps(f"psT{k}", [P, M]) for k in range(2)]
        psH = [r.ps(f"psH{k}", [P, W]) for k in range(2)]
        x_in, stored = ([r.sem(f"{n}{k}") for k in range(DEEP)] for n in ("x_in", "stored"))
        free, biased, scaled, turned, evac, product, ready = (r.sem(n) for n in (
            "free", "biased", "scaled", "turned", "evac", "product", "ready"))
        with nc.Block() as block:
            @block.sync
            def _(sp):
                sp.sem_inc(free, DEEP)

                def load(b):
                    sp.wait_ge(free, b.number + 1)
                    sp.dma_start(acc[b.slot][:, :], chunk_of(g.acc4, b.number)).then_inc(x_in[b.slot], 16)
                    sp.dma_start(x[b.slot][:, :], chunk_of(g.x3, b.number)).then_inc(x_in[b.slot], 16)
                pipeline(sp, load, slots=DEEP)

            @block.vector
            def _(dve):
                def scale(b):
                    s = b.slot
                    dve.wait_ge(x_in[s], 32 * b.nth)
                    nc.vector.tensor_tensor(grouped(acc[s][:, :], MID), grouped(acc[s][:, :], MID),
                                            spread(g.dinv[:, bass.ds(b.number * J, J)], MID), ALU.mult).then_inc(scaled, 1)

                def close(b):
                    s = b.slot
                    dve.wait_ge(product, b.number + 1)
                    dve.wait_ge(biased, b.number + 1)
                    nc.vector.tensor_tensor(x[s][:, :], x[s][:, :], psH[s % 2][:, :], ALU.add).then_inc(ready, 1)
                pipeline(dve, scale, close, slots=DEEP)

            @block.tensor
            def _(pe):
                def turn(b):
                    s = b.slot
                    pe.wait_ge(scaled, b.number + 1)
                    transpose_pairs(nc, psT[s % 2], acc[s], g.ident, J // 4).then_inc(turned, 1)
                    pe.wait_ge(evac, b.number + 1)
                    once_past(pe, ready, b, 2)
                    times(nc, psH[s % 2], uT[s % 2], g.w["gcn2"], J // 4).then_inc(product, 1)
                pipeline(pe, order=[(0, turn), (2, nothing)], slots=DEEP)

            @block.scalar
            def _(act):
                def turn(b):
                    act.wait_ge(turned, b.number + 1)
                    nc.scalar.activation(uT[b.slot % 2][:, :], psT[b.slot % 2][:, :], ACT.Copy).then_inc(evac, 1)

                whole = out[0:(STEPS - 1) * CHUNK, :].rearrange("(c p j) d -> c p (j d)", p=P, j=J)

                def store(b):
                    act.wait_ge(ready, b.number + 1)
                    if isinstance(b.number, int) and b.number == STEPS - 1:
                        act.dma_start(out[(STEPS - 1) * CHUNK:N, :].rearrange("(p j) d -> p (j d)", j=J), x[b.slot][0:LASTP, :]).then_inc(stored[b.slot], 16)
                    else:
                        act.dma_start(whole[b.number], x[b.slot][:, :]).then_inc(stored[b.slot], 16)

                def landed(b):
                    act.wait_ge(stored[b.slot], 16 * b.nth)
                    act.sem_inc(free, 1)
                pipeline(act, order=[(0, turn), (2, store), (4, landed)], slots=DEEP)

            @block.gpsimd
            def _(pool):
                def bias(b):
                    s = b.slot
                    held(pool, x_in[s], 32 * b.nth, g.passed)
                    nc.gpsimd.tensor_tensor(grouped(x[s][:, :], D), grouped(x[s][:, :], D), each_group(g.w["bg2"][:, :], J), ALU.add).then_inc(biased, 1)

                pipeline(pool, bias, slots=DEEP)


NAMES = ["x", "src", "dst", "edge_attr_32", "edge_type_8", "edge_weight1", "L0_gnn_b", "L1_gnn_weight",
         "L2_gnn_q1_w", "L2_gnn_q1_b", "L2_gnn_k1_w", "L2_gnn_k1_b", "L2_gnn_v1_w", "L2_gnn_v1_b", "L2_gnn_e1_w",
         "L2_gnn_s1_w", "L2_gnn_s1_b", "L2_gnn_q2_w", "L2_gnn_q2_b", "L2_gnn_k2_w", "L2_gnn_k2_b", "L2_gnn_v2_w",
         "L2_gnn_v2_b", "L2_gnn_e2_w", "L2_gnn_s2_w", "L2_gnn_s2_b", "L2_gnn_skip_w", "L2_gnn_skip_b",
         "L3_gnn_W1", "L3_gnn_b1", "L3_gnn_W2", "L3_gnn_b2"]


def kernel(**inputs):
    import numpy as _np
    import concourse.bacc as _bacc
    from concourse import mybir as _mybir
    from concourse.bass_utils import run_bass_kernel_spmd as _run

    nc = _bacc.Bacc("TRN2", target_bir_lowering=False, num_devices=1)
    arrays, given = {}, {}
    for name in NAMES + ["W0T"]:
        v = _np.asarray(inputs["L0_gnn_W"]).T if name == "W0T" else _np.asarray(inputs[name])
        v = _np.ascontiguousarray(v)
        arrays[f"in_{name}"] = v
        given[name] = nc.dram_tensor(f"in_{name}", v.shape, _mybir.dt.from_np(v.dtype), kind="ExternalInput").ap()
    out = nc.dram_tensor("out_x", (N, D), _mybir.dt.float32, kind="ExternalOutput").ap()
    build(nc, given, out)
    r = _run(nc, [arrays], core_ids=[0])
    return r.results[0]["out_x"]
```
